# Optimizing a Trainium2 kernel written in Bass

```python
import numpy as np
import jax
import jax.numpy as jnp

def _softmax(x, axis=-1):
    return jax.nn.softmax(x, axis=axis)

def _gelu(x):
    return jax.nn.gelu(x, approximate=True)

def _silu(x):
    return jax.nn.silu(x)

def _sigmoid(x):
    return jax.nn.sigmoid(x)

def _layernorm(x, axis=-1, eps=1e-05):
    m = jnp.mean(x, axis=axis, keepdims=True)
    v = jnp.var(x, axis=axis, keepdims=True)
    return (x - m) / jnp.sqrt(v + eps)

def _scatter_add(tgt, idx, src, axis=0):
    return tgt.at[idx].add(src)

def _segment_sum(src, seg, n):
    return jax.ops.segment_sum(src, seg, n)
kernel_name = 'mk_seq_preln_d2_jaxref_r8_9b7748'

def setup_inputs(seed: int=0):
    np.random.seed(seed)
    _w = jnp.asarray

    def _L0_attn_setup():
        import jax, jax.numpy as jnp
        import numpy as np
        B, S, D = (2, 512, 256)
        H, DK, DV = (16, 128, 128)
        SEG = 64
        UPDATE = 'delta'
        CAUSAL = True
        key = jax.random.key(seed)
        ks = jax.random.split(key, 6)
        s = 0.02
        return {'x': jax.random.normal(ks[0], (B, S, D), jnp.float32), 'Wq': jax.random.normal(ks[1], (D, H * DK), jnp.float32) * s, 'Wk': jax.random.normal(ks[2], (D, H * DK), jnp.float32) * s, 'Wv': jax.random.normal(ks[3], (D, H * DV), jnp.float32) * s, 'Wo': jax.random.normal(ks[4], (H * DV, D), jnp.float32) * s, 'betas': jax.random.normal(ks[5], (1, H, 1, DV), jnp.float32)}
    _L0_attn_in = _L0_attn_setup()

    def _L0_ffn_setup():
        import jax, jax.numpy as jnp
        import numpy as np
        H = 256
        I = 176
        E = 16
        K = 2
        SI = I * 2

        def _swiglu(gu, inter):
            g, u = (gu[..., :inter], gu[..., inter:])
            return jax.nn.silu(g) * u
        key = jax.random.key(seed)
        ks = jax.random.split(key, 6)
        s = 0.02
        hidden_states = jax.random.normal(ks[0], (1, 128, H), dtype=jnp.float32)
        gate_w = jax.random.normal(ks[1], (E, H), dtype=jnp.float32) * s
        w_gate_up = jax.random.normal(ks[2], (E, H, 2 * I), dtype=jnp.float32) * s
        w_down = jax.random.normal(ks[3], (E, I, H), dtype=jnp.float32) * s
        shared_gate_up = jax.random.normal(ks[4], (H, 2 * SI), dtype=jnp.float32) * s
        shared_down = jax.random.normal(ks[5], (SI, H), dtype=jnp.float32) * s
        return {'hidden_states': hidden_states, 'gate_w': gate_w, 'w_gate_up': w_gate_up, 'w_down': w_down, 'shared_gate_up': shared_gate_up, 'shared_down': shared_down}
    _L0_ffn_in = _L0_ffn_setup()

    def _L1_attn_setup():
        import jax, jax.numpy as jnp
        import numpy as np
        HIDDEN = 256
        GAMMA = 0.96875
        SCALE_BASE = 64

        def _xpos(x, downscale=False):
            B, L, d = x.shape
            half = d // 2
            scale_vec = (jnp.arange(0, d, 2, dtype=jnp.float32) + 0.4 * d) / (1.4 * d)
            power = jnp.arange(L, dtype=jnp.float32) / SCALE_BASE
            scale = scale_vec[None, :] ** power[:, None]
            inv_freq = 1.0 / 10000.0 ** (jnp.arange(half, dtype=jnp.float32) / half)
            sinusoid = jnp.arange(L, dtype=jnp.float32)[:, None] * inv_freq[None, :]
            sin, cos = (jnp.sin(sinusoid), jnp.cos(sinusoid))
            if downscale:
                scale = 1.0 / scale
            sin_s = jnp.repeat(sin * scale, 2, axis=-1)
            cos_s = jnp.repeat(cos * scale, 2, axis=-1)
            x1 = x[..., 0::2]
            x2 = x[..., 1::2]
            rot = jnp.stack((-x2, x1), axis=-1).reshape(x.shape)
            return x * cos_s[None] + rot * sin_s[None]

        def _decay_matrix(L):
            n = jnp.arange(L)[:, None]
            m = jnp.arange(L)[None, :]
            mask = n >= m
            D = jnp.where(mask, GAMMA ** jnp.maximum(n - m, 0).astype(jnp.float32), 0.0)
            return D
        key = jax.random.key(seed)
        kx, kq, kk, kv = jax.random.split(key, 4)
        B, S, H = (4, 256, HIDDEN)
        X = jax.random.normal(kx, (B, S, H), dtype=jnp.float32)
        W_Q = jax.random.normal(kq, (H, H), dtype=jnp.float32) / H
        W_K = jax.random.normal(kk, (H, H), dtype=jnp.float32) / H
        W_V = jax.random.normal(kv, (H, H), dtype=jnp.float32) / H
        return {'X': X, 'W_Q': W_Q, 'W_K': W_K, 'W_V': W_V}
    _L1_attn_in = _L1_attn_setup()

    def _L1_ffn_setup():
        import jax, jax.numpy as jnp
        import numpy as np
        B, S, H, I, E = (2, 256, 256, 176, 8)
        TOP_K = 2
        key = jax.random.key(seed)
        k0, k1, k2, k3, k4 = jax.random.split(key, 5)
        scale = float(np.sqrt(2.0 / (H + I)))
        return {'hidden_states': jax.random.normal(k0, (B, S, H), dtype=jnp.float32), 'router_w': jax.random.normal(k1, (E, H), dtype=jnp.float32) * H ** (-0.5), 'gate_w': jax.random.normal(k2, (E, I, H), dtype=jnp.float32) * scale, 'up_w': jax.random.normal(k3, (E, I, H), dtype=jnp.float32) * scale, 'down_w': jax.random.normal(k4, (E, H, I), dtype=jnp.float32) * scale}
    _L1_ffn_in = _L1_ffn_setup()
    _d = {'L0_attn_x': _L0_attn_in['x'], 'L0_attn_Wq': _L0_attn_in['Wq'], 'L0_attn_Wk': _L0_attn_in['Wk'], 'L0_attn_Wv': _L0_attn_in['Wv'], 'L0_attn_Wo': _L0_attn_in['Wo'], 'L0_attn_betas': _L0_attn_in['betas'], 'L0_ffn_gate_w': _L0_ffn_in['gate_w'], 'L0_ffn_w_gate_up': _L0_ffn_in['w_gate_up'], 'L0_ffn_w_down': _L0_ffn_in['w_down'], 'L0_ffn_shared_gate_up': _L0_ffn_in['shared_gate_up'], 'L0_ffn_shared_down': _L0_ffn_in['shared_down'], 'L1_attn_W_Q': _L1_attn_in['W_Q'], 'L1_attn_W_K': _L1_attn_in['W_K'], 'L1_attn_W_V': _L1_attn_in['W_V'], 'L1_ffn_router_w': _L1_ffn_in['router_w'], 'L1_ffn_gate_w': _L1_ffn_in['gate_w'], 'L1_ffn_up_w': _L1_ffn_in['up_w'], 'L1_ffn_down_w': _L1_ffn_in['down_w']}
    _x0 = _d['L0_attn_x']
    _d['L0_attn_x'] = jax.random.normal(jax.random.fold_in(jax.random.key(seed), 1), (1, 1024, 256), dtype=_x0.dtype)
    del _x0
    return _d

def reference(L0_attn_x, L0_attn_Wq, L0_attn_Wk, L0_attn_Wv, L0_attn_Wo, L0_attn_betas, L0_ffn_gate_w, L0_ffn_w_gate_up, L0_ffn_w_down, L0_ffn_shared_gate_up, L0_ffn_shared_down, L1_attn_W_Q, L1_attn_W_K, L1_attn_W_V, L1_ffn_router_w, L1_ffn_gate_w, L1_ffn_up_w, L1_ffn_down_w):

    def _L0_attn_ref(x, Wq, Wk, Wv, Wo, betas):
        import jax, jax.numpy as jnp
        import numpy as np
        B, S, D = (2, 512, 256)
        H, DK, DV = (16, 128, 128)
        SEG = 64
        UPDATE = 'delta'
        CAUSAL = True
        Bsz, seq, _ = x.shape
        nseg = seq // SEG
        q = (x @ Wq).reshape(Bsz, seq, H, DK).transpose(0, 2, 1, 3)
        k = (x @ Wk).reshape(Bsz, seq, H, DK).transpose(0, 2, 1, 3)
        v = (x @ Wv).reshape(Bsz, seq, H, DV).transpose(0, 2, 1, 3)
        qs = q.reshape(Bsz, H, nseg, SEG, DK).transpose(2, 0, 1, 3, 4)
        ks_ = k.reshape(Bsz, H, nseg, SEG, DK).transpose(2, 0, 1, 3, 4)
        vs = v.reshape(Bsz, H, nseg, SEG, DV).transpose(2, 0, 1, 3, 4)
        causal_mask = jnp.tril(jnp.ones((SEG, SEG), bool))
        scale = DK ** 0.5
        beta = jax.nn.sigmoid(betas)

        def step(carry, seg):
            mem, z = carry
            qq, kk, vv = seg
            sigma_q = jax.nn.elu(qq) + 1.0
            scores = jnp.einsum('bhsk,bhtk->bhst', qq, kk) / scale
            if CAUSAL:
                scores = jnp.where(causal_mask, scores, -jnp.inf)
            att_dot = jax.nn.softmax(scores, axis=-1) @ vv
            att_mem = sigma_q @ mem / (sigma_q @ z)
            sigma_k = jax.nn.elu(kk) + 1.0
            if UPDATE == 'linear':
                mem_new = mem + jnp.einsum('bhsk,bhsv->bhkv', sigma_k, vv)
            else:
                delta = vv - sigma_k @ mem / (sigma_k @ z)
                mem_new = mem + jnp.einsum('bhsk,bhsv->bhkv', sigma_k, delta)
            z_new = z + sigma_k.sum(axis=-2, keepdims=True).transpose(0, 1, 3, 2)
            att = beta * att_mem + (1.0 - beta) * att_dot
            out = att.reshape(Bsz, SEG, H * DV) @ Wo
            return ((mem_new, z_new), out)
        mem0 = jnp.zeros((Bsz, H, DK, DV), x.dtype)
        z0 = jnp.ones((Bsz, H, DK, 1), x.dtype) / DK
        _, outs = jax.lax.scan(step, (mem0, z0), (qs, ks_, vs))
        return outs.transpose(1, 0, 2, 3).reshape(Bsz, seq, D)

    def _L0_ffn_ref(hidden_states, gate_w, w_gate_up, w_down, shared_gate_up, shared_down):
        import jax, jax.numpy as jnp
        import numpy as np
        H = 256
        I = 176
        E = 16
        K = 2
        SI = I * 2

        def _swiglu(gu, inter):
            g, u = (gu[..., :inter], gu[..., inter:])
            return jax.nn.silu(g) * u
        orig_shape = hidden_states.shape
        x = hidden_states.reshape(-1, H)
        logits = jnp.einsum('th,eh->te', x, gate_w)
        scores = jax.nn.softmax(logits, axis=-1)
        topk_w, topk_idx = jax.lax.top_k(scores, K)
        combine = jnp.sum(jax.nn.one_hot(topk_idx, E, dtype=x.dtype) * topk_w[..., None], axis=1)
        gu = jnp.einsum('th,ehj->etj', x, w_gate_up)
        h = _swiglu(gu, I)
        y = jnp.einsum('eti,eih,te->th', h, w_down, combine)
        gu_s = x @ shared_gate_up
        y = y + _swiglu(gu_s, SI) @ shared_down
        return y.reshape(orig_shape)

    def _L1_attn_ref(X, W_Q, W_K, W_V):
        import jax, jax.numpy as jnp
        import numpy as np
        HIDDEN = 256
        GAMMA = 0.96875
        SCALE_BASE = 64

        def _xpos(x, downscale=False):
            B, L, d = x.shape
            half = d // 2
            scale_vec = (jnp.arange(0, d, 2, dtype=jnp.float32) + 0.4 * d) / (1.4 * d)
            power = jnp.arange(L, dtype=jnp.float32) / SCALE_BASE
            scale = scale_vec[None, :] ** power[:, None]
            inv_freq = 1.0 / 10000.0 ** (jnp.arange(half, dtype=jnp.float32) / half)
            sinusoid = jnp.arange(L, dtype=jnp.float32)[:, None] * inv_freq[None, :]
            sin, cos = (jnp.sin(sinusoid), jnp.cos(sinusoid))
            if downscale:
                scale = 1.0 / scale
            sin_s = jnp.repeat(sin * scale, 2, axis=-1)
            cos_s = jnp.repeat(cos * scale, 2, axis=-1)
            x1 = x[..., 0::2]
            x2 = x[..., 1::2]
            rot = jnp.stack((-x2, x1), axis=-1).reshape(x.shape)
            return x * cos_s[None] + rot * sin_s[None]

        def _decay_matrix(L):
            n = jnp.arange(L)[:, None]
            m = jnp.arange(L)[None, :]
            mask = n >= m
            D = jnp.where(mask, GAMMA ** jnp.maximum(n - m, 0).astype(jnp.float32), 0.0)
            return D
        B, S, H = X.shape
        Q = _xpos(X @ W_Q)
        K = _xpos(X @ W_K, downscale=True)
        V = X @ W_V
        D = _decay_matrix(S)
        att = jnp.einsum('bnh,bmh->bnm', Q, K) * D[None]
        return att @ V

    def _L1_ffn_ref(hidden_states, router_w, gate_w, up_w, down_w):
        import jax, jax.numpy as jnp
        import numpy as np
        B, S, H, I, E = (2, 256, 256, 176, 8)
        TOP_K = 2
        b, s, h = hidden_states.shape
        e = router_w.shape[0]
        x = hidden_states.reshape(-1, h)
        logits = jnp.einsum('th,eh->te', x, router_w)
        top_vals, top_idx = jax.lax.top_k(logits, TOP_K)
        top_w = jax.nn.softmax(top_vals, axis=-1)
        expert = top_idx[:, 0]
        weight = top_w[:, 0]
        gate = jnp.einsum('th,eih->eti', x, gate_w)
        up = jnp.einsum('th,eih->eti', x, up_w)
        act = jax.nn.silu(gate) * up
        out_e = jnp.einsum('eti,ehi->eth', act, down_w)
        combine = jax.nn.one_hot(expert, e, dtype=x.dtype) * weight[:, None]
        out = jnp.einsum('eth,te->th', out_e, combine)
        return out.reshape(b, s, h)
    x = L0_attn_x
    x = x + _L0_attn_ref(_layernorm(x, axis=-1), L0_attn_Wq, L0_attn_Wk, L0_attn_Wv, L0_attn_Wo, L0_attn_betas)
    x = x + _L0_ffn_ref(_layernorm(x, axis=-1), L0_ffn_gate_w, L0_ffn_w_gate_up, L0_ffn_w_down, L0_ffn_shared_gate_up, L0_ffn_shared_down)
    x = x + _L1_attn_ref(_layernorm(x, axis=-1), L1_attn_W_Q, L1_attn_W_K, L1_attn_W_V)
    x = x + _L1_ffn_ref(_layernorm(x, axis=-1), L1_ffn_router_w, L1_ffn_gate_w, L1_ffn_up_w, L1_ffn_down_w)
    return x

_drawn_inputs = setup_inputs


def setup_inputs(seed=0):
    import zlib

    import numpy as np

    out = dict(_drawn_inputs(seed))
    spreads = {}
    factors = {'L0_attn_Wq': 3.739,
     'L0_attn_Wk': 3.565,
     'L0_ffn_gate_w': 3.831,
     'L0_ffn_w_gate_up': 4.658,
     'L0_ffn_w_down': 3.663}
    for name, (base, spread) in spreads.items():
        noise = np.random.default_rng([zlib.crc32(name.encode()), seed]).standard_normal(out[name].shape)
        drawn = base * np.exp(spread * noise) if base else spread * noise
        out[name] = jnp.asarray(drawn.astype(out[name].dtype))
    for name, factor in factors.items():
        out[name] = (out[name] * factor).astype(out[name].dtype)
    return out
```

```python
from contextlib import ExitStack

import concourse.bass as bass
from concourse import mybir

F32 = mybir.dt.float32
F32R = mybir.dt.float32r
BF16 = mybir.dt.bfloat16
ALU = mybir.AluOpType
ACT = mybir.ActivationFunctionType
AX = mybir.AxisListType

P = 128
T = 1024
D = 256
NT = T // P
KD = D // P
HALF = T // 2
TPH = NT // 2
EPS = 1e-5

H, DK, SEG = 16, 128, 64
NSEG = T // SEG
HQ = 4
NQ = H // HQ
GROUP = 2
MC = DK + 1
SCORE_SCALE = float(1.0 / DK ** 0.5)

GAMMA, SCALE_BASE = 0.96875, 64

INTER = 176
E0, E1 = 16, 8
SHARED = 2 * INTER
LARGE = 1e30


def fr(ap):
    return ap.bitcast(F32)


class NormSemaphores:

    def __init__(self, sem):
        self.stats_done, self.mean_var_done = sem("norm_stats_done"), sem("norm_mean_var_done")
        self.var_eps_done, self.power_set, self.rstd_done = sem("var_eps_done"), sem("power_set"), sem("rstd_done")
        self.xn_done, self.xT_done, self.xh_done, self.xl_done = (
            sem("xn_done"), sem("xT_done"), sem("xh_done"), sem("xl_done"))


class Norm:

    def __init__(self, nc, ctx, sems, n, x, xn, xh, xl, ident, banks):
        def sb(name, shape):
            return ctx.enter_context(nc.sbuf_tensor(f"{name}_norm{n}", shape, F32))

        self.x, self.xn, self.xh, self.xl, self.ident, self.banks = x, xn, xh, xl, ident, banks
        self.stats, self.mean_var = sb("stats", [P, NT, 6]), sb("mean_var", [P, NT, 2])
        self.var_eps, self.power, self.rstd = sb("var_eps", [P, NT]), sb("power", [P, NT]), sb("rstd", [P, NT])
        self.n, self.sems = n, sems
        self.xl_done, self.all_split = sems.xl_done, 4 * n + 4

    def pool_part(self, pool):
        sems, n = self.sems, self.n
        pool.memset(self.power[:, :], -0.5).then_inc(sems.power_set, 1)
        pool.wait_ge(sems.power_set, n + 1)
        pool.wait_ge(sems.var_eps_done, n + 1)
        pool.tensor_tensor(self.rstd[:, :], self.var_eps[:, :], self.power[:, :], ALU.pow)\
            .then_inc(sems.rstd_done, 1)

    def vector_part(self, dve, x_ready=None, x_count=0):
        sems, n = self.sems, self.n
        for j in range(NT):
            if x_ready is not None:
                dve.wait_ge(x_ready, x_count)
            dve.bn_stats(out=self.stats[:, j, :], in_=self.x[:, j, :]).then_inc(sems.stats_done, 1)
        for j in range(NT):
            dve.wait_ge(sems.stats_done, NT * n + j + 1)
            dve.bn_aggr(out=self.mean_var[:, j, :], in_=self.stats[:, j, :]).then_inc(sems.mean_var_done, 1)
        dve.wait_ge(sems.mean_var_done, NT * n + NT)
        dve.tensor_scalar(self.var_eps[:, :], self.mean_var[:, :, 1], EPS, None, ALU.add)\
           .then_inc(sems.var_eps_done, 1)
        dve.wait_ge(sems.rstd_done, n + 1)
        for j in range(NT):
            dve.tensor_scalar(self.xn[:, j, :], self.x[:, j, :], self.mean_var[:, j, 0:1],
                              self.rstd[:, j:j + 1], ALU.subtract, ALU.mult).then_inc(sems.xn_done, 1)
        for b in range(4):
            half, k = b // KD, b % KD
            dve.wait_ge(sems.xh_done, 4 * n + b + 1)
            dve.tensor_tensor(self.xl[:, k, half * HALF:(half + 1) * HALF], self.banks[b][:, :],
                              fr(self.xh[:, k, half * HALF:(half + 1) * HALF]), ALU.subtract)\
               .then_inc(sems.xl_done, 1)

    def tensor_part(self, pe, ident_ready, ident_count):
        sems, n = self.sems, self.n
        pe.wait_ge(ident_ready, ident_count)
        for b in range(4):
            half, k = b // KD, b % KD
            pe.wait_ge(sems.xn_done, NT * n + (half + 1) * TPH)
            for t in range(TPH):
                last = pe.transpose(self.banks[b][:, t * P:(t + 1) * P],
                                    self.xn[:, half * TPH + t, k * P:(k + 1) * P], self.ident[:, :])
            last.then_inc(sems.xT_done, 1)

    def scalar_part(self, act):
        sems, n = self.sems, self.n
        for b in range(4):
            half, k = b // KD, b % KD
            act.wait_ge(sems.xT_done, 4 * n + b + 1)
            act.activation(self.xh[:, k, half * HALF:(half + 1) * HALF], self.banks[b][:, :], ACT.Copy)\
               .then_inc(sems.xh_done, 1)


def split3(pe, out, stationary, moving, first, last, **kw):
    (sh, sl), (mh, ml) = stationary, moving
    pe.matmul(out, sh, mh, start=first, stop=False, **kw)
    pe.matmul(out, sh, ml, start=False, stop=False, **kw)
    return pe.matmul(out, sl, mh, start=False, stop=last, **kw)


def delta_attention(nc, outer, norm_sems, x, ident, ident_ready, scratch, x_in, Wq, Wk, Wv, Wo, betas, mask_in):
    with ExitStack() as ctx:
        def sb(name, shape, dt=F32):
            return ctx.enter_context(nc.sbuf_tensor(name, shape, dt))

        def sem(name):
            return outer.enter_context(nc.semaphore(name))

        def bank(name):
            return ctx.enter_context(nc.psum_tensor(name, [P, HALF], F32))

        W = [bank(f"work{i}") for i in range(4)]
        KQ = [bank(f"readings{g}") for g in range(2)]
        MM = [bank(f"memory{g}") for g in range(2)]

        xh, xl = sb("xh", [P, KD, T], F32R), sb("xl", [P, KD, T], F32R)
        w_high = [sb(f"w_high{i}", [P, KD, HQ * DK], F32R) for i in range(2)]
        w_low = [sb(f"w_low{i}", [P, KD, HQ * DK], F32R) for i in range(2)]
        w_stage = sb("w_stage", [P, KD, HQ * DK])
        wo = sb("wo", [P, H, D])
        ones = sb("ones", [P, 1])
        mask = sb("mask", [P, SEG])
        beta_t, beta_e = sb("beta_t", [P, H]), sb("beta_e", [P, H])
        beta, one_less_beta = sb("beta", [P, H]), sb("one_less_beta", [P, H])
        beta_q, one_less_q = sb("beta_q", [P, HQ]), sb("one_less_q", [P, HQ])
        seed_row, ones_row = sb("seed_row", [1, GROUP * MC]), sb("ones_row", [1, P])
        qT, kT = sb("qT", [P, HQ, T]), sb("kT", [P, HQ, T])
        e = [sb(f"exp{i}", [P, HALF]) for i in range(2)]
        sqk = sb("sigma", [P, HQ, NT, 4, SEG])
        skt = sb("sigma_k_tokens", [P, HQ, NT, DK])
        v = sb("v", [P, NT, HQ * DK])
        read = sb("memory_reading", [P, HQ, NT, DK])
        att = sb("attT", [P, HQ, T])
        mz = [sb(f"memory_copy{g}", [P, GROUP, MC]) for g in range(2)]
        nr = [sb(f"denominators{g}", [P, GROUP]) for g in range(2)]
        dl = [[sb(f"minus_delta{g}{par}", [P, GROUP, MC]) for par in range(2)] for g in range(2)]
        sm = sb("scores", [P, NT, SEG])
        mx, ssum, rs = sb("score_max", [P, NT]), sb("exp_sum", [P, NT]), sb("exp_sum_inverse", [P, NT])
        probs = sb("probs", [P, NT, P])
        pTs = e
        y_out = e[0][:, :].rearrange("p (i d) -> p i d", d=D)
        y_in = read[:, :, :, :].rearrange("p h t c -> p (h t c)")[:, 0:NT * D].rearrange("p (t d) -> p t d", d=D)

        x_loaded, mask_loaded, beta_loaded = sem("x_loaded"), sem("mask_loaded"), sem("beta_loaded")
        w_loaded, wo_loaded = sem("w_loaded"), sem("wo_loaded")
        consts_set, beta_exp, beta_step, beta_q_set = (
            sem("consts_set"), sem("beta_exp"), sem("beta_step"), sem("beta_q_set"))
        high_done, low_done = sem("w_high_done"), sem("w_split_done")
        proj_ready, qk_copied, exp_capped, sigma_ready = (
            sem("proj_ready"), sem("qk_copied"), sem("exp_capped"), sem("sigma_ready"))
        v_copied, skt_ready, skt_copied = sem("v_copied"), sem("sigma_k_turned"), sem("sigma_k_copied")
        upd_ready = [sem(f"memory_updated{g}") for g in range(2)]
        mem_copied = [sem(f"memory_copied{g}") for g in range(2)]
        kq_ready = [sem(f"readings_ready{g}") for g in range(2)]
        nr_ready = [sem(f"denominators_ready{g}") for g in range(2)]
        dl_ready = [sem(f"delta_ready{g}") for g in range(2)]
        read_ready = [sem(f"reading_scaled{g}") for g in range(2)]
        sc_ready, masked, max_ready, shifted, exp_ready = (
            sem("scores_ready"), sem("scores_masked"), sem("max_ready"), sem("scores_shifted"), sem("exp_ready"))
        sum_ready, inv_ready, p_ready = sem("exp_sum_ready"), sem("exp_sum_inverted"), sem("probs_ready")
        pT_ready, pTs_ready, bt_ready, bt_copied = (
            sem("probsT_ready"), sem("probsT_copied"), sem("local_ready"), sem("local_copied"))
        at_ready, att_ready, wo_ready, y_copied = (
            sem("readingT_ready"), sem("attT_ready"), sem("out_ready"), sem("out_copied"))
        y_stored, y_free, y_loaded = sem("out_stored"), sem("out_buffer_free"), sem("out_loaded")

        xn = att[:, 0:2, :].rearrange("p h (t d) -> p (h t) d", d=D)
        norm = Norm(nc, ctx, norm_sems, 0, x, xn, xh, xl, ident, W)

        def w_cols(w, turn):
            return w[:, bass.ts(turn, HQ * DK)].rearrange("(k p) n -> p k n", p=P)

        with nc.Block() as block:
            @block.sync
            def _(sp):
                x_tiles = x_in.rearrange("a (t p) n -> p (a t) n", p=P)
                for t in range(2):
                    sp.dma_start(x[:, t * TPH:(t + 1) * TPH, :], x_tiles[:, t * TPH:(t + 1) * TPH, :])\
                      .then_inc(x_loaded, 16)
                sp.sem_inc(y_free, 1)
                sp.dma_start(w_stage[:, :, :], w_cols(Wq, 0)).then_inc(w_loaded, 16)
                sp.dma_start(mask[:, :], mask_in).then_inc(mask_loaded, 16)
                sp.dma_start(beta_t[:, :], betas).then_inc(beta_loaded, 16)
                sp.dma_start(wo[:, :, :], Wo.rearrange("(i p) n -> p i n", p=P)).then_inc(wo_loaded, 16)

                def load_weights(w, turn, splits):
                    sp.wait_ge(low_done, splits)
                    sp.dma_start(w_stage[:, :, :], w_cols(w, turn)).then_inc(w_loaded, 16)

                def store_out(it):
                    tokens = scratch.rearrange("(s q h m) d -> s q h m d", s=NSEG, h=HQ, m=4)
                    for pp in range(2):
                        sp.wait_ge(y_copied, 2 * it + pp + 2)
                        for hh in range(GROUP):
                            sp.dma_start(tokens[:, bass.ds(it, 1), GROUP * pp + hh, :, :],
                                         y_out[hh * SEG:(hh + 1) * SEG, pp, :]).then_inc(y_stored, 16)
                    sp.wait_ge(y_stored, 64 * it + 64)

                load_weights(Wk, 0, 1)
                with sp.Fori(0, NQ - 1) as it:
                    load_weights(Wv, it, 3 * it + 2)
                    load_weights(Wq, it + 1, 3 * it + 3)
                    load_weights(Wk, it + 1, 3 * it + 4)
                    store_out(it)
                    sp.sem_inc(y_free, 1)
                load_weights(Wv, NQ - 1, 3 * NQ - 1)
                store_out(NQ - 1)
                sp.dma_start(y_in, scratch.rearrange("(t p) d -> p t d", p=P)).then_inc(y_loaded, 16)

            @block.gpsimd
            def _(pool):
                pool.memset(ones[:, :], 1.0).then_inc(consts_set, 1)
                pool.memset(ones_row[:, :], 1.0).then_inc(consts_set, 1)
                pool.memset(seed_row[:, :], 0.0).then_inc(consts_set, 1)
                pool.wait_ge(consts_set, 3)
                pool.memset(seed_row[:, :].rearrange("p (g c) -> p g c", g=GROUP)[:, :, DK:MC], -1.0 / DK)\
                    .then_inc(consts_set, 1)
                norm.pool_part(pool)
                for g in range(2):
                    for par in range(2):
                        rows = slice(par * SEG, (par + 1) * SEG)
                        pool.wait_ge(consts_set, 4 + 2 * (2 * g + par))
                        pool.memset(dl[g][par][:, :, :], 0.0).then_inc(consts_set, 1)
                        pool.wait_ge(consts_set, 5 + 2 * (2 * g + par))
                        pool.memset(dl[g][par][rows, :, DK:MC], -1.0).then_inc(consts_set, 1)
                pool.wait_ge(consts_set, 12)
                pool.memset(probs[:, :, :], 0.0).then_inc(consts_set, 1)

                one = ones[:, 0:1].unsqueeze(2).to_broadcast([P, KD, HQ * DK])

                def split(i, n):
                    pool.wait_ge(w_loaded, 16 * n)
                    pool.tensor_tensor(w_high[i][:, :, :], w_stage[:, :, :], one, ALU.mult).then_inc(high_done, 1)
                    pool.wait_ge(high_done, n)
                    pool.tensor_tensor(w_low[i][:, :, :], w_stage[:, :, :], fr(w_high[i][:, :, :]),
                                       ALU.subtract).then_inc(low_done, 1)

                split(0, 1)
                split(1, 2)
                with pool.Fori(0, NQ - 1) as it:
                    pool.wait_ge(proj_ready, 24 * it + 8)
                    split(0, 3 * it + 3)
                    pool.wait_ge(proj_ready, 24 * it + 24)
                    split(0, 3 * it + 4)
                    split(1, 3 * it + 5)
                pool.wait_ge(proj_ready, 24 * (NQ - 1) + 8)
                split(0, 3 * NQ)

            @block.tensor
            def _(pe):
                norm.tensor_part(pe, ident_ready, 2)
                pe.wait_ge(wo_loaded, 16)
                pe.wait_ge(norm.xl_done, norm.all_split)
                pe.wait_ge(consts_set, 13)

                def project(it):
                    for u in range(24):
                        b = W[u % 4]
                        if u == 0:
                            pe.wait_ge(y_copied, 2 * it + 1)
                            pe.wait_ge(low_done, 3 * it + 1)
                        if u == 8:
                            pe.wait_ge(low_done, 3 * it + 2)
                        if u == 16:
                            pe.wait_ge(low_done, 3 * it + 3)
                        if 4 <= u < 20:
                            pe.wait_ge(qk_copied, 16 * it + u - 3)
                        if u >= 20:
                            pe.wait_ge(v_copied, 8 * it + u - 19)
                        for k in range(KD):
                            if u < 16:
                                i, h, half = u // 8, u % 8 // 2, u % 2
                                cols = slice(half * HALF, (half + 1) * HALF)
                                last = split3(pe, b[:, :],
                                              (w_high[i][:, k, h * DK:(h + 1) * DK], w_low[i][:, k, h * DK:(h + 1) * DK]),
                                              (xh[:, k, cols], xl[:, k, cols]), k == 0, k == KD - 1)
                            else:
                                j = u - 16
                                last = split3(pe, b[:, :],
                                              (xh[:, k, j * P:(j + 1) * P], xl[:, k, j * P:(j + 1) * P]),
                                              (w_high[0][:, k, :], w_low[0][:, k, :]), k == 0, k == KD - 1)
                        last.then_inc(proj_ready, 1)

                def seed(g):
                    pe.matmul(MM[g][:, 0:GROUP * MC], ones_row[:, :], seed_row[:, :], start=True, stop=True,
                              skip_group_check=True).then_inc(upd_ready[g], 1)

                def turn_sigma_k(it):
                    for b in range(8):
                        h, half = b // 2, b % 2
                        if b < 4:
                            pe.wait_ge(v_copied, 8 * it + b + 5)
                        else:
                            pe.wait_ge(skt_copied, 8 * it + b - 3)
                        pe.wait_ge(sigma_ready, 16 * it + 9 + b)
                        for t in range(TPH):
                            pe.transpose(W[b % 4][:, t * P:(t + 1) * P],
                                         sqk[:, h, half * TPH + t, 2:4, :], ident[:, :])
                            last = pe.transpose(W[b % 4][0:SEG, t * P:(t + 1) * P],
                                                sqk[:, h, half * TPH + t, 0, :], ident[:, :])
                        last.then_inc(skt_ready, 1)

                def read_memory(it, g, s):
                    pair, par = s // 2, s % 2
                    pe.wait_ge(mem_copied[g], 16 * it + s + 1)
                    for hh in range(GROUP):
                        last = pe.matmul(KQ[g][:, hh * MC:(hh + 1) * MC],
                                         sqk[:, GROUP * g + hh, pair, 2 * par:2 * par + 2, :], mz[g][:, hh, :],
                                         start=True, stop=True)
                    last.then_inc(kq_ready[g], 1)

                def update_memory(it, g, s):
                    pair, par = s // 2, s % 2
                    pe.wait_ge(dl_ready[g], 15 * it + s + 1)
                    for hh in range(GROUP):
                        last = pe.matmul(MM[g][:, hh * MC:(hh + 1) * MC], skt[:, GROUP * g + hh, pair, :],
                                         dl[g][par][:, hh, :], start=False, stop=True, skip_group_check=True)
                    last.then_inc(upd_ready[g], 1)

                def scores(it, h, part):
                    if part == 0 and h:
                        pe.wait_ge(masked, 4 * it + h)
                    for s in range(8 * part, 8 * part + 8):
                        pair, par = s // 2, s % 2
                        last = pe.matmul(W[0][par * SEG:(par + 1) * SEG, pair * SEG:(pair + 1) * SEG],
                                         qT[:, h, s * SEG:(s + 1) * SEG], kT[:, h, s * SEG:(s + 1) * SEG],
                                         start=True, stop=True)
                    if part:
                        last.then_inc(sc_ready, 1)

                def turn_probs(it, h, half):
                    if half == 0:
                        pe.wait_ge(p_ready, 4 * it + h + 1)
                        if h:
                            pe.wait_ge(bt_copied, 8 * it + 2 * h)
                    b = W[1] if half == 0 else W[3]
                    for t in range(TPH):
                        last = pe.transpose(b[:, t * P:(t + 1) * P], probs[:, half * TPH + t, :], ident[:, :])
                    last.then_inc(pT_ready, 1)

                def local(it, h, half):
                    pe.wait_ge(pTs_ready, 8 * it + 2 * h + half + 1)
                    if half == 0 and h:
                        pe.wait_ge(bt_copied, 8 * it + 2 * h - 1)
                    b = W[2] if half == 0 else W[1]
                    for t in range(TPH):
                        last = pe.matmul(b[:, t * P:(t + 1) * P], v[:, half * TPH + t, h * DK:(h + 1) * DK],
                                         pTs[half][:, t * P:(t + 1) * P], start=True, stop=True)
                    last.then_inc(bt_ready, 1)

                def between(it, s, part):
                    h, at = s // 4, s % 4
                    if at == 0 and h:
                        local(it, h - 1, part)
                    if at == 2 and h < HQ - 1:
                        scores(it, h + 1, part)
                    if at == 3:
                        turn_probs(it, h, part)

                tail = [W[0], W[3], W[2], W[1]]

                def finish(it):
                    for u in range(8):
                        h, half = u // 2, u % 2
                        if u == 0:
                            pe.wait_ge(masked, 4 * it + 4)
                            for g in range(2):
                                pe.wait_ge(read_ready[g], 16 * it + 16)
                        if u == 1:
                            pe.wait_ge(pTs_ready, 8 * it + 8)
                        if u in (2, 3):
                            pe.wait_ge(bt_copied, 8 * it + 5 + u)
                        if u >= 4:
                            pe.wait_ge(att_ready, 8 * it + u - 3)
                        for t in range(TPH):
                            last = pe.transpose(tail[u % 4][:, t * P:(t + 1) * P],
                                                read[:, h, half * TPH + t, :], ident[:, :])
                        last.then_inc(at_ready, 1)
                    for pp in range(2):
                        pe.wait_ge(att_ready, 8 * it + 5 + 3 * pp)
                        rows = att[:, GROUP * pp:GROUP * (pp + 1), :].rearrange("p h t -> p (h t)")
                        for i in range(H):
                            last = pe.matmul(tail[pp][:, 0:D], rows[:, i::H], wo[:, i, :],
                                             start=(i == 0), stop=(i == H - 1))
                        last.then_inc(wo_ready, 1)

                with pe.Fori(0, NQ) as it:
                    project(it)
                    seed(0)
                    seed(1)
                    turn_sigma_k(it)
                    pe.wait_ge(skt_copied, 8 * it + 8)
                    scores(it, 0, 0)
                    scores(it, 0, 1)
                    for s in range(NSEG):
                        read_memory(it, 0, s)
                        between(it, s, 0)
                        if s:
                            update_memory(it, 1, s - 1)
                        read_memory(it, 1, s)
                        between(it, s, 1)
                        if s < NSEG - 1:
                            update_memory(it, 0, s)
                    local(it, HQ - 1, 0)
                    local(it, HQ - 1, 1)
                    finish(it)

            @block.scalar
            def _(act):
                norm.scalar_part(act)
                act.wait_ge(beta_loaded, 16)
                act.activation(beta_e[:, :], beta_t[:, :], ACT.Exp, scale=-1.0).then_inc(beta_exp, 1)

                def project(it):
                    for u in range(16):
                        i, h, half = u // 8, u % 8 // 2, u % 2
                        cols = slice(half * HALF, (half + 1) * HALF)
                        act.wait_ge(proj_ready, 24 * it + u + 1)
                        if u >= 2:
                            act.wait_ge(sigma_ready, 16 * it + u - 1)
                        act.activation(e[u % 2][:, :], W[u % 4][:, :], ACT.Exp)
                        act.activation((qT, kT)[i][:, h, cols], W[u % 4][:, :], ACT.Copy).then_inc(qk_copied, 1)
                    for j in range(NT):
                        act.wait_ge(proj_ready, 24 * it + 17 + j)
                        act.activation(v[:, j, :], W[j % 4][:, :], ACT.Copy).then_inc(v_copied, 1)

                def copy_memory(it, g, n):
                    act.wait_ge(upd_ready[g], 16 * it + n + 1)
                    act.activation(mz[g][:, :, :], MM[g][:, 0:GROUP * MC].rearrange("p (h c) -> p h c", h=GROUP),
                                   ACT.Copy).then_inc(mem_copied[g], 1)

                def copy_sigma_k(it):
                    for b in range(8):
                        h, half = b // 2, b % 2
                        act.wait_ge(skt_ready, 8 * it + b + 1)
                        act.activation(skt[:, h, half * TPH:(half + 1) * TPH, :],
                                       W[b % 4][:, :].rearrange("p (t c) -> p t c", t=TPH), ACT.Copy)\
                           .then_inc(skt_copied, 1)

                def scale_reading(it, g, s):
                    pair, par = s // 2, s % 2
                    rows = slice(SEG, P) if par == 0 else slice(0, SEG)
                    act.wait_ge(nr_ready[g], 16 * it + s + 1)
                    for hh in range(GROUP):
                        last = act.activation(read[rows, GROUP * g + hh, pair, :], KQ[g][rows, hh * MC:hh * MC + DK],
                                              ACT.Copy, scale=nr[g][rows, hh:hh + 1])
                    last.then_inc(read_ready[g], 1)

                def exp_scores(it, h):
                    act.wait_ge(shifted, 4 * it + h + 1)
                    act.activation(sm[:, :, :], sm[:, :, :], ACT.Exp).then_inc(exp_ready, 1)

                def copy_probs(it, h, half):
                    act.wait_ge(pT_ready, 8 * it + 2 * h + half + 1)
                    act.activation(pTs[half][:, :], (W[1], W[3])[half][:, :], ACT.Copy).then_inc(pTs_ready, 1)

                def scale_local(it, h, half):
                    act.wait_ge(bt_ready, 8 * it + 2 * h + half + 1)
                    act.activation(att[:, h, half * HALF:(half + 1) * HALF], (W[2], W[1])[half][:, :], ACT.Copy,
                                   scale=one_less_q[:, h:h + 1]).then_inc(bt_copied, 1)

                def between(it, s, part):
                    h, at = s // 4, s % 4
                    if at == 1 and part == 1:
                        exp_scores(it, h)
                    if at == 3 and part == 1:
                        copy_probs(it, h, 0)
                    if at == 0 and part == 0 and h:
                        copy_probs(it, h - 1, 1)
                    if at == 0 and part == 1 and h:
                        scale_local(it, h - 1, 0)
                    if at == 1 and part == 0 and h:
                        scale_local(it, h - 1, 1)

                with act.Fori(0, NQ) as it:
                    act.wait_ge(y_free, it + 1)
                    project(it)
                    act.wait_ge(beta_q_set, it + 1)
                    copy_memory(it, 0, 0)
                    copy_memory(it, 1, 0)
                    copy_sigma_k(it)
                    for s in range(NSEG):
                        scale_reading(it, 0, s)
                        if s:
                            copy_memory(it, 1, s)
                        between(it, s, 0)
                        scale_reading(it, 1, s)
                        if s < NSEG - 1:
                            copy_memory(it, 0, s + 1)
                        between(it, s, 1)
                    copy_probs(it, HQ - 1, 1)
                    scale_local(it, HQ - 1, 0)
                    scale_local(it, HQ - 1, 1)
                    for pp in range(2):
                        act.wait_ge(wo_ready, 2 * it + pp + 1)
                        act.activation(y_out[:, pp, :], (W[0], W[3])[pp][:, 0:D], ACT.Copy).then_inc(y_copied, 1)

            @block.vector
            def _(dve):
                norm.vector_part(dve, x_loaded, 32)
                dve.wait_ge(beta_exp, 1)
                dve.tensor_scalar(beta_e[:, :], beta_e[:, :], 1.0, None, ALU.add).then_inc(beta_step, 1)
                dve.wait_ge(beta_step, 1)
                dve.reciprocal(beta[:, :], beta_e[:, :]).then_inc(beta_step, 1)
                dve.wait_ge(beta_step, 2)
                dve.tensor_scalar(one_less_beta[:, :], beta[:, :], -1.0, 1.0, ALU.mult, ALU.add).then_inc(y_copied, 1)
                dve.wait_ge(y_copied, 1)
                dve.wait_ge(consts_set, 13)
                dve.wait_ge(mask_loaded, 16)

                def sigma(it):
                    for u in range(16):
                        i, h, half = u // 8, u % 8 // 2, u % 2
                        dve.wait_ge(qk_copied, 16 * it + u + 1)
                        dve.tensor_scalar(e[u % 2][:, :], e[u % 2][:, :], 1.0, None, ALU.min).then_inc(exp_capped, 1)
                        dve.wait_ge(exp_capped, 16 * it + u + 1)
                        halves = [t.rearrange("p (a b c) -> p a b c", b=2, c=SEG)
                                  for t in ((qT, kT)[i][:, h, half * HALF:(half + 1) * HALF], e[u % 2][:, :])]
                        for par in range(2):
                            block_at = 1 + par if i == 0 else 3 * par
                            last = dve.scalar_tensor_tensor(
                                out=sqk[:, h, half * TPH:(half + 1) * TPH, block_at, :], in0=halves[0][:, :, par, :],
                                scalar=0.0, in1=halves[1][:, :, par, :], op0=ALU.max, op1=ALU.add)
                        last.then_inc(sigma_ready, 1)

                def step(it, g, s):
                    pair, par = s // 2, s % 2
                    rows = slice(par * SEG, (par + 1) * SEG)
                    dve.wait_ge(kq_ready[g], 16 * it + s + 1)
                    both = KQ[g][:, 0:GROUP * MC].rearrange("p (h c) -> p h c", h=GROUP)
                    dve.reciprocal(nr[g][:, :], both[:, :, DK]).then_inc(nr_ready[g], 1)
                    if s == NSEG - 1:
                        return
                    dve.wait_ge(nr_ready[g], 16 * it + s + 1)
                    for hh in range(GROUP):
                        h = GROUP * g + hh
                        last = dve.scalar_tensor_tensor(
                            out=dl[g][par][rows, hh, 0:DK], in0=KQ[g][rows, hh * MC:hh * MC + DK],
                            scalar=nr[g][rows, hh:hh + 1], in1=v[rows, pair, h * DK:(h + 1) * DK],
                            op0=ALU.mult, op1=ALU.subtract)
                    last.then_inc(dl_ready[g], 1)

                def mask_scores(it, h):
                    dve.wait_ge(sc_ready, 4 * it + h + 1)
                    dve.scalar_tensor_tensor(
                        out=sm[:, :, :], in0=W[0][:, :].rearrange("p (a c) -> p a c", a=NT), scalar=SCORE_SCALE,
                        in1=mask[:, :].unsqueeze(1).to_broadcast([P, NT, SEG]), op0=ALU.mult, op1=ALU.add)\
                       .then_inc(masked, 1)

                def max_scores(it, h):
                    dve.wait_ge(masked, 4 * it + h + 1)
                    dve.tensor_reduce(mx[:, :], sm[:, :, :], AX.X, ALU.max).then_inc(max_ready, 1)

                def shift_scores(it, h):
                    dve.wait_ge(max_ready, 4 * it + h + 1)
                    dve.tensor_tensor(sm[:, :, :], sm[:, :, :], mx[:, :].unsqueeze(2).to_broadcast([P, NT, SEG]),
                                      ALU.subtract).then_inc(shifted, 1)

                def sum_exp(it, h):
                    dve.wait_ge(exp_ready, 4 * it + h + 1)
                    dve.tensor_reduce(ssum[:, :], sm[:, :, :], AX.X, ALU.add).then_inc(sum_ready, 1)
                    dve.wait_ge(sum_ready, 4 * it + h + 1)
                    dve.reciprocal(rs[:, :], ssum[:, :]).then_inc(inv_ready, 1)

                def probabilities(it, h):
                    dve.wait_ge(inv_ready, 4 * it + h + 1)
                    if h:
                        dve.wait_ge(pT_ready, 8 * it + 2 * h)
                    for par in range(2):
                        rows = slice(par * SEG, (par + 1) * SEG)
                        last = dve.tensor_tensor(probs[rows, :, par * SEG:(par + 1) * SEG], sm[rows, :, :],
                                                 rs[rows, :].unsqueeze(2).to_broadcast([SEG, NT, SEG]), ALU.mult)
                    last.then_inc(p_ready, 1)

                def between(it, s, part):
                    h, at = s // 4, s % 4
                    if at == 0:
                        (mask_scores, max_scores)[part](it, h)
                    if at == 1 and part == 0:
                        shift_scores(it, h)
                    if at == 2:
                        (sum_exp, probabilities)[part](it, h)

                with dve.Fori(0, NQ) as it:
                    dve.wait_ge(y_copied, 2 * it + 1)
                    dve.tensor_scalar(beta_q[:, :], beta[:, bass.ts(it, HQ)], 1.0, None, ALU.mult)
                    dve.tensor_scalar(one_less_q[:, :], one_less_beta[:, bass.ts(it, HQ)], 1.0, None, ALU.mult)\
                       .then_inc(beta_q_set, 1)
                    sigma(it)
                    dve.wait_ge(v_copied, 8 * it + 8)
                    for s in range(NSEG):
                        step(it, 0, s)
                        between(it, s, 0)
                        step(it, 1, s)
                        between(it, s, 1)
                    tail = [W[0], W[3], W[2], W[1]]
                    dve.wait_ge(bt_copied, 8 * it + 8)
                    dve.wait_ge(beta_q_set, it + 1)
                    for u in range(8):
                        h, half = u // 2, u % 2
                        dve.wait_ge(at_ready, 8 * it + u + 1)
                        src = tail[u % 4][:, :].rearrange("p (a b c) -> p a b c", b=2, c=SEG)
                        dst = att[:, h, half * HALF:(half + 1) * HALF].rearrange("p (a b c) -> p a b c", b=2, c=SEG)
                        for par in range(2):
                            last = dve.scalar_tensor_tensor(
                                out=dst[:, :, par, :], in0=src[:, :, 1 - par, :], scalar=beta_q[:, h:h + 1],
                                in1=dst[:, :, par, :], op0=ALU.mult, op1=ALU.add)
                        last.then_inc(att_ready, 1)
                dve.wait_ge(y_loaded, 16)
                for t in range(0, NT, 2):
                    dve.tensor_tensor(x[:, t:t + 2, :], x[:, t:t + 2, :], y_in[:, t:t + 2, :], ALU.add)


def experts_layer(nc, outer, norm_sems, x, ident, ident_ready, tag, experts, w, shared):
    with ExitStack() as ctx:
        def sb(name, shape, dt=F32):
            return ctx.enter_context(nc.sbuf_tensor(f"{name}_{tag}", shape, dt))

        def sem(name):
            return outer.enter_context(nc.semaphore(f"{name}_{tag}"))

        def bank(name):
            return ctx.enter_context(nc.psum_tensor(f"{name}_{tag}", [P, HALF], F32))

        E = experts
        n_tiles = E * INTER // P
        before = [("shared", j, min(P, SHARED - j * P)) for j in range(-(-SHARED // P))] if shared else []
        peeled = 2 + n_tiles % 2
        before += [("expert", j, P) for j in range(peeled)]
        turns = (n_tiles - peeled) // 2
        nb = len(before)
        par_of = [(q - nb) % 2 for q in range(nb)]
        par_count = [par_of.count(0), par_of.count(1)]
        total = nb + 2 * turns

        acc = [bank(f"down{i}") for i in range(4)]
        G, U, C, R = bank("gate"), bank("up"), bank("weights"), bank("routing")
        xh, xl = sb("xh", [P, KD, T], F32R), sb("xl", [P, KD, T], F32R)
        xn = sb("xn", [P, NT, D])
        stage = [sb(f"stage{i}", [P, 3, D]) for i in range(2)]
        w_high = [sb(f"w_high{i}", [P, 3, D], F32R) for i in range(2)]
        w_low = [sb(f"w_low{i}", [P, 3, D], F32R) for i in range(2)]
        ones = sb("ones", [P, 1])
        router = sb("router", [P, KD, E])
        router_high, router_low = sb("router_high", [P, KD, E], F32R), sb("router_low", [P, KD, E], F32R)
        rank = sb("rank", [P, E])
        spread32, spread = sb("spread32", [P, E * INTER]), sb("spread", [P, E * INTER], BF16)
        logitsT = sb("logitsT", [E, T])
        s, s2, comb = sb("route", [P, NT, E]), sb("route2", [P, NT, E]), sb("combine", [P, NT, E])
        eq = sb("equal", [P, NT, E])
        best = [sb(f"best{i}", [P, NT, E]) for i in range(2)]
        m = [sb(f"max{i}", [P, NT]) for i in range(6)]
        c_mid, c_rest = sb("c_mid", [E, T], BF16), sb("c_rest", [E, T])
        combT = sb("combT", [P, T], BF16)
        sg = [sb(f"silu{i}", [P, HALF]) for i in range(2)]
        ht = [sb(f"hidden{i}", [P, HALF]) for i in range(2)]
        h_high = [sb(f"h_high{i}", [P, HALF], F32R) for i in range(2)]
        h_low = [sb(f"h_low{i}", [P, HALF], F32R) for i in range(2)]

        loaded = [sem("tiles_loaded0"), sem("tiles_loaded1")]
        high_done, split_done, pool_step = sem("high_done"), sem("tile_split"), sem("pool_step")
        router_loaded, rank_loaded, spread_loaded = sem("router_loaded"), sem("rank_loaded"), sem("spread_loaded")
        router_split, spread_ready = sem("router_split"), sem("spread_ready")
        lT_ready, lT_copied, l_ready = sem("logitsT_ready"), sem("logitsT_copied"), sem("logits_ready")
        route = sem("route_step")
        to_exp, exp_done, comb_ready = sem("route_to_exp"), sem("route_exp"), sem("combine_ready")
        cT_ready, combT_ready = sem("combineT_ready"), sem("combine_parts")
        g_ready, c_ready, silu_done = sem("gate_ready"), sem("up_ready"), sem("silu_done")
        h1_done, h_done, hh_done, hl_done = sem("gated"), sem("weighted"), sem("h_high_done"), sem("h_low_done")
        down_done, added = sem("down_done"), sem("added")

        norm = Norm(nc, ctx, norm_sems, 1 if shared else 3, x, xn, xh, xl, ident, acc)

        def tile_sources(kind, j, rows):
            if kind == "shared":
                gate = w["shared_gate_up"][:, j * P:j * P + rows]
                up = w["shared_gate_up"][:, SHARED + j * P:SHARED + j * P + rows]
                down = w["shared_down"][j * P:j * P + rows, :]
            else:
                gate, up = w["gate"][:, bass.ts(j, P)], w["up"][:, bass.ts(j, P)]
                down = w["down"][bass.ts(j, P), :]
            return gate, up, down

        with nc.Block() as block:
            @block.sync
            def _(sp):
                def load(par, kind, j, rows):
                    gate, up, down = tile_sources(kind, j, rows)
                    for i, src in ((0, gate), (1, up)):
                        dst = stage[par][:, i, :].rearrange("p (k n) -> p k n", k=KD)[:, :, 0:rows]
                        sp.dma_start(dst, src.rearrange("(k p) n -> p k n", p=P)).then_inc(loaded[par], 16)
                    sp.dma_start(stage[par][0:rows, 2, :], down).then_inc(loaded[par], 16)

                sp.dma_start(router[:, :, :], w["router"].rearrange("(k p) e -> p k e", p=P))\
                  .then_inc(router_loaded, 16)
                sp.dma_start(rank[:, :], w["rank"]).then_inc(rank_loaded, 16)
                for q in range(nb):
                    if q == 2:
                        sp.dma_start(spread32[:, :], w["spread"]).then_inc(spread_loaded, 16)
                    if q >= 2:
                        sp.wait_ge(split_done, q - 1)
                    load(par_of[q], *before[q])
                with sp.Fori(0, turns) as i:
                    for a in range(2):
                        sp.wait_ge(split_done, 2 * i + nb + a - 1)
                        load(a, "expert", 2 * i + peeled + a, P)

            @block.gpsimd
            def _(pool):
                pool.memset(ones[:, :], 1.0).then_inc(pool_step, 1)
                pool.memset(combT[:, :], 0.0).then_inc(pool_step, 1)
                pool.wait_ge(pool_step, 2)

                def split(par, n):
                    pool.tensor_tensor(w_high[par][:, :, :], stage[par][:, :, :],
                                       ones[:, 0:1].unsqueeze(2).to_broadcast([P, 3, D]), ALU.mult)\
                        .then_inc(high_done, 1)
                    pool.wait_ge(high_done, n)
                    pool.tensor_tensor(w_low[par][:, :, :], stage[par][:, :, :], fr(w_high[par][:, :, :]),
                                       ALU.subtract).then_inc(split_done, 1)

                seen = [0, 0]
                norm.pool_part(pool)
                pool.wait_ge(router_loaded, 16)
                pool.tensor_tensor(router_high[:, :, :], router[:, :, :],
                                   ones[:, 0:1].unsqueeze(2).to_broadcast([P, KD, E]), ALU.mult)\
                    .then_inc(pool_step, 1)
                pool.wait_ge(pool_step, 3)
                pool.tensor_tensor(router_low[:, :, :], router[:, :, :], fr(router_high[:, :, :]),
                                   ALU.subtract).then_inc(router_split, 1)
                for q in range(nb):
                    par = par_of[q]
                    seen[par] += 1
                    pool.wait_ge(loaded[par], 48 * seen[par])
                    if q >= 2:
                        pool.wait_ge(down_done, 2 * q - 2)
                    split(par, q + 1)
                    if q == 1:
                        pool.wait_ge(spread_loaded, 16)
                        pool.tensor_copy(spread[:, :], spread32[:, :]).then_inc(spread_ready, 1)
                with pool.Fori(0, turns) as i:
                    for a in range(2):
                        pool.wait_ge(loaded[a], 48 * i + 48 * par_count[a] + 48)
                        pool.wait_ge(down_done, 4 * i + 2 * (nb + a) - 2)
                        split(a, 2 * i + nb + a + 1)

            def rows_of(q):
                return before[q][2] if q < nb else P

            @block.tensor
            def _(pe):
                norm.tensor_part(pe, ident_ready, 2)
                pe.wait_ge(norm.xl_done, norm.all_split)
                pe.wait_ge(router_split, 1)
                for half in range(2):
                    cols = slice(half * HALF, (half + 1) * HALF)
                    for k in range(KD):
                        last = split3(pe, (R, C)[half][0:E, :], (router_high[:, k, :], router_low[:, k, :]),
                                      (xh[:, k, cols], xl[:, k, cols]), k == 0, k == KD - 1)
                    last.then_inc(lT_ready, 1)
                pe.wait_ge(lT_copied, 2)
                for t in range(NT):
                    last = pe.transpose(R[:, t * E:(t + 1) * E], logitsT[:, t * P:(t + 1) * P], ident[0:E, 0:E])
                last.then_inc(l_ready, 1)

                def gate_up(n, half, par, rows, first=False):
                    cols = slice(half * HALF, (half + 1) * HALF)
                    for i, b in ((0, G), (1, U)):
                        if not first:
                            if i == 0:
                                pe.wait_ge(silu_done, n)
                            else:
                                pe.wait_ge(h_done, n)
                        for k in range(KD):
                            at = slice(k * P, k * P + rows)
                            last = split3(pe, b[0:rows, :], (w_high[par][:, i, at], w_low[par][:, i, at]),
                                          (xh[:, k, cols], xl[:, k, cols]), k == 0, k == KD - 1)
                        if i == 0:
                            last.then_inc(g_ready, 1)
                    return last

                def weights(j, half):
                    return pe.matmul(C[:, :], spread[:, bass.ts(j, P)], combT[:, half * HALF:(half + 1) * HALF],
                                     start=True, stop=True)

                def down(n, half, par, rows, first=False):
                    pe.wait_ge(hl_done, n + 1)
                    d = (w_high[par][0:rows, 2, :], w_low[par][0:rows, 2, :])
                    for t in range(TPH):
                        tok = slice(t * P, (t + 1) * P)
                        last = split3(pe, acc[2 * half + t // 2][:, t % 2 * D:(t % 2 + 1) * D],
                                      (h_high[half][0:rows, tok], h_low[half][0:rows, tok]), d,
                                      first and t % 2 == 0, True, skip_group_check=True)
                    last.then_inc(down_done, 1)

                def turn_combine():
                    pe.wait_ge(comb_ready, 1)
                    for half in range(2):
                        for t in range(TPH):
                            j = half * TPH + t
                            last = pe.transpose((R, C)[half][0:E, t * P:(t + 1) * P], comb[:, j, :], ident[:, :])
                        last.then_inc(cT_ready, 1)

                for q in range(nb):
                    kind, j, rows = before[q]
                    for half in range(2):
                        n = 2 * q + half
                        if half == 0:
                            pe.wait_ge(split_done, q + 1)
                        last = gate_up(n, half, par_of[q], rows, n == 0)
                        if n == 0:
                            turn_combine()
                        if kind == "shared":
                            last.then_inc(c_ready, 1)
                        else:
                            pe.wait_ge(combT_ready, 2)
                            pe.wait_ge(spread_ready, 1)
                            weights(j, half).then_inc(c_ready, 1)
                        if n:
                            pq = (n - 1) // 2
                            down(n - 1, (n - 1) % 2, par_of[pq], before[pq][2], pq == 0)
                with pe.Fori(0, turns) as i:
                    for a in range(2):
                        for half in range(2):
                            n = 4 * i + 2 * (nb + a) + half
                            if half == 0:
                                pe.wait_ge(split_done, 2 * i + nb + a + 1)
                            gate_up(n, half, a, P)
                            weights(2 * i + peeled + a, half).then_inc(c_ready, 1)
                            down(n - 1, 1 - half, a if half else 1 - a, P)
                down(2 * total - 1, 1, 1, P)

            @block.scalar
            def _(act):
                norm.scalar_part(act)
                for half in range(2):
                    act.wait_ge(lT_ready, half + 1)
                    act.activation(logitsT[:, half * HALF:(half + 1) * HALF], (R, C)[half][0:E, :], ACT.Copy)\
                       .then_inc(lT_copied, 1)
                act.wait_ge(to_exp, 1)
                if shared:
                    act.activation(s[:, :, :], s[:, :, :], ACT.Exp).then_inc(exp_done, 1)
                else:
                    act.activation(m[5][:, :], m[4][:, :], ACT.Exp).then_inc(exp_done, 1)

                def unit(n, half, rows, again=True):
                    act.wait_ge(g_ready, n + 1)
                    act.activation(sg[half][0:rows, :], G[0:rows, :], ACT.Silu).then_inc(silu_done, 1)
                    act.wait_ge(h_done, n + 1)
                    if again:
                        act.wait_ge(down_done, n - 1)
                    act.activation(h_high[half][0:rows, :], ht[half][0:rows, :], ACT.Copy).then_inc(hh_done, 1)

                for n in range(2 * nb):
                    unit(n, n % 2, rows_of(n // 2), n >= 2)
                with act.Fori(0, turns) as i:
                    for c in range(4):
                        unit(4 * i + 2 * nb + c, c % 2, P)

            @block.vector
            def _(dve):
                norm.vector_part(dve)
                steps = [0]

                def step(ins):
                    steps[0] += 1
                    ins.then_inc(route, 1)
                    dve.wait_ge(route, steps[0])

                def wide(a):
                    return a[:, :].unsqueeze(2).to_broadcast([P, NT, E])

                def first_max(src, mx, key, out):
                    step(dve.tensor_reduce(mx[:, :], src[:, :, :], AX.X, ALU.max))
                    step(dve.tensor_tensor(eq[:, :, :], src[:, :, :], wide(mx), ALU.is_equal))
                    step(dve.tensor_tensor(eq[:, :, :], eq[:, :, :],
                                           rank[:, :].unsqueeze(1).to_broadcast([P, NT, E]), ALU.mult))
                    step(dve.tensor_reduce(key[:, :], eq[:, :, :], AX.X, ALU.max))
                    step(dve.tensor_tensor(out[:, :, :], eq[:, :, :], wide(key), ALU.is_equal))

                dve.wait_ge(rank_loaded, 16)
                dve.wait_ge(l_ready, 1)
                step(dve.tensor_copy(s[:, :, :], R[:, 0:NT * E].rearrange("p (t e) -> p t e", t=NT)))
                if shared:
                    step(dve.tensor_reduce(m[0][:, :], s[:, :, :], AX.X, ALU.max))
                    dve.tensor_tensor(s[:, :, :], s[:, :, :], wide(m[0]), ALU.subtract).then_inc(to_exp, 1)
                    dve.wait_ge(exp_done, 1)
                    step(dve.tensor_reduce(m[1][:, :], s[:, :, :], AX.X, ALU.add))
                    step(dve.reciprocal(m[2][:, :], m[1][:, :]))
                    step(dve.tensor_tensor(s[:, :, :], s[:, :, :], wide(m[2]), ALU.mult))
                first_max(s, m[0], m[1], best[0])
                step(dve.scalar_tensor_tensor(out=s2[:, :, :], in0=best[0][:, :, :], scalar=-LARGE, in1=s[:, :, :],
                                              op0=ALU.mult, op1=ALU.add))
                if shared:
                    first_max(s2, m[2], m[3], best[1])
                    step(dve.tensor_tensor(best[0][:, :, :], best[0][:, :, :], best[1][:, :, :], ALU.add))
                    dve.tensor_tensor(comb[:, :, :], s[:, :, :], best[0][:, :, :], ALU.mult).then_inc(comb_ready, 1)
                else:
                    step(dve.tensor_reduce(m[2][:, :], s2[:, :, :], AX.X, ALU.max))
                    dve.tensor_tensor(m[4][:, :], m[2][:, :], m[0][:, :], ALU.subtract).then_inc(to_exp, 1)
                    dve.wait_ge(exp_done, 1)
                    step(dve.tensor_scalar(m[5][:, :], m[5][:, :], 1.0, None, ALU.add))
                    step(dve.reciprocal(m[1][:, :], m[5][:, :]))
                    dve.tensor_tensor(comb[:, :, :], best[0][:, :, :], wide(m[1]), ALU.mult).then_inc(comb_ready, 1)
                dve.wait_ge(pool_step, 2)
                for half in range(2):
                    cols = slice(half * HALF, (half + 1) * HALF)
                    src = (R, C)[half][0:E, :]
                    dve.wait_ge(cT_ready, half + 1)
                    step(dve.tensor_copy(combT[0:E, cols], src))
                    step(dve.tensor_tensor(c_rest[:, cols], src, combT[0:E, cols], ALU.subtract))
                    step(dve.tensor_copy(c_mid[:, cols], c_rest[:, cols]))
                    step(dve.tensor_copy(combT[32:32 + E, cols], c_mid[:, cols]))
                    step(dve.tensor_tensor(c_rest[:, cols], c_rest[:, cols], c_mid[:, cols], ALU.subtract))
                    dve.tensor_copy(combT[64:64 + E, cols], c_rest[:, cols]).then_inc(combT_ready, 1)

                def unit(n, half, rows, weighted):
                    dve.wait_ge(c_ready, n + 1)
                    dve.wait_ge(silu_done, n + 1)
                    gated = dve.tensor_tensor(ht[half][0:rows, :], sg[half][0:rows, :], U[0:rows, :], ALU.mult)
                    if weighted:
                        gated.then_inc(h1_done, 1)
                        dve.wait_ge(h1_done, n - 2 * (nb - peeled) + 1)
                        gated = dve.tensor_tensor(ht[half][:, :], ht[half][:, :], C[:, :], ALU.mult)
                    gated.then_inc(h_done, 1)
                    dve.wait_ge(hh_done, n + 1)
                    dve.tensor_tensor(h_low[half][0:rows, :], ht[half][0:rows, :], fr(h_high[half][0:rows, :]),
                                      ALU.subtract).then_inc(hl_done, 1)

                for n in range(2 * nb):
                    unit(n, n % 2, rows_of(n // 2), before[n // 2][0] == "expert")
                with dve.Fori(0, turns) as i:
                    for c in range(4):
                        unit(4 * i + 2 * nb + c, c % 2, P, True)
                dve.wait_ge(down_done, 2 * total)
                for b in range(4):
                    dve.tensor_tensor(x[:, 2 * b:2 * b + 2, :], x[:, 2 * b:2 * b + 2, :],
                                      acc[b][:, :].rearrange("p (t d) -> p t d", t=2), ALU.add).then_inc(added, 1)


def retention(nc, outer, norm_sems, x, ident, ident_ready, W_Q, W_K, W_V, tables, decay_in):
    with ExitStack() as ctx:
        def sb(name, shape, dt=F32):
            return ctx.enter_context(nc.sbuf_tensor(f"{name}_r", shape, dt))

        def sem(name):
            return outer.enter_context(nc.semaphore(f"{name}_r"))

        B = [ctx.enter_context(nc.psum_tensor(f"bank{i}_r", [P, HALF], F32)) for i in range(8)]
        xh, xl = sb("xh", [P, KD, T], F32R), sb("xl", [P, KD, T], F32R)
        xn = sb("xn", [P, NT, D])
        w_stage = [sb(f"w_stage{i}", [P, KD, D]) for i in range(3)]
        w_high = [sb(f"w_high{i}", [P, KD, D], F32R) for i in range(3)]
        w_low = [sb(f"w_low{i}", [P, KD, D], F32R) for i in range(3)]
        ones = sb("ones", [P, 1])
        cos_sin = sb("cos_sin", [P, 4, T])
        decay = sb("decay", [P, T])
        prod = [sb(f"product{i}", [P, 4, HALF]) for i in range(2)]
        turned = [sb(f"turned{i}", [P, KD, HALF]) for i in range(2)]
        qk_high = [sb(f"{n}_high", [P, KD, T], F32R) for n in "qk"]
        qk_low = [sb(f"{n}_low", [P, KD, T], F32R) for n in "qk"]
        v = sb("v", [P, NT, D])
        att = [sb(f"att{i}", [P, T - i * P]) for i in range(NT)]

        w_loaded = [sem(f"{n}_loaded") for n in ("w_q", "w_k", "w_v")]
        tables_loaded, decay_loaded, ones_set = sem("tables_loaded"), sem("decay_loaded"), sem("ones_set")
        high_done, w_split = sem("w_high_done"), sem("w_split")
        proj_ready, prod_done, turn_done = sem("proj_ready"), sem("products_done"), sem("turn_done")
        qk_high_done, qk_split = sem("qk_high_done"), sem("qk_split")
        v_ready, v_copied = sem("v_ready"), sem("v_copied")
        s_ready, att_done, out_ready, added = sem("scores_ready"), sem("att_done"), sem("out_ready"), sem("added")
        norm = Norm(nc, ctx, norm_sems, 2, x, xn, xh, xl, ident, B[0:4])

        units = [(0, 0), (1, 0), (0, 1), (1, 1)]
        unit_banks = [(B[4], B[5]), (B[6], B[7]), (B[0], B[1]), (B[2], B[3])]
        chunks = [(i, c, min(HALF, T - c)) for i in range(NT) for c in range(i * P, T, HALF)]
        chunks_to = [sum(1 for c in chunks if c[0] <= i) for i in range(NT)]

        with nc.Block() as block:
            @block.sync
            def _(sp):
                for i, w in enumerate((W_Q, W_K, W_V)):
                    sp.dma_start(w_stage[i][:, :, :], w.rearrange("(k p) n -> p k n", p=P)).then_inc(w_loaded[i], 16)
                for i, t in enumerate(tables):
                    sp.dma_start(cos_sin[:, i, :], t).then_inc(tables_loaded, 16)
                sp.dma_start(decay[:, :], decay_in).then_inc(decay_loaded, 16)

            @block.gpsimd
            def _(pool):
                pool.memset(ones[:, :], 1.0).then_inc(ones_set, 1)
                pool.wait_ge(ones_set, 1)
                for i in range(3):
                    pool.wait_ge(w_loaded[i], 16)
                    pool.tensor_tensor(w_high[i][:, :, :], w_stage[i][:, :, :],
                                       ones[:, 0:1].unsqueeze(2).to_broadcast([P, KD, D]), ALU.mult)\
                        .then_inc(high_done, 1)
                    pool.wait_ge(high_done, i + 1)
                    pool.tensor_tensor(w_low[i][:, :, :], w_stage[i][:, :, :], fr(w_high[i][:, :, :]),
                                       ALU.subtract).then_inc(w_split, 1)
                    if i == 0:
                        norm.pool_part(pool)
                for u in range(4):
                    if u >= 2:
                        pool.wait_ge(qk_split, u - 1)
                    for part, op in ((0, ALU.subtract), (1, ALU.add)):
                        pool.wait_ge(prod_done, 2 * u + part + 1)
                        pool.tensor_tensor(turned[u % 2][:, part, :], prod[u % 2][:, 2 * part, :],
                                           prod[u % 2][:, 2 * part + 1, :], op).then_inc(turn_done, 1)

            @block.tensor
            def _(pe):
                norm.tensor_part(pe, ident_ready, 2)
                pe.wait_ge(norm.xl_done, norm.all_split)
                for u, (qk, half) in enumerate(units):
                    pe.wait_ge(w_split, qk + 1)
                    cols = slice(half * HALF, (half + 1) * HALF)
                    for c in range(KD):
                        for k in range(KD):
                            last = split3(pe, unit_banks[u][c][:, :],
                                          (w_high[qk][:, k, c * P:(c + 1) * P], w_low[qk][:, k, c * P:(c + 1) * P]),
                                          (xh[:, k, cols], xl[:, k, cols]), k == 0, k == KD - 1)
                        last.then_inc(proj_ready, 1)
                pe.wait_ge(w_split, 3)
                for j in range(NT):
                    if j % 4 == 0:
                        pe.wait_ge(prod_done, j // 2 + 2)
                    for k in range(KD):
                        last = split3(pe, B[4 + j // 2][:, j % 2 * D:(j % 2 + 1) * D],
                                      (xh[:, k, j * P:(j + 1) * P], xl[:, k, j * P:(j + 1) * P]),
                                      (w_high[2][:, k, :], w_low[2][:, k, :]), k == 0, k == KD - 1)
                    last.then_inc(v_ready, 1)

                def scores(i):
                    for n, (tile, c, w) in enumerate(chunks):
                        if tile != i:
                            continue
                        pe.wait_ge(qk_split, 4)
                        if n >= 4:
                            pe.wait_ge(att_done, n - 3)
                        for k in range(KD):
                            last = split3(pe, B[n % 4][:, 0:w],
                                          (qk_high[1][:, k, i * P:(i + 1) * P], qk_low[1][:, k, i * P:(i + 1) * P]),
                                          (qk_high[0][:, k, c:c + w], qk_low[0][:, k, c:c + w]), k == 0, k == KD - 1)
                        last.then_inc(s_ready, 1)

                def output(i):
                    pe.wait_ge(v_copied, 4)
                    pe.wait_ge(att_done, chunks_to[i])
                    for j in range(i, NT):
                        last = pe.matmul(B[4 + j // 2][:, j % 2 * D:(j % 2 + 1) * D], att[i][:, (j - i) * P:(j - i + 1) * P],
                                         v[:, i, :], start=(i == 0 and j % 2 == 0), stop=True, skip_group_check=True)
                        if j == i and i % 2:
                            last.then_inc(out_ready, 1)

                scores(0)
                for i in range(NT):
                    if i < NT - 1:
                        scores(i + 1)
                    output(i)

            @block.scalar
            def _(act):
                norm.scalar_part(act)

                def high(u):
                    qk, half = units[u]
                    act.wait_ge(turn_done, 2 * u + 2)
                    act.activation(qk_high[qk][:, :, half * HALF:(half + 1) * HALF], turned[u % 2][:, :, :], ACT.Copy)\
                       .then_inc(qk_high_done, 1)

                def copy_v(b):
                    act.wait_ge(v_ready, 2 * b + 2)
                    act.activation(v[:, 2 * b:2 * b + 2, :], B[4 + b][:, :].rearrange("p (t d) -> p t d", t=2), ACT.Copy)\
                       .then_inc(v_copied, 1)

                high(0)
                high(1)
                copy_v(0)
                copy_v(1)
                high(2)
                copy_v(2)
                copy_v(3)
                high(3)

            @block.vector
            def _(dve):
                norm.vector_part(dve)
                dve.wait_ge(tables_loaded, 64)
                dve.wait_ge(decay_loaded, 16)

                def products(u):
                    qk, half = units[u]
                    cols = slice(half * HALF, (half + 1) * HALF)
                    even, odd = unit_banks[u]
                    cos, sin = cos_sin[:, 2 * qk, cols], cos_sin[:, 2 * qk + 1, cols]
                    dve.wait_ge(proj_ready, 2 * u + 2)
                    if u >= 2:
                        dve.wait_ge(turn_done, 2 * u - 2)
                    for part, (a, b) in enumerate(((even, odd), (odd, even))):
                        dve.tensor_tensor(prod[u % 2][:, 2 * part, :], a[:, :], cos, ALU.mult)
                        dve.tensor_tensor(prod[u % 2][:, 2 * part + 1, :], b[:, :], sin, ALU.mult).then_inc(prod_done, 1)

                def low(u):
                    qk, half = units[u]
                    cols = slice(half * HALF, (half + 1) * HALF)
                    dve.wait_ge(qk_high_done, u + 1)
                    dve.tensor_tensor(qk_low[qk][:, :, cols], turned[u % 2][:, :, :], fr(qk_high[qk][:, :, cols]),
                                      ALU.subtract).then_inc(qk_split, 1)

                for u in range(4):
                    products(u)
                    if u:
                        low(u - 1)
                low(3)
                for n, (i, c, w) in enumerate(chunks):
                    dve.wait_ge(s_ready, n + 1)
                    at = c - i * P
                    dve.tensor_tensor(att[i][:, at:at + w], B[n % 4][:, 0:w], decay[:, at:at + w], ALU.mult)\
                       .then_inc(att_done, 1)
                for b in range(4):
                    dve.wait_ge(out_ready, b + 1)
                    dve.tensor_tensor(x[:, 2 * b:2 * b + 2, :], x[:, 2 * b:2 * b + 2, :],
                                      B[4 + b][:, :].rearrange("p (t d) -> p t d", t=2), ALU.add).then_inc(added, 1)


def build(nc, ins, out):
    with ExitStack() as outer:
        x = outer.enter_context(nc.sbuf_tensor("x", [P, NT, D], F32))
        ident = outer.enter_context(nc.sbuf_tensor("ident", [P, P], F32))
        ident_ready = outer.enter_context(nc.semaphore("ident_ready"))
        norm_sems = NormSemaphores(lambda name: outer.enter_context(nc.semaphore(name)))
        with nc.Block() as block:
            @block.gpsimd
            def _(pool):
                pool.memset(ident[:, :], 0.0).then_inc(ident_ready, 1)
                pool.wait_ge(ident_ready, 1)
                pool.affine_select(out=ident[:, :], in_=ident[:, :], compare_op=ALU.not_equal, fill=1.0, base=0,
                                   pattern=[[-1, P]], channel_multiplier=1).then_inc(ident_ready, 1)
        scratch = nc.dram_tensor("attention_out", (T, D), F32).ap()
        delta_attention(nc, outer, norm_sems, x, ident, ident_ready, scratch, ins["L0_attn_x"], ins["L0_attn_Wq"], ins["L0_attn_Wk"],
                        ins["L0_attn_Wv"], ins["L0_attn_Wo"], ins["betas_by_head"], ins["causal_mask"])
        experts_layer(nc, outer, norm_sems, x, ident, ident_ready, "e0", E0, {
            "router": ins["router0"], "gate": ins["gate0"], "up": ins["up0"], "down": ins["down0"],
            "shared_gate_up": ins["L0_ffn_shared_gate_up"], "shared_down": ins["L0_ffn_shared_down"],
            "rank": ins["rank0"], "spread": ins["spread0"]}, True)
        retention(nc, outer, norm_sems, x, ident, ident_ready, ins["W_Q"], ins["W_K"], ins["L1_attn_W_V"],
                  [ins[n] for n in ("cos_q", "sin_q", "cos_k", "sin_k")], ins["decay"])
        experts_layer(nc, outer, norm_sems, x, ident, ident_ready, "e1", E1, {
            "router": ins["router1"], "gate": ins["gate1"], "up": ins["up1"], "down": ins["down1"],
            "rank": ins["rank1"], "spread": ins["spread1"]}, False)
        stored = outer.enter_context(nc.semaphore("stored"))
        with nc.Block() as block:
            @block.sync
            def _(sp):
                sp.dma_start(out.rearrange("a (t p) n -> p (a t) n", p=P), x[:, :, :]).then_inc(stored, 16)
                sp.wait_ge(stored, 16)


def shape_constants(np):
    s = np.arange(P)[:, None] % SEG
    tables = {"causal_mask": np.where(np.arange(SEG)[None, :] <= s, 0.0, -LARGE)}
    pair, pos = np.arange(P, dtype=np.float32), np.arange(T, dtype=np.float32)
    scale_vec = (2 * pair + np.float32(0.4 * D)) / np.float32(1.4 * D)
    scale = scale_vec[:, None] ** (pos / np.float32(SCALE_BASE))[None, :]
    angle = pos[None, :] * (np.float32(1) / np.float32(10000) ** (pair / np.float32(P)))[:, None]
    for name, sc in (("q", scale), ("k", np.float32(1) / scale)):
        tables[f"cos_{name}"], tables[f"sin_{name}"] = np.cos(angle) * sc, np.sin(angle) * sc
    distance = np.arange(T)[None, :] - np.arange(P)[:, None]
    tables["decay"] = np.where(distance >= 0, np.float32(GAMMA) ** np.maximum(distance, 0).astype(np.float32), 0.0)
    for n, e in ((0, E0), (1, E1)):
        tables[f"rank{n}"] = np.tile(e - np.arange(e), (P, 1))
        spread = np.zeros((P, e * INTER))
        for part in range(3):
            spread[32 * part + np.arange(e * INTER) // INTER, np.arange(e * INTER)] = 1.0
        tables[f"spread{n}"] = spread
    return {n: a.astype(np.float32) for n, a in tables.items()}


def layouts(np, inputs):
    a = {n: np.asarray(inputs[n]) for n in (
        "L0_attn_x", "L0_attn_Wq", "L0_attn_Wk", "L0_attn_Wv", "L0_attn_Wo",
        "L0_ffn_shared_gate_up", "L0_ffn_shared_down", "L1_attn_W_V")}
    for n in ("W_Q", "W_K"):
        a[n] = np.asarray(inputs[f"L1_attn_{n}"]).reshape(D, D // 2, 2).transpose(0, 2, 1).reshape(D, D)
    a["betas_by_head"] = np.asarray(inputs["L0_attn_betas"]).reshape(H, DK).T
    gate_up = np.asarray(inputs["L0_ffn_w_gate_up"]).transpose(1, 0, 2)
    a["gate0"] = gate_up[:, :, :INTER].reshape(D, E0 * INTER)
    a["up0"] = gate_up[:, :, INTER:].reshape(D, E0 * INTER)
    a["down0"] = np.asarray(inputs["L0_ffn_w_down"]).reshape(E0 * INTER, D)
    a["router0"] = np.asarray(inputs["L0_ffn_gate_w"]).T
    a["gate1"] = np.asarray(inputs["L1_ffn_gate_w"]).transpose(2, 0, 1).reshape(D, E1 * INTER)
    a["up1"] = np.asarray(inputs["L1_ffn_up_w"]).transpose(2, 0, 1).reshape(D, E1 * INTER)
    a["down1"] = np.asarray(inputs["L1_ffn_down_w"]).transpose(0, 2, 1).reshape(E1 * INTER, D)
    a["router1"] = np.asarray(inputs["L1_ffn_router_w"]).T
    return a


def kernel(**inputs):
    import numpy as np
    import concourse.bacc as bacc
    from concourse.bass_utils import run_bass_kernel_spmd as run

    nc = bacc.Bacc("TRN2", target_bir_lowering=False, num_devices=1)
    arrays = {**layouts(np, inputs), **shape_constants(np)}
    arrays = {n: np.ascontiguousarray(a) for n, a in arrays.items()}
    ins = {n: nc.dram_tensor(n, a.shape, F32, kind="ExternalInput").ap() for n, a in arrays.items()}
    out = nc.dram_tensor("out", (1, T, D), F32, kind="ExternalOutput").ap()
    build(nc, ins, out)
    r = run(nc, [arrays], core_ids=[0])
    return r.results[0]["out"]
```

```python
from contextlib import ExitStack

import concourse.bass as bass
from concourse import mybir

F32 = mybir.dt.float32
F32R = mybir.dt.float32r
BF16 = mybir.dt.bfloat16
ALU = mybir.AluOpType
ACT = mybir.ActivationFunctionType
AX = mybir.AxisListType

P = 128
T = 1024
D = 256
NT = T // P
KD = D // P
HALF = T // 2
TPH = NT // 2
EPS = 1e-5

H, DK, SEG = 16, 128, 64
NSEG = T // SEG
HQ = 4
NQ = H // HQ
GROUP = 2
MC = DK + 1
SCORE_SCALE = float(1.0 / DK ** 0.5)

GAMMA, SCALE_BASE = 0.96875, 64

INTER = 176
E0, E1 = 16, 8
SHARED = 2 * INTER
LARGE = 1e30


def fr(ap):
    return ap.bitcast(F32)


class NormSemaphores:

    def __init__(self, sem):
        self.stats_done, self.mean_var_done = sem("norm_stats_done"), sem("norm_mean_var_done")
        self.var_eps_done, self.power_set, self.rstd_done = sem("var_eps_done"), sem("power_set"), sem("rstd_done")
        self.xn_done, self.xT_done, self.xh_done, self.xl_done = (
            sem("xn_done"), sem("xT_done"), sem("xh_done"), sem("xl_done"))


class Norm:

    def __init__(self, nc, ctx, sems, n, x, xn, xh, xl, ident, banks):
        def sb(name, shape):
            return ctx.enter_context(nc.sbuf_tensor(f"{name}_norm{n}", shape, F32))

        self.x, self.xn, self.xh, self.xl, self.ident, self.banks = x, xn, xh, xl, ident, banks
        self.stats, self.mean_var = sb("stats", [P, NT, 6]), sb("mean_var", [P, NT, 2])
        self.var_eps, self.power, self.rstd = sb("var_eps", [P, NT]), sb("power", [P, NT]), sb("rstd", [P, NT])
        self.n, self.sems = n, sems
        self.xl_done, self.all_split = sems.xl_done, 4 * n + 4

    def pool_part(self, pool):
        sems, n = self.sems, self.n
        pool.memset(self.power[:, :], -0.5).then_inc(sems.power_set, 1)
        pool.wait_ge(sems.power_set, n + 1)
        pool.wait_ge(sems.var_eps_done, n + 1)
        pool.tensor_tensor(self.rstd[:, :], self.var_eps[:, :], self.power[:, :], ALU.pow)\
            .then_inc(sems.rstd_done, 1)

    def vector_part(self, dve, x_ready=None, x_count=0):
        sems, n = self.sems, self.n
        for j in range(NT):
            if x_ready is not None:
                dve.wait_ge(x_ready, x_count)
            dve.bn_stats(out=self.stats[:, j, :], in_=self.x[:, j, :]).then_inc(sems.stats_done, 1)
        for j in range(NT):
            dve.wait_ge(sems.stats_done, NT * n + j + 1)
            dve.bn_aggr(out=self.mean_var[:, j, :], in_=self.stats[:, j, :]).then_inc(sems.mean_var_done, 1)
        dve.wait_ge(sems.mean_var_done, NT * n + NT)
        dve.tensor_scalar(self.var_eps[:, :], self.mean_var[:, :, 1], EPS, None, ALU.add)\
           .then_inc(sems.var_eps_done, 1)
        dve.wait_ge(sems.rstd_done, n + 1)
        for j in range(NT):
            dve.tensor_scalar(self.xn[:, j, :], self.x[:, j, :], self.mean_var[:, j, 0:1],
                              self.rstd[:, j:j + 1], ALU.subtract, ALU.mult).then_inc(sems.xn_done, 1)
        for b in range(4):
            half, k = b // KD, b % KD
            dve.wait_ge(sems.xh_done, 4 * n + b + 1)
            dve.tensor_tensor(self.xl[:, k, half * HALF:(half + 1) * HALF], self.banks[b][:, :],
                              fr(self.xh[:, k, half * HALF:(half + 1) * HALF]), ALU.subtract)\
               .then_inc(sems.xl_done, 1)

    def tensor_part(self, pe, ident_ready, ident_count):
        sems, n = self.sems, self.n
        pe.wait_ge(ident_ready, ident_count)
        for b in range(4):
            half, k = b // KD, b % KD
            pe.wait_ge(sems.xn_done, NT * n + (half + 1) * TPH)
            for t in range(TPH):
                last = pe.transpose(self.banks[b][:, t * P:(t + 1) * P],
                                    self.xn[:, half * TPH + t, k * P:(k + 1) * P], self.ident[:, :])
            last.then_inc(sems.xT_done, 1)

    def scalar_part(self, act):
        sems, n = self.sems, self.n
        for b in range(4):
            half, k = b // KD, b % KD
            act.wait_ge(sems.xT_done, 4 * n + b + 1)
            act.activation(self.xh[:, k, half * HALF:(half + 1) * HALF], self.banks[b][:, :], ACT.Copy)\
               .then_inc(sems.xh_done, 1)


def split3(pe, out, stationary, moving, first, last, **kw):
    (sh, sl), (mh, ml) = stationary, moving
    pe.matmul(out, sh, mh, start=first, stop=False, **kw)
    pe.matmul(out, sh, ml, start=False, stop=False, **kw)
    return pe.matmul(out, sl, mh, start=False, stop=last, **kw)


def delta_attention(nc, outer, norm_sems, x, ident, ident_ready, scratch, x_in, Wq, Wk, Wv, Wo, betas, mask_in):
    with ExitStack() as ctx:
        def sb(name, shape, dt=F32):
            return ctx.enter_context(nc.sbuf_tensor(name, shape, dt))

        def sem(name):
            return outer.enter_context(nc.semaphore(name))

        def bank(name):
            return ctx.enter_context(nc.psum_tensor(name, [P, HALF], F32))

        A = [bank(f"ahead{i}") for i in range(2)]
        L = [bank(f"local{i}") for i in range(2)]
        KQ = [bank(f"readings{g}") for g in range(2)]
        MM = [bank(f"memory{g}") for g in range(2)]

        xh, xl = sb("xh", [P, KD, T], F32R), sb("xl", [P, KD, T], F32R)
        w_high = [sb(f"w_high{i}", [P, KD, HQ * DK], F32R) for i in range(2)]
        w_low = [sb(f"w_low{i}", [P, KD, HQ * DK], F32R) for i in range(2)]
        w_stage = sb("w_stage", [P, KD, HQ * DK])
        wo = sb("wo", [P, H, D])
        ones = sb("ones", [P, 1])
        mask = sb("mask", [P, SEG])
        beta_t, beta_e = sb("beta_t", [P, H]), sb("beta_e", [P, H])
        beta, one_less_beta = sb("beta", [P, H]), sb("one_less_beta", [P, H])
        beta_q, one_less_q = sb("beta_q", [P, HQ]), sb("one_less_q", [P, HQ])
        seed_row, ones_row = sb("seed_row", [1, GROUP * MC]), sb("ones_row", [1, P])
        qT, kT = sb("qT", [P, HQ, T]), sb("kT", [P, HQ, T])
        sqk = sb("sigma", [P, HQ, NT, 4, SEG])
        skt = sb("sigma_k_tokens", [P, HQ, NT, DK])
        v = sb("v", [P, NT, HQ * DK])
        read = sb("memory_reading", [P, 2, HQ, TPH, DK])
        att = sb("attT", [P, 2, HQ, HALF])
        mz = [sb(f"memory_copy{g}", [P, GROUP, MC]) for g in range(2)]
        nr = [sb(f"denominators{g}", [P, GROUP]) for g in range(2)]
        dl = [[sb(f"minus_delta{g}{par}", [P, GROUP, MC]) for par in range(2)] for g in range(2)]
        sm = sb("scores", [P, NT, SEG])
        mx, ssum, rs = sb("score_max", [P, NT]), sb("exp_sum", [P, NT]), sb("exp_sum_inverse", [P, NT])
        probs = sb("probs", [P, NT, P])
        y_out = sb("out_rows", [P, D])
        x_space = x[:, :, :].rearrange("p t d -> p (t d)")
        e = [x_space[:, i * HALF:(i + 1) * HALF] for i in range(2)]
        pTs = [x_space[:, (2 + i) * HALF:(3 + i) * HALF] for i in range(2)]
        y_in = read[:, 0, :, :, :].rearrange("p h t c -> p (h t c)").rearrange("p (t d) -> p t d", d=D)

        x_loaded, mask_loaded, beta_loaded = sem("x_loaded"), sem("mask_loaded"), sem("beta_loaded")
        w_loaded, wo_loaded = sem("w_loaded"), sem("wo_loaded")
        consts_set, beta_exp, beta_step, beta_q_set = (
            sem("consts_set"), sem("beta_exp"), sem("beta_step"), sem("beta_q_set"))
        high_done, low_done = sem("w_high_done"), sem("w_split_done")
        proj_ready, qk_copied, exp_capped, sigma_ready = (
            sem("proj_ready"), sem("qk_copied"), sem("exp_capped"), sem("sigma_ready"))
        v_copied, skt_ready, skt_copied = sem("v_copied"), sem("sigma_k_turned"), sem("sigma_k_copied")
        upd_ready = [sem(f"memory_updated{g}") for g in range(2)]
        mem_copied = [sem(f"memory_copied{g}") for g in range(2)]
        kq_ready = [sem(f"readings_ready{g}") for g in range(2)]
        nr_ready = [sem(f"denominators_ready{g}") for g in range(2)]
        dl_ready = [sem(f"delta_ready{g}") for g in range(2)]
        read_ready = [sem(f"reading_scaled{g}") for g in range(2)]
        sc_ready, masked, max_ready, shifted, exp_ready = (
            sem("scores_ready"), sem("scores_masked"), sem("max_ready"), sem("scores_shifted"), sem("exp_ready"))
        sum_ready, inv_ready, p_ready = sem("exp_sum_ready"), sem("exp_sum_inverted"), sem("probs_ready")
        pT_ready, pTs_ready, bt_ready, bt_copied = (
            sem("probsT_ready"), sem("probsT_copied"), sem("local_ready"), sem("local_copied"))
        at_ready, att_ready, wo_ready, y_copied = (
            sem("readingT_ready"), sem("attT_ready"), sem("out_ready"), sem("out_copied"))
        y_stored, y_loaded, x_reloaded, x_added = (
            sem("out_stored"), [sem(f"out_loaded{i}") for i in range(2)], sem("x_reloaded"), sem("x_added"))

        xn = att[:, 0, :, :].rearrange("p h t -> p (h t)").rearrange("p (t d) -> p t d", d=D)
        norm = Norm(nc, ctx, norm_sems, 0, x, xn, xh, xl, ident, [*A, *L])

        STAGES, STEPS = 2 * NQ, NSEG // 2
        PROJECT_AT = {0: [0], 1: [1], 2: [2], 3: [3], 4: [4], 5: [5], 6: [6], 7: [7], 8: [8], 9: [9, 10], 10: [11]}
        SIGMA_K_AT = {11: [0, 1], 12: [2], 14: [3]}
        SIGMA_K_BANK = (0, 1, 0, 0)
        OUT_AT = {12: range(0, 3), 13: range(3, 8), 14: range(8, 10), 15: range(10, 16)}
        READINGS_AT = {1: 0, 3: 1, 4: 2, 5: 3}
        READINGS_BANK = (1, 1, 0, 1)

        def all_turns(engine, turn):
            turn(0, True, False)
            with engine.Fori(0, NQ - 2) as i:
                turn(i + 1, False, False)
            turn(NQ - 1, False, True)

        def w_cols(w, turn):
            return w[:, bass.ts(turn, HQ * DK)].rearrange("(k p) n -> p k n", p=P)

        with nc.Block() as block:
            @block.sync
            def _(sp):
                x_tiles = x_in.rearrange("a (t p) n -> p (a t) n", p=P)
                for t in range(2):
                    sp.dma_start(x[:, t * TPH:(t + 1) * TPH, :], x_tiles[:, t * TPH:(t + 1) * TPH, :])\
                      .then_inc(x_loaded, 16)
                sp.dma_start(w_stage[:, :, :], w_cols(Wq, 0)).then_inc(w_loaded, 16)
                sp.dma_start(mask[:, :], mask_in).then_inc(mask_loaded, 16)
                sp.dma_start(beta_t[:, :], betas).then_inc(beta_loaded, 16)

                def load_weights(w, turn, splits):
                    sp.wait_ge(low_done, splits)
                    sp.dma_start(w_stage[:, :, :], w_cols(w, turn)).then_inc(w_loaded, 16)

                def store_out(it, half, n):
                    tokens = scratch.rearrange("(b s q h m) d -> b s q h m d", b=2, s=STEPS, h=HQ, m=4)
                    sp.wait_ge(y_copied, n + 1)
                    for h in range(HQ):
                        sp.dma_start(tokens[half, :, bass.ds(it, 1), h, :, :],
                                     y_out[32 * h:32 * h + 32, :]).then_inc(y_stored, 16)

                load_weights(Wk, 0, 1)
                sp.dma_start(wo[:, :, :], Wo.rearrange("(i p) n -> p i n", p=P)).then_inc(wo_loaded, 16)
                load_weights(Wv, 0, 2)
                load_weights(Wq, 0, 3)
                load_weights(Wk, 0, 4)

                def turn(it, first, last):
                    load_weights(Wv, it, 6 * it + 5)
                    if not first:
                        store_out(it - 1, 0, 2 * it - 2)
                    if not last:
                        load_weights(Wq, it + 1, 6 * it + 6)
                        load_weights(Wk, it + 1, 6 * it + 7)
                        load_weights(Wv, it + 1, 6 * it + 8)
                    if not first:
                        store_out(it - 1, 1, 2 * it - 1)
                    if not last:
                        load_weights(Wq, it + 1, 6 * it + 9)
                        load_weights(Wk, it + 1, 6 * it + 10)

                all_turns(sp, turn)
                sp.wait_ge(bt_ready, 4 * STAGES)
                sp.dma_start(x[:, :, :], x_tiles).then_inc(x_reloaded, 16)
                y_tiles = scratch.rearrange("(t p) d -> p t d", p=P)
                for half in range(2):
                    store_out(NQ - 1, half, STAGES - 2 + half)
                    sp.wait_ge(y_stored, 64 * (STAGES - 1 + half))
                    sp.dma_start(y_in[:, half * TPH:(half + 1) * TPH, :], y_tiles[:, half * TPH:(half + 1) * TPH, :])\
                      .then_inc(y_loaded[half], 16)

            @block.gpsimd
            def _(pool):
                pool.memset(ones[:, :], 1.0).then_inc(consts_set, 1)
                pool.memset(ones_row[:, :], 1.0).then_inc(consts_set, 1)
                pool.memset(seed_row[:, :], 0.0).then_inc(consts_set, 1)
                pool.wait_ge(consts_set, 3)
                pool.memset(seed_row[:, :].rearrange("p (g c) -> p g c", g=GROUP)[:, :, DK:MC], -1.0 / DK)\
                    .then_inc(consts_set, 1)
                norm.pool_part(pool)
                for g in range(2):
                    for par in range(2):
                        rows = slice(par * SEG, (par + 1) * SEG)
                        pool.wait_ge(consts_set, 4 + 2 * (2 * g + par))
                        pool.memset(dl[g][par][:, :, :], 0.0).then_inc(consts_set, 1)
                        pool.wait_ge(consts_set, 5 + 2 * (2 * g + par))
                        pool.memset(dl[g][par][rows, :, DK:MC], -1.0).then_inc(consts_set, 1)
                pool.wait_ge(consts_set, 12)
                pool.memset(probs[:, :, :], 0.0).then_inc(consts_set, 1)

                one = ones[:, 0:1].unsqueeze(2).to_broadcast([P, KD, HQ * DK])

                def split(i, n):
                    pool.wait_ge(w_loaded, 16 * n)
                    pool.tensor_tensor(w_high[i][:, :, :], w_stage[:, :, :], one, ALU.mult).then_inc(high_done, 1)
                    pool.wait_ge(high_done, n)
                    pool.tensor_tensor(w_low[i][:, :, :], w_stage[:, :, :], fr(w_high[i][:, :, :]),
                                       ALU.subtract).then_inc(low_done, 1)

                split(0, 1)
                split(1, 2)
                pool.wait_ge(proj_ready, 4)
                split(0, 3)

                with pool.Fori(0, STAGES - 1) as i:
                    pool.wait_ge(proj_ready, 12 * i + 12)
                    split(0, 3 * i + 4)
                    split(1, 3 * i + 5)
                    pool.wait_ge(proj_ready, 12 * i + 16)
                    split(0, 3 * i + 6)

            @block.tensor
            def _(pe):
                norm.tensor_part(pe, ident_ready, 2)
                pe.wait_ge(norm.xl_done, norm.all_split)
                pe.wait_ge(consts_set, 13)

                def project(n, half, u, free=None):
                    b = A[u % 2]
                    if free is not None:
                        pe.wait_ge(*free)
                    if u % 4 == 0:
                        pe.wait_ge(low_done, 3 * n + u // 4 + 1)
                    if 2 <= u < 10:
                        pe.wait_ge(qk_copied, 8 * n + u - 1)
                    if u >= 10:
                        pe.wait_ge(v_copied, 4 * n + u - 9)
                    for k in range(KD):
                        if u < 8:
                            i, h = u // 4, u % 4
                            cols = slice(half * HALF, (half + 1) * HALF)
                            last = split3(pe, b[:, :],
                                          (w_high[i][:, k, h * DK:(h + 1) * DK], w_low[i][:, k, h * DK:(h + 1) * DK]),
                                          (xh[:, k, cols], xl[:, k, cols]), k == 0, k == KD - 1)
                        else:
                            j = half * TPH + u - 8
                            last = split3(pe, b[:, :], (xh[:, k, j * P:(j + 1) * P], xl[:, k, j * P:(j + 1) * P]),
                                          (w_high[0][:, k, :], w_low[0][:, k, :]), k == 0, k == KD - 1)
                    last.then_inc(proj_ready, 1)

                def turn_sigma_k(n, half, h):
                    if h < 2:
                        pe.wait_ge(v_copied, 4 * n + h + 3)
                    else:
                        pe.wait_ge(skt_copied, 4 * n + 2 * h - 3)
                    pe.wait_ge(sigma_ready, 8 * n + h + 5)
                    b = A[SIGMA_K_BANK[h]]
                    for t in range(TPH):
                        pe.transpose(b[:, t * P:(t + 1) * P], sqk[:, h, half * TPH + t, 2:4, :], ident[:, :])
                        last = pe.transpose(b[0:SEG, t * P:(t + 1) * P], sqk[:, h, half * TPH + t, 0, :], ident[:, :])
                    last.then_inc(skt_ready, 1)

                def seed(g):
                    pe.matmul(MM[g][:, 0:GROUP * MC], ones_row[:, :], seed_row[:, :], start=True, stop=True,
                              skip_group_check=True).then_inc(upd_ready[g], 1)

                def read_memory(it, g, s):
                    pair, par = s // 2, s % 2
                    pe.wait_ge(mem_copied[g], 16 * it + s + 1)
                    for hh in range(GROUP):
                        last = pe.matmul(KQ[g][:, hh * MC:(hh + 1) * MC],
                                         sqk[:, GROUP * g + hh, pair, 2 * par:2 * par + 2, :], mz[g][:, hh, :],
                                         start=True, stop=True)
                    last.then_inc(kq_ready[g], 1)

                def update_memory(it, g, s):
                    pair, par = s // 2, s % 2
                    pe.wait_ge(dl_ready[g], 15 * it + s + 1)
                    for hh in range(GROUP):
                        last = pe.matmul(MM[g][:, hh * MC:(hh + 1) * MC], skt[:, GROUP * g + hh, pair, :],
                                         dl[g][par][:, hh, :], start=False, stop=True, skip_group_check=True)
                    last.then_inc(upd_ready[g], 1)

                def scores(n, half, pp):
                    for s in range(STEPS):
                        for hh in range(GROUP):
                            h, pair, par = GROUP * pp + hh, s // 2, s % 2
                            seg = slice((half * STEPS + s) * SEG, (half * STEPS + s + 1) * SEG)
                            at = (hh * TPH + pair) * SEG
                            last = pe.matmul(L[0][par * SEG:(par + 1) * SEG, at:at + SEG], qT[:, h, seg], kT[:, h, seg],
                                             start=True, stop=True)
                    last.then_inc(sc_ready, 1)

                def turn_probs(n, pp, hh):
                    for t in range(TPH):
                        last = pe.transpose(L[hh][:, t * P:(t + 1) * P], probs[:, hh * TPH + t, :], ident[:, :])
                    last.then_inc(pT_ready, 1)

                def local(n, half, pp, hh):
                    h = GROUP * pp + hh
                    pe.wait_ge(pTs_ready, 4 * n + h + 1)
                    for t in range(TPH):
                        last = pe.matmul(L[hh][:, t * P:(t + 1) * P], v[:, half * TPH + t, h * DK:(h + 1) * DK],
                                         pTs[hh][:, t * P:(t + 1) * P], start=True, stop=True)
                    last.then_inc(bt_ready, 1)

                def turn_reading(half, h):
                    for t in range(TPH):
                        last = pe.transpose(L[READINGS_BANK[h]][:, t * P:(t + 1) * P], read[:, half, h, t, :], ident[:, :])
                    last.then_inc(at_ready, 1)

                def project_out(half, part):
                    rows = att[:, half, :, :].rearrange("p h t -> p (h t)")
                    for i in part:
                        last = pe.matmul(A[1][:, 0:D], rows[:, i::H], wo[:, i, :], start=(i == 0), stop=(i == H - 1))
                        if i == H - 1:
                            last.then_inc(wo_ready, 1)

                def slot(it, half, m, first, last):
                    n = 2 * it + half
                    ahead, behind = not (last and half), not (first and not half)
                    if m == 0:
                        if behind:
                            pe.wait_ge(bt_copied, 4 * n - 1)
                        scores(n, half, 0)
                    if m == 6:
                        if behind:
                            pe.wait_ge(att_ready, 4 * n - 1)
                        pe.wait_ge(masked, 2 * n + 1)
                        scores(n, half, 1)
                    if behind and m in READINGS_AT:
                        h = READINGS_AT[m]
                        if h == 0:
                            pe.wait_ge(bt_copied, 4 * n)
                            for g in range(2):
                                pe.wait_ge(read_ready[g], STEPS * n)
                        elif h == 2:
                            pe.wait_ge(masked, 2 * n + 1)
                        else:
                            pe.wait_ge(att_ready, 4 * n - 4 + (h + 1) // 2)
                        turn_reading(1 - half, h)
                    if m == 8:
                        pe.wait_ge(p_ready, 2 * n + 1)
                        pe.wait_ge(masked, 2 * n + 2)
                        turn_probs(n, 0, 0)
                        if behind:
                            pe.wait_ge(att_ready, 4 * n)
                        turn_probs(n, 0, 1)
                    if m == 12:
                        pe.wait_ge(p_ready, 2 * n + 2)
                        for hh in range(2):
                            pe.wait_ge(bt_copied, 4 * n + hh + 1)
                            turn_probs(n, 1, hh)
                    if m in (10, 14):
                        for hh in range(2):
                            local(n, half, (m - 10) // 4, hh)
                    if ahead:
                        for u in PROJECT_AT.get(m, ()):
                            free = None
                            if u == 0:
                                free = skt_copied, 4 * n + 4
                            elif u == 1 and not first:
                                free = y_copied, n - 1
                            project(n + 1, 1 - half, u, free)
                        for h in SIGMA_K_AT.get(m, ()):
                            turn_sigma_k(n + 1, 1 - half, h)
                    if behind and m in OUT_AT:
                        if m == 12:
                            pe.wait_ge(att_ready, 4 * n)
                            if ahead:
                                pe.wait_ge(skt_copied, 4 * n + 6)
                            else:
                                pe.wait_ge(y_copied, n - 1)
                        project_out(1 - half, OUT_AT[m])

                def turn(it, first, last):
                    for half in range(2):
                        n = 2 * it + half
                        pe.wait_ge(sigma_ready, 8 * n + 8)
                        pe.wait_ge(skt_copied, 4 * n + 4)
                        for at in range(STEPS):
                            s = half * STEPS + at
                            read_memory(it, 0, s)
                            if s:
                                update_memory(it, 1, s - 1)
                            else:
                                seed(1)
                            slot(it, half, 2 * at, first, last)
                            read_memory(it, 1, s)
                            if s < NSEG - 1:
                                update_memory(it, 0, s)
                            elif not last:
                                seed(0)
                            slot(it, half, 2 * at + 1, first, last)

                for u in range(12):
                    project(0, 0, u)
                for h in range(HQ):
                    turn_sigma_k(0, 0, h)
                seed(0)
                pe.wait_ge(wo_loaded, 16)
                all_turns(pe, turn)
                n = STAGES
                for h in range(HQ):
                    if h == 0:
                        pe.wait_ge(bt_copied, 4 * n)
                        for g in range(2):
                            pe.wait_ge(read_ready[g], STEPS * n)
                    elif h != 2:
                        pe.wait_ge(att_ready, 4 * n - 4 + (h + 1) // 2)
                    turn_reading(1, h)
                pe.wait_ge(att_ready, 4 * n)
                pe.wait_ge(y_copied, n - 1)
                project_out(1, range(H))

            @block.scalar
            def _(act):
                norm.scalar_part(act)
                act.wait_ge(beta_loaded, 16)
                act.activation(beta_e[:, :], beta_t[:, :], ACT.Exp, scale=-1.0).then_inc(beta_exp, 1)

                def copy_projection(n, half, u):
                    act.wait_ge(proj_ready, 12 * n + u + 1)
                    if u < 8:
                        if u >= 2:
                            act.wait_ge(sigma_ready, 8 * n + u - 1)
                        act.activation(e[u % 2][:, :], A[u % 2][:, :], ACT.Exp)
                        act.activation((qT, kT)[u // 4][:, u % 4, half * HALF:(half + 1) * HALF], A[u % 2][:, :],
                                       ACT.Copy).then_inc(qk_copied, 1)
                    else:
                        act.activation(v[:, half * TPH + u - 8, :], A[u % 2][:, :], ACT.Copy).then_inc(v_copied, 1)

                def copy_sigma_k(n, half, h):
                    act.wait_ge(skt_ready, 4 * n + h + 1)
                    act.activation(skt[:, h, half * TPH:(half + 1) * TPH, :],
                                   A[SIGMA_K_BANK[h]][:, :].rearrange("p (t c) -> p t c", t=TPH), ACT.Copy)\
                       .then_inc(skt_copied, 1)

                def copy_memory(it, g, n):
                    act.wait_ge(upd_ready[g], 16 * it + n + 1)
                    act.activation(mz[g][:, :, :], MM[g][:, 0:GROUP * MC].rearrange("p (h c) -> p h c", h=GROUP),
                                   ACT.Copy).then_inc(mem_copied[g], 1)

                def scale_reading(it, g, s):
                    half, pair, par = s // STEPS, s % STEPS // 2, s % 2
                    rows = slice(SEG, P) if par == 0 else slice(0, SEG)
                    act.wait_ge(nr_ready[g], 16 * it + s + 1)
                    for hh in range(GROUP):
                        last = act.activation(read[rows, half, GROUP * g + hh, pair, :],
                                              KQ[g][rows, hh * MC:hh * MC + DK], ACT.Copy, scale=nr[g][rows, hh:hh + 1])
                    last.then_inc(read_ready[g], 1)

                def exp_scores(n, pp):
                    act.wait_ge(shifted, 2 * n + pp + 1)
                    act.activation(sm[:, :, :], sm[:, :, :], ACT.Exp).then_inc(exp_ready, 1)

                def copy_probs(n, pp):
                    for hh in range(2):
                        act.wait_ge(pT_ready, 4 * n + 2 * pp + hh + 1)
                        act.activation(pTs[hh][:, :], L[hh][:, :], ACT.Copy).then_inc(pTs_ready, 1)

                def scale_local(n, half, pp):
                    for hh in range(2):
                        h = GROUP * pp + hh
                        act.wait_ge(bt_ready, 4 * n + h + 1)
                        act.activation(att[:, half, h, :], L[hh][:, :], ACT.Copy, scale=one_less_q[:, h:h + 1])\
                           .then_inc(bt_copied, 1)

                def copy_out(n, first=False):
                    if not first:
                        act.wait_ge(y_stored, 64 * n)
                    act.wait_ge(wo_ready, n + 1)
                    act.activation(y_out[:, :], A[1][:, 0:D], ACT.Copy).then_inc(y_copied, 1)

                def slot(it, half, m, first, last):
                    n = 2 * it + half
                    if not (last and half):
                        for u in PROJECT_AT.get(m - 1, ()):
                            copy_projection(n + 1, 1 - half, u)
                        for h in SIGMA_K_AT.get(m - 1, ()):
                            copy_sigma_k(n + 1, 1 - half, h)
                    if m == 0 and not first:
                        copy_out(n - 2, None)
                    if m in (4, 9):
                        exp_scores(n, m // 8)
                    if m in (9, 13):
                        copy_probs(n, (m - 9) // 4)
                    if m in (11, 15):
                        if m == 11 and not half:
                            act.wait_ge(beta_q_set, it + 1)
                        scale_local(n, half, (m - 11) // 4)

                def turn(it, first, last):
                    for half in range(2):
                        for at in range(STEPS):
                            s = half * STEPS + at
                            copy_memory(it, 1, s)
                            scale_reading(it, 0, s)
                            slot(it, half, 2 * at, first, last)
                            if s < NSEG - 1:
                                copy_memory(it, 0, s + 1)
                            elif not last:
                                copy_memory(it, 0, NSEG)
                            scale_reading(it, 1, s)
                            slot(it, half, 2 * at + 1, first, last)

                for u in range(12):
                    copy_projection(0, 0, u)
                for h in range(HQ):
                    copy_sigma_k(0, 0, h)
                copy_memory(0, 0, 0)
                all_turns(act, turn)
                copy_out(STAGES - 2)
                copy_out(STAGES - 1)

            @block.vector
            def _(dve):
                norm.vector_part(dve, x_loaded, 32)
                dve.wait_ge(beta_exp, 1)
                dve.tensor_scalar(beta_e[:, :], beta_e[:, :], 1.0, None, ALU.add).then_inc(beta_step, 1)
                dve.wait_ge(beta_step, 1)
                dve.reciprocal(beta[:, :], beta_e[:, :]).then_inc(beta_step, 1)
                dve.wait_ge(beta_step, 2)
                dve.tensor_scalar(one_less_beta[:, :], beta[:, :], -1.0, 1.0, ALU.mult, ALU.add).then_inc(beta_step, 1)
                dve.wait_ge(consts_set, 13)
                dve.wait_ge(mask_loaded, 16)

                def sigma(n, half, u):
                    i, h = u // 4, u % 4
                    dve.wait_ge(qk_copied, 8 * n + u + 1)
                    dve.tensor_scalar(e[u % 2][:, :], e[u % 2][:, :], 1.0, None, ALU.min).then_inc(exp_capped, 1)
                    dve.wait_ge(exp_capped, 8 * n + u + 1)
                    halves = [t.rearrange("p (a b c) -> p a b c", b=2, c=SEG)
                              for t in ((qT, kT)[i][:, h, half * HALF:(half + 1) * HALF], e[u % 2][:, :])]
                    for par in range(2):
                        block_at = 1 + par if i == 0 else 3 * par
                        last = dve.scalar_tensor_tensor(
                            out=sqk[:, h, half * TPH:(half + 1) * TPH, block_at, :], in0=halves[0][:, :, par, :],
                            scalar=0.0, in1=halves[1][:, :, par, :], op0=ALU.max, op1=ALU.add)
                    last.then_inc(sigma_ready, 1)

                def step(it, g, s):
                    pair, par = s // 2, s % 2
                    rows = slice(par * SEG, (par + 1) * SEG)
                    dve.wait_ge(kq_ready[g], 16 * it + s + 1)
                    both = KQ[g][:, 0:GROUP * MC].rearrange("p (h c) -> p h c", h=GROUP)
                    dve.reciprocal(nr[g][:, :], both[:, :, DK]).then_inc(nr_ready[g], 1)
                    if s == NSEG - 1:
                        return
                    dve.wait_ge(nr_ready[g], 16 * it + s + 1)
                    for hh in range(GROUP):
                        h = GROUP * g + hh
                        last = dve.scalar_tensor_tensor(
                            out=dl[g][par][rows, hh, 0:DK], in0=KQ[g][rows, hh * MC:hh * MC + DK],
                            scalar=nr[g][rows, hh:hh + 1], in1=v[rows, pair, h * DK:(h + 1) * DK],
                            op0=ALU.mult, op1=ALU.subtract)
                    last.then_inc(dl_ready[g], 1)

                def mask_scores(n):
                    dve.wait_ge(sc_ready, n + 1)
                    dve.scalar_tensor_tensor(
                        out=sm[:, :, :], in0=L[0][:, :].rearrange("p (a c) -> p a c", a=NT), scalar=SCORE_SCALE,
                        in1=mask[:, :].unsqueeze(1).to_broadcast([P, NT, SEG]), op0=ALU.mult, op1=ALU.add)\
                       .then_inc(masked, 1)
                    dve.wait_ge(masked, n + 1)
                    dve.tensor_reduce(mx[:, :], sm[:, :, :], AX.X, ALU.max).then_inc(max_ready, 1)

                def shift_scores(n):
                    dve.wait_ge(max_ready, n + 1)
                    dve.tensor_tensor(sm[:, :, :], sm[:, :, :], mx[:, :].unsqueeze(2).to_broadcast([P, NT, SEG]),
                                      ALU.subtract).then_inc(shifted, 1)

                def sum_exp(n):
                    dve.wait_ge(exp_ready, n + 1)
                    dve.tensor_reduce(ssum[:, :], sm[:, :, :], AX.X, ALU.add).then_inc(sum_ready, 1)
                    dve.wait_ge(sum_ready, n + 1)
                    dve.reciprocal(rs[:, :], ssum[:, :]).then_inc(inv_ready, 1)

                def probabilities(n, before):
                    dve.wait_ge(inv_ready, n + 1)
                    if before:
                        dve.wait_ge(pT_ready, 2 * n)
                    for par in range(2):
                        rows = slice(par * SEG, (par + 1) * SEG)
                        last = dve.tensor_tensor(probs[rows, :, par * SEG:(par + 1) * SEG], sm[rows, :, :],
                                                 rs[rows, :].unsqueeze(2).to_broadcast([SEG, NT, SEG]), ALU.mult)
                    last.then_inc(p_ready, 1)

                def add_reading(n, half, h):
                    dve.wait_ge(at_ready, 4 * n + h + 1)
                    src = L[READINGS_BANK[h]][:, :].rearrange("p (a b c) -> p a b c", b=2, c=SEG)
                    dst = att[:, half, h, :].rearrange("p (a b c) -> p a b c", b=2, c=SEG)
                    for par in range(2):
                        last = dve.scalar_tensor_tensor(
                            out=dst[:, :, par, :], in0=src[:, :, 1 - par, :], scalar=beta_q[:, h:h + 1],
                            in1=dst[:, :, par, :], op0=ALU.mult, op1=ALU.add)
                    last.then_inc(att_ready, 1)

                def set_beta(it):
                    dve.tensor_scalar(beta_q[:, :], beta[:, bass.ts(it, HQ)], 1.0, None, ALU.mult)
                    dve.tensor_scalar(one_less_q[:, :], one_less_beta[:, bass.ts(it, HQ)], 1.0, None, ALU.mult)\
                       .then_inc(beta_q_set, 1)

                def slot(it, half, m, first, last):
                    n = 2 * it + half
                    ahead, behind = not (last and half), not (first and not half)
                    if ahead:
                        for u in PROJECT_AT.get(m - 2, ()):
                            if u < 8:
                                sigma(n + 1, 1 - half, u)
                    if behind and m - 1 in READINGS_AT:
                        add_reading(n - 1, 1 - half, READINGS_AT[m - 1])
                    if m in (1, 7):
                        mask_scores(2 * n + m // 7)
                    if m in (3, 8):
                        shift_scores(2 * n + m // 8)
                    if m in (5, 10):
                        sum_exp(2 * n + m // 10)
                    if m in (6, 11):
                        probabilities(2 * n + m // 11, behind or m == 11)
                    if m == 7 and not half:
                        set_beta(it)

                def turn(it, first, last):
                    for half in range(2):
                        dve.wait_ge(v_copied, 8 * it + 4 * half + 4)
                        for at in range(STEPS):
                            for g in range(2):
                                step(it, g, half * STEPS + at)
                                slot(it, half, 2 * at + g, first, last)

                for u in range(8):
                    sigma(0, 0, u)
                dve.wait_ge(beta_step, 3)
                all_turns(dve, turn)
                dve.wait_ge(beta_q_set, NQ)
                for h in range(HQ):
                    add_reading(STAGES - 1, 1, h)
                dve.wait_ge(x_reloaded, 16)
                for half in range(2):
                    tiles = slice(half * TPH, (half + 1) * TPH)
                    dve.wait_ge(y_loaded[half], 16)
                    dve.tensor_tensor(x[:, tiles, :], x[:, tiles, :], y_in[:, tiles, :], ALU.add).then_inc(x_added, 1)


def experts_layer(nc, outer, norm_sems, x, ident, ident_ready, tag, experts, w, shared):
    with ExitStack() as ctx:
        def sb(name, shape, dt=F32):
            return ctx.enter_context(nc.sbuf_tensor(f"{name}_{tag}", shape, dt))

        def sem(name):
            return outer.enter_context(nc.semaphore(f"{name}_{tag}"))

        def bank(name):
            return ctx.enter_context(nc.psum_tensor(f"{name}_{tag}", [P, HALF], F32))

        E = experts
        n_tiles = E * INTER // P
        before = [("shared", j, min(P, SHARED - j * P)) for j in range(-(-SHARED // P))] if shared else []
        peeled = 2 + n_tiles % 2
        before += [("expert", j, P) for j in range(peeled)]
        turns = (n_tiles - peeled) // 2
        nb = len(before)
        par_of = [(q - nb) % 2 for q in range(nb)]
        par_count = [par_of.count(0), par_of.count(1)]
        total = nb + 2 * turns

        acc = [bank(f"down{i}") for i in range(4)]
        G, U, C, R = bank("gate"), bank("up"), bank("weights"), bank("routing")
        xh, xl = sb("xh", [P, KD, T], F32R), sb("xl", [P, KD, T], F32R)
        xn = sb("xn", [P, NT, D])
        stage = [sb(f"stage{i}", [P, 3, D]) for i in range(2)]
        w_high = [sb(f"w_high{i}", [P, 3, D], F32R) for i in range(2)]
        w_low = [sb(f"w_low{i}", [P, 3, D], F32R) for i in range(2)]
        ones = sb("ones", [P, 1])
        router = sb("router", [P, KD, E])
        router_high, router_low = sb("router_high", [P, KD, E], F32R), sb("router_low", [P, KD, E], F32R)
        rank = sb("rank", [P, E])
        spread32, spread = sb("spread32", [P, E * INTER]), sb("spread", [P, E * INTER], BF16)
        logitsT = sb("logitsT", [E, T])
        s, s2, comb = sb("route", [P, NT, E]), sb("route2", [P, NT, E]), sb("combine", [P, NT, E])
        eq = sb("equal", [P, NT, E])
        best = [sb(f"best{i}", [P, NT, E]) for i in range(2)]
        m = [sb(f"max{i}", [P, NT]) for i in range(6)]
        c_mid, c_rest = sb("c_mid", [E, T], BF16), sb("c_rest", [E, T])
        combT = sb("combT", [P, T], BF16)
        sg = [sb(f"silu{i}", [P, HALF]) for i in range(2)]
        ht = [sb(f"hidden{i}", [P, HALF]) for i in range(2)]
        h_high = [sb(f"h_high{i}", [P, HALF], F32R) for i in range(2)]
        h_low = [sb(f"h_low{i}", [P, HALF], F32R) for i in range(2)]

        loaded = [sem("tiles_loaded0"), sem("tiles_loaded1")]
        high_done, split_done, pool_step = sem("high_done"), sem("tile_split"), sem("pool_step")
        router_loaded, rank_loaded, spread_loaded = sem("router_loaded"), sem("rank_loaded"), sem("spread_loaded")
        router_split, spread_ready = sem("router_split"), sem("spread_ready")
        lT_ready, lT_copied, l_ready = sem("logitsT_ready"), sem("logitsT_copied"), sem("logits_ready")
        route = sem("route_step")
        to_exp, exp_done, comb_ready = sem("route_to_exp"), sem("route_exp"), sem("combine_ready")
        cT_ready, combT_ready = sem("combineT_ready"), sem("combine_parts")
        g_ready, c_ready, silu_done = sem("gate_ready"), sem("up_ready"), sem("silu_done")
        h1_done, h_done, hh_done, hl_done = sem("gated"), sem("weighted"), sem("h_high_done"), sem("h_low_done")
        down_done, added = sem("down_done"), sem("added")

        norm = Norm(nc, ctx, norm_sems, 1 if shared else 3, x, xn, xh, xl, ident, acc)

        def tile_sources(kind, j, rows):
            if kind == "shared":
                gate = w["shared_gate_up"][:, j * P:j * P + rows]
                up = w["shared_gate_up"][:, SHARED + j * P:SHARED + j * P + rows]
                down = w["shared_down"][j * P:j * P + rows, :]
            else:
                gate, up = w["gate"][:, bass.ts(j, P)], w["up"][:, bass.ts(j, P)]
                down = w["down"][bass.ts(j, P), :]
            return gate, up, down

        with nc.Block() as block:
            @block.sync
            def _(sp):
                def load(par, kind, j, rows):
                    gate, up, down = tile_sources(kind, j, rows)
                    for i, src in ((0, gate), (1, up)):
                        dst = stage[par][:, i, :].rearrange("p (k n) -> p k n", k=KD)[:, :, 0:rows]
                        sp.dma_start(dst, src.rearrange("(k p) n -> p k n", p=P)).then_inc(loaded[par], 16)
                    sp.dma_start(stage[par][0:rows, 2, :], down).then_inc(loaded[par], 16)

                sp.dma_start(router[:, :, :], w["router"].rearrange("(k p) e -> p k e", p=P))\
                  .then_inc(router_loaded, 16)
                sp.dma_start(rank[:, :], w["rank"]).then_inc(rank_loaded, 16)
                for q in range(nb):
                    if q == 2:
                        sp.dma_start(spread32[:, :], w["spread"]).then_inc(spread_loaded, 16)
                    if q >= 2:
                        sp.wait_ge(split_done, q - 1)
                    load(par_of[q], *before[q])
                with sp.Fori(0, turns) as i:
                    for a in range(2):
                        sp.wait_ge(split_done, 2 * i + nb + a - 1)
                        load(a, "expert", 2 * i + peeled + a, P)

            @block.gpsimd
            def _(pool):
                pool.memset(ones[:, :], 1.0).then_inc(pool_step, 1)
                pool.memset(combT[:, :], 0.0).then_inc(pool_step, 1)
                pool.wait_ge(pool_step, 2)

                def split(par, n):
                    pool.tensor_tensor(w_high[par][:, :, :], stage[par][:, :, :],
                                       ones[:, 0:1].unsqueeze(2).to_broadcast([P, 3, D]), ALU.mult)\
                        .then_inc(high_done, 1)
                    pool.wait_ge(high_done, n)
                    pool.tensor_tensor(w_low[par][:, :, :], stage[par][:, :, :], fr(w_high[par][:, :, :]),
                                       ALU.subtract).then_inc(split_done, 1)

                seen = [0, 0]
                norm.pool_part(pool)
                pool.wait_ge(router_loaded, 16)
                pool.tensor_tensor(router_high[:, :, :], router[:, :, :],
                                   ones[:, 0:1].unsqueeze(2).to_broadcast([P, KD, E]), ALU.mult)\
                    .then_inc(pool_step, 1)
                pool.wait_ge(pool_step, 3)
                pool.tensor_tensor(router_low[:, :, :], router[:, :, :], fr(router_high[:, :, :]),
                                   ALU.subtract).then_inc(router_split, 1)
                for q in range(nb):
                    par = par_of[q]
                    seen[par] += 1
                    pool.wait_ge(loaded[par], 48 * seen[par])
                    if q >= 2:
                        pool.wait_ge(down_done, 2 * q - 2)
                    split(par, q + 1)
                    if q == 1:
                        pool.wait_ge(spread_loaded, 16)
                        pool.tensor_copy(spread[:, :], spread32[:, :]).then_inc(spread_ready, 1)
                with pool.Fori(0, turns) as i:
                    for a in range(2):
                        pool.wait_ge(loaded[a], 48 * i + 48 * par_count[a] + 48)
                        pool.wait_ge(down_done, 4 * i + 2 * (nb + a) - 2)
                        split(a, 2 * i + nb + a + 1)

            def rows_of(q):
                return before[q][2] if q < nb else P

            @block.tensor
            def _(pe):
                norm.tensor_part(pe, ident_ready, 2)
                pe.wait_ge(norm.xl_done, norm.all_split)
                pe.wait_ge(router_split, 1)
                for half in range(2):
                    cols = slice(half * HALF, (half + 1) * HALF)
                    for k in range(KD):
                        last = split3(pe, (R, C)[half][0:E, :], (router_high[:, k, :], router_low[:, k, :]),
                                      (xh[:, k, cols], xl[:, k, cols]), k == 0, k == KD - 1)
                    last.then_inc(lT_ready, 1)
                pe.wait_ge(lT_copied, 2)
                for t in range(NT):
                    last = pe.transpose(R[:, t * E:(t + 1) * E], logitsT[:, t * P:(t + 1) * P], ident[0:E, 0:E])
                last.then_inc(l_ready, 1)

                def gate_up(n, half, par, rows, first=False):
                    cols = slice(half * HALF, (half + 1) * HALF)
                    for i, b in ((0, G), (1, U)):
                        if not first:
                            if i == 0:
                                pe.wait_ge(silu_done, n)
                            else:
                                pe.wait_ge(h_done, n)
                        for k in range(KD):
                            at = slice(k * P, k * P + rows)
                            last = split3(pe, b[0:rows, :], (w_high[par][:, i, at], w_low[par][:, i, at]),
                                          (xh[:, k, cols], xl[:, k, cols]), k == 0, k == KD - 1)
                        if i == 0:
                            last.then_inc(g_ready, 1)
                    return last

                def weights(j, half):
                    return pe.matmul(C[:, :], spread[:, bass.ts(j, P)], combT[:, half * HALF:(half + 1) * HALF],
                                     start=True, stop=True)

                def down(n, half, par, rows, first=False):
                    pe.wait_ge(hl_done, n + 1)
                    d = (w_high[par][0:rows, 2, :], w_low[par][0:rows, 2, :])
                    for t in range(TPH):
                        tok = slice(t * P, (t + 1) * P)
                        last = split3(pe, acc[2 * half + t // 2][:, t % 2 * D:(t % 2 + 1) * D],
                                      (h_high[half][0:rows, tok], h_low[half][0:rows, tok]), d,
                                      first and t % 2 == 0, True, skip_group_check=True)
                    last.then_inc(down_done, 1)

                def turn_combine():
                    pe.wait_ge(comb_ready, 1)
                    for half in range(2):
                        for t in range(TPH):
                            j = half * TPH + t
                            last = pe.transpose((R, C)[half][0:E, t * P:(t + 1) * P], comb[:, j, :], ident[:, :])
                        last.then_inc(cT_ready, 1)

                for q in range(nb):
                    kind, j, rows = before[q]
                    for half in range(2):
                        n = 2 * q + half
                        if half == 0:
                            pe.wait_ge(split_done, q + 1)
                        last = gate_up(n, half, par_of[q], rows, n == 0)
                        if n == 0:
                            turn_combine()
                        if kind == "shared":
                            last.then_inc(c_ready, 1)
                        else:
                            pe.wait_ge(combT_ready, 2)
                            pe.wait_ge(spread_ready, 1)
                            weights(j, half).then_inc(c_ready, 1)
                        if n:
                            pq = (n - 1) // 2
                            down(n - 1, (n - 1) % 2, par_of[pq], before[pq][2], pq == 0)
                with pe.Fori(0, turns) as i:
                    for a in range(2):
                        for half in range(2):
                            n = 4 * i + 2 * (nb + a) + half
                            if half == 0:
                                pe.wait_ge(split_done, 2 * i + nb + a + 1)
                            gate_up(n, half, a, P)
                            weights(2 * i + peeled + a, half).then_inc(c_ready, 1)
                            down(n - 1, 1 - half, a if half else 1 - a, P)
                down(2 * total - 1, 1, 1, P)

            @block.scalar
            def _(act):
                norm.scalar_part(act)
                for half in range(2):
                    act.wait_ge(lT_ready, half + 1)
                    act.activation(logitsT[:, half * HALF:(half + 1) * HALF], (R, C)[half][0:E, :], ACT.Copy)\
                       .then_inc(lT_copied, 1)
                act.wait_ge(to_exp, 1)
                if shared:
                    act.activation(s[:, :, :], s[:, :, :], ACT.Exp).then_inc(exp_done, 1)
                else:
                    act.activation(m[5][:, :], m[4][:, :], ACT.Exp).then_inc(exp_done, 1)

                def unit(n, half, rows, again=True):
                    act.wait_ge(g_ready, n + 1)
                    act.activation(sg[half][0:rows, :], G[0:rows, :], ACT.Silu).then_inc(silu_done, 1)
                    act.wait_ge(h_done, n + 1)
                    if again:
                        act.wait_ge(down_done, n - 1)
                    act.activation(h_high[half][0:rows, :], ht[half][0:rows, :], ACT.Copy).then_inc(hh_done, 1)

                for n in range(2 * nb):
                    unit(n, n % 2, rows_of(n // 2), n >= 2)
                with act.Fori(0, turns) as i:
                    for c in range(4):
                        unit(4 * i + 2 * nb + c, c % 2, P)

            @block.vector
            def _(dve):
                norm.vector_part(dve)
                steps = [0]

                def step(ins):
                    steps[0] += 1
                    ins.then_inc(route, 1)
                    dve.wait_ge(route, steps[0])

                def wide(a):
                    return a[:, :].unsqueeze(2).to_broadcast([P, NT, E])

                def first_max(src, mx, key, out):
                    step(dve.tensor_reduce(mx[:, :], src[:, :, :], AX.X, ALU.max))
                    step(dve.tensor_tensor(eq[:, :, :], src[:, :, :], wide(mx), ALU.is_equal))
                    step(dve.tensor_tensor(eq[:, :, :], eq[:, :, :],
                                           rank[:, :].unsqueeze(1).to_broadcast([P, NT, E]), ALU.mult))
                    step(dve.tensor_reduce(key[:, :], eq[:, :, :], AX.X, ALU.max))
                    step(dve.tensor_tensor(out[:, :, :], eq[:, :, :], wide(key), ALU.is_equal))

                dve.wait_ge(rank_loaded, 16)
                dve.wait_ge(l_ready, 1)
                step(dve.tensor_copy(s[:, :, :], R[:, 0:NT * E].rearrange("p (t e) -> p t e", t=NT)))
                if shared:
                    step(dve.tensor_reduce(m[0][:, :], s[:, :, :], AX.X, ALU.max))
                    dve.tensor_tensor(s[:, :, :], s[:, :, :], wide(m[0]), ALU.subtract).then_inc(to_exp, 1)
                    dve.wait_ge(exp_done, 1)
                    step(dve.tensor_reduce(m[1][:, :], s[:, :, :], AX.X, ALU.add))
                    step(dve.reciprocal(m[2][:, :], m[1][:, :]))
                    step(dve.tensor_tensor(s[:, :, :], s[:, :, :], wide(m[2]), ALU.mult))
                first_max(s, m[0], m[1], best[0])
                step(dve.scalar_tensor_tensor(out=s2[:, :, :], in0=best[0][:, :, :], scalar=-LARGE, in1=s[:, :, :],
                                              op0=ALU.mult, op1=ALU.add))
                if shared:
                    first_max(s2, m[2], m[3], best[1])
                    step(dve.tensor_tensor(best[0][:, :, :], best[0][:, :, :], best[1][:, :, :], ALU.add))
                    dve.tensor_tensor(comb[:, :, :], s[:, :, :], best[0][:, :, :], ALU.mult).then_inc(comb_ready, 1)
                else:
                    step(dve.tensor_reduce(m[2][:, :], s2[:, :, :], AX.X, ALU.max))
                    dve.tensor_tensor(m[4][:, :], m[2][:, :], m[0][:, :], ALU.subtract).then_inc(to_exp, 1)
                    dve.wait_ge(exp_done, 1)
                    step(dve.tensor_scalar(m[5][:, :], m[5][:, :], 1.0, None, ALU.add))
                    step(dve.reciprocal(m[1][:, :], m[5][:, :]))
                    dve.tensor_tensor(comb[:, :, :], best[0][:, :, :], wide(m[1]), ALU.mult).then_inc(comb_ready, 1)
                dve.wait_ge(pool_step, 2)
                for half in range(2):
                    cols = slice(half * HALF, (half + 1) * HALF)
                    src = (R, C)[half][0:E, :]
                    dve.wait_ge(cT_ready, half + 1)
                    step(dve.tensor_copy(combT[0:E, cols], src))
                    step(dve.tensor_tensor(c_rest[:, cols], src, combT[0:E, cols], ALU.subtract))
                    step(dve.tensor_copy(c_mid[:, cols], c_rest[:, cols]))
                    step(dve.tensor_copy(combT[32:32 + E, cols], c_mid[:, cols]))
                    step(dve.tensor_tensor(c_rest[:, cols], c_rest[:, cols], c_mid[:, cols], ALU.subtract))
                    dve.tensor_copy(combT[64:64 + E, cols], c_rest[:, cols]).then_inc(combT_ready, 1)

                def unit(n, half, rows, weighted):
                    dve.wait_ge(c_ready, n + 1)
                    dve.wait_ge(silu_done, n + 1)
                    gated = dve.tensor_tensor(ht[half][0:rows, :], sg[half][0:rows, :], U[0:rows, :], ALU.mult)
                    if weighted:
                        gated.then_inc(h1_done, 1)
                        dve.wait_ge(h1_done, n - 2 * (nb - peeled) + 1)
                        gated = dve.tensor_tensor(ht[half][:, :], ht[half][:, :], C[:, :], ALU.mult)
                    gated.then_inc(h_done, 1)
                    dve.wait_ge(hh_done, n + 1)
                    dve.tensor_tensor(h_low[half][0:rows, :], ht[half][0:rows, :], fr(h_high[half][0:rows, :]),
                                      ALU.subtract).then_inc(hl_done, 1)

                for n in range(2 * nb):
                    unit(n, n % 2, rows_of(n // 2), before[n // 2][0] == "expert")
                with dve.Fori(0, turns) as i:
                    for c in range(4):
                        unit(4 * i + 2 * nb + c, c % 2, P, True)
                dve.wait_ge(down_done, 2 * total)
                for b in range(4):
                    dve.tensor_tensor(x[:, 2 * b:2 * b + 2, :], x[:, 2 * b:2 * b + 2, :],
                                      acc[b][:, :].rearrange("p (t d) -> p t d", t=2), ALU.add).then_inc(added, 1)


def retention(nc, outer, norm_sems, x, ident, ident_ready, W_Q, W_K, W_V, tables, decay_in):
    with ExitStack() as ctx:
        def sb(name, shape, dt=F32):
            return ctx.enter_context(nc.sbuf_tensor(f"{name}_r", shape, dt))

        def sem(name):
            return outer.enter_context(nc.semaphore(f"{name}_r"))

        B = [ctx.enter_context(nc.psum_tensor(f"bank{i}_r", [P, HALF], F32)) for i in range(8)]
        xh, xl = sb("xh", [P, KD, T], F32R), sb("xl", [P, KD, T], F32R)
        xn = sb("xn", [P, NT, D])
        w_stage = [sb(f"w_stage{i}", [P, KD, D]) for i in range(3)]
        w_high = [sb(f"w_high{i}", [P, KD, D], F32R) for i in range(3)]
        w_low = [sb(f"w_low{i}", [P, KD, D], F32R) for i in range(3)]
        ones = sb("ones", [P, 1])
        cos_sin = sb("cos_sin", [P, 4, T])
        decay = sb("decay", [P, T])
        prod = [sb(f"product{i}", [P, 4, HALF]) for i in range(2)]
        turned = [sb(f"turned{i}", [P, KD, HALF]) for i in range(2)]
        qk_high = [sb(f"{n}_high", [P, KD, T], F32R) for n in "qk"]
        qk_low = [sb(f"{n}_low", [P, KD, T], F32R) for n in "qk"]
        v = sb("v", [P, NT, D])
        att = [sb(f"att{i}", [P, T - i * P]) for i in range(NT)]

        w_loaded = [sem(f"{n}_loaded") for n in ("w_q", "w_k", "w_v")]
        tables_loaded, decay_loaded, ones_set = sem("tables_loaded"), sem("decay_loaded"), sem("ones_set")
        high_done, w_split = sem("w_high_done"), sem("w_split")
        proj_ready, prod_done, turn_done = sem("proj_ready"), sem("products_done"), sem("turn_done")
        qk_high_done, qk_split = sem("qk_high_done"), sem("qk_split")
        v_ready, v_copied = sem("v_ready"), sem("v_copied")
        s_ready, att_done, out_ready, added = sem("scores_ready"), sem("att_done"), sem("out_ready"), sem("added")
        norm = Norm(nc, ctx, norm_sems, 2, x, xn, xh, xl, ident, B[0:4])

        units = [(0, 0), (1, 0), (0, 1), (1, 1)]
        unit_banks = [(B[4], B[5]), (B[6], B[7]), (B[0], B[1]), (B[2], B[3])]
        chunks = [(i, c, min(HALF, T - c)) for i in range(NT) for c in range(i * P, T, HALF)]
        chunks_to = [sum(1 for c in chunks if c[0] <= i) for i in range(NT)]

        with nc.Block() as block:
            @block.sync
            def _(sp):
                for i, w in enumerate((W_Q, W_K, W_V)):
                    sp.dma_start(w_stage[i][:, :, :], w.rearrange("(k p) n -> p k n", p=P)).then_inc(w_loaded[i], 16)
                for i, t in enumerate(tables):
                    sp.dma_start(cos_sin[:, i, :], t).then_inc(tables_loaded, 16)
                sp.dma_start(decay[:, :], decay_in).then_inc(decay_loaded, 16)

            @block.gpsimd
            def _(pool):
                pool.memset(ones[:, :], 1.0).then_inc(ones_set, 1)
                pool.wait_ge(ones_set, 1)
                for i in range(3):
                    pool.wait_ge(w_loaded[i], 16)
                    pool.tensor_tensor(w_high[i][:, :, :], w_stage[i][:, :, :],
                                       ones[:, 0:1].unsqueeze(2).to_broadcast([P, KD, D]), ALU.mult)\
                        .then_inc(high_done, 1)
                    pool.wait_ge(high_done, i + 1)
                    pool.tensor_tensor(w_low[i][:, :, :], w_stage[i][:, :, :], fr(w_high[i][:, :, :]),
                                       ALU.subtract).then_inc(w_split, 1)
                    if i == 0:
                        norm.pool_part(pool)
                for u in range(4):
                    if u >= 2:
                        pool.wait_ge(qk_split, u - 1)
                    for part, op in ((0, ALU.subtract), (1, ALU.add)):
                        pool.wait_ge(prod_done, 2 * u + part + 1)
                        pool.tensor_tensor(turned[u % 2][:, part, :], prod[u % 2][:, 2 * part, :],
                                           prod[u % 2][:, 2 * part + 1, :], op).then_inc(turn_done, 1)

            @block.tensor
            def _(pe):
                norm.tensor_part(pe, ident_ready, 2)
                pe.wait_ge(norm.xl_done, norm.all_split)
                for u, (qk, half) in enumerate(units):
                    pe.wait_ge(w_split, qk + 1)
                    cols = slice(half * HALF, (half + 1) * HALF)
                    for c in range(KD):
                        for k in range(KD):
                            last = split3(pe, unit_banks[u][c][:, :],
                                          (w_high[qk][:, k, c * P:(c + 1) * P], w_low[qk][:, k, c * P:(c + 1) * P]),
                                          (xh[:, k, cols], xl[:, k, cols]), k == 0, k == KD - 1)
                        last.then_inc(proj_ready, 1)
                pe.wait_ge(w_split, 3)
                for j in range(NT):
                    if j % 4 == 0:
                        pe.wait_ge(prod_done, j // 2 + 2)
                    for k in range(KD):
                        last = split3(pe, B[4 + j // 2][:, j % 2 * D:(j % 2 + 1) * D],
                                      (xh[:, k, j * P:(j + 1) * P], xl[:, k, j * P:(j + 1) * P]),
                                      (w_high[2][:, k, :], w_low[2][:, k, :]), k == 0, k == KD - 1)
                    last.then_inc(v_ready, 1)

                def scores(i):
                    for n, (tile, c, w) in enumerate(chunks):
                        if tile != i:
                            continue
                        pe.wait_ge(qk_split, 4)
                        if n >= 4:
                            pe.wait_ge(att_done, n - 3)
                        for k in range(KD):
                            last = split3(pe, B[n % 4][:, 0:w],
                                          (qk_high[1][:, k, i * P:(i + 1) * P], qk_low[1][:, k, i * P:(i + 1) * P]),
                                          (qk_high[0][:, k, c:c + w], qk_low[0][:, k, c:c + w]), k == 0, k == KD - 1)
                        last.then_inc(s_ready, 1)

                def output(i):
                    pe.wait_ge(v_copied, 4)
                    pe.wait_ge(att_done, chunks_to[i])
                    for j in range(i, NT):
                        last = pe.matmul(B[4 + j // 2][:, j % 2 * D:(j % 2 + 1) * D], att[i][:, (j - i) * P:(j - i + 1) * P],
                                         v[:, i, :], start=(i == 0 and j % 2 == 0), stop=True, skip_group_check=True)
                        if j == i and i % 2:
                            last.then_inc(out_ready, 1)

                scores(0)
                for i in range(NT):
                    if i < NT - 1:
                        scores(i + 1)
                    output(i)

            @block.scalar
            def _(act):
                norm.scalar_part(act)

                def high(u):
                    qk, half = units[u]
                    act.wait_ge(turn_done, 2 * u + 2)
                    act.activation(qk_high[qk][:, :, half * HALF:(half + 1) * HALF], turned[u % 2][:, :, :], ACT.Copy)\
                       .then_inc(qk_high_done, 1)

                def copy_v(b):
                    act.wait_ge(v_ready, 2 * b + 2)
                    act.activation(v[:, 2 * b:2 * b + 2, :], B[4 + b][:, :].rearrange("p (t d) -> p t d", t=2), ACT.Copy)\
                       .then_inc(v_copied, 1)

                high(0)
                high(1)
                copy_v(0)
                copy_v(1)
                high(2)
                copy_v(2)
                copy_v(3)
                high(3)

            @block.vector
            def _(dve):
                norm.vector_part(dve)
                dve.wait_ge(tables_loaded, 64)
                dve.wait_ge(decay_loaded, 16)

                def products(u):
                    qk, half = units[u]
                    cols = slice(half * HALF, (half + 1) * HALF)
                    even, odd = unit_banks[u]
                    cos, sin = cos_sin[:, 2 * qk, cols], cos_sin[:, 2 * qk + 1, cols]
                    dve.wait_ge(proj_ready, 2 * u + 2)
                    if u >= 2:
                        dve.wait_ge(turn_done, 2 * u - 2)
                    for part, (a, b) in enumerate(((even, odd), (odd, even))):
                        dve.tensor_tensor(prod[u % 2][:, 2 * part, :], a[:, :], cos, ALU.mult)
                        dve.tensor_tensor(prod[u % 2][:, 2 * part + 1, :], b[:, :], sin, ALU.mult).then_inc(prod_done, 1)

                def low(u):
                    qk, half = units[u]
                    cols = slice(half * HALF, (half + 1) * HALF)
                    dve.wait_ge(qk_high_done, u + 1)
                    dve.tensor_tensor(qk_low[qk][:, :, cols], turned[u % 2][:, :, :], fr(qk_high[qk][:, :, cols]),
                                      ALU.subtract).then_inc(qk_split, 1)

                for u in range(4):
                    products(u)
                    if u:
                        low(u - 1)
                low(3)
                for n, (i, c, w) in enumerate(chunks):
                    dve.wait_ge(s_ready, n + 1)
                    at = c - i * P
                    dve.tensor_tensor(att[i][:, at:at + w], B[n % 4][:, 0:w], decay[:, at:at + w], ALU.mult)\
                       .then_inc(att_done, 1)
                for b in range(4):
                    dve.wait_ge(out_ready, b + 1)
                    dve.tensor_tensor(x[:, 2 * b:2 * b + 2, :], x[:, 2 * b:2 * b + 2, :],
                                      B[4 + b][:, :].rearrange("p (t d) -> p t d", t=2), ALU.add).then_inc(added, 1)


def build(nc, ins, out):
    with ExitStack() as outer:
        x = outer.enter_context(nc.sbuf_tensor("x", [P, NT, D], F32))
        ident = outer.enter_context(nc.sbuf_tensor("ident", [P, P], F32))
        ident_ready = outer.enter_context(nc.semaphore("ident_ready"))
        norm_sems = NormSemaphores(lambda name: outer.enter_context(nc.semaphore(name)))
        with nc.Block() as block:
            @block.gpsimd
            def _(pool):
                pool.memset(ident[:, :], 0.0).then_inc(ident_ready, 1)
                pool.wait_ge(ident_ready, 1)
                pool.affine_select(out=ident[:, :], in_=ident[:, :], compare_op=ALU.not_equal, fill=1.0, base=0,
                                   pattern=[[-1, P]], channel_multiplier=1).then_inc(ident_ready, 1)
        scratch = nc.dram_tensor("attention_out", (T, D), F32).ap()
        delta_attention(nc, outer, norm_sems, x, ident, ident_ready, scratch, ins["L0_attn_x"], ins["L0_attn_Wq"], ins["L0_attn_Wk"],
                        ins["L0_attn_Wv"], ins["L0_attn_Wo"], ins["betas_by_head"], ins["causal_mask"])
        experts_layer(nc, outer, norm_sems, x, ident, ident_ready, "e0", E0, {
            "router": ins["router0"], "gate": ins["gate0"], "up": ins["up0"], "down": ins["down0"],
            "shared_gate_up": ins["L0_ffn_shared_gate_up"], "shared_down": ins["L0_ffn_shared_down"],
            "rank": ins["rank0"], "spread": ins["spread0"]}, True)
        retention(nc, outer, norm_sems, x, ident, ident_ready, ins["W_Q"], ins["W_K"], ins["L1_attn_W_V"],
                  [ins[n] for n in ("cos_q", "sin_q", "cos_k", "sin_k")], ins["decay"])
        experts_layer(nc, outer, norm_sems, x, ident, ident_ready, "e1", E1, {
            "router": ins["router1"], "gate": ins["gate1"], "up": ins["up1"], "down": ins["down1"],
            "rank": ins["rank1"], "spread": ins["spread1"]}, False)
        stored = outer.enter_context(nc.semaphore("stored"))
        with nc.Block() as block:
            @block.sync
            def _(sp):
                sp.dma_start(out.rearrange("a (t p) n -> p (a t) n", p=P), x[:, :, :]).then_inc(stored, 16)
                sp.wait_ge(stored, 16)


def shape_constants(np):
    s = np.arange(P)[:, None] % SEG
    tables = {"causal_mask": np.where(np.arange(SEG)[None, :] <= s, 0.0, -LARGE)}
    pair, pos = np.arange(P, dtype=np.float32), np.arange(T, dtype=np.float32)
    scale_vec = (2 * pair + np.float32(0.4 * D)) / np.float32(1.4 * D)
    scale = scale_vec[:, None] ** (pos / np.float32(SCALE_BASE))[None, :]
    angle = pos[None, :] * (np.float32(1) / np.float32(10000) ** (pair / np.float32(P)))[:, None]
    for name, sc in (("q", scale), ("k", np.float32(1) / scale)):
        tables[f"cos_{name}"], tables[f"sin_{name}"] = np.cos(angle) * sc, np.sin(angle) * sc
    distance = np.arange(T)[None, :] - np.arange(P)[:, None]
    tables["decay"] = np.where(distance >= 0, np.float32(GAMMA) ** np.maximum(distance, 0).astype(np.float32), 0.0)
    for n, e in ((0, E0), (1, E1)):
        tables[f"rank{n}"] = np.tile(e - np.arange(e), (P, 1))
        spread = np.zeros((P, e * INTER))
        for part in range(3):
            spread[32 * part + np.arange(e * INTER) // INTER, np.arange(e * INTER)] = 1.0
        tables[f"spread{n}"] = spread
    return {n: a.astype(np.float32) for n, a in tables.items()}


def layouts(np, inputs):
    a = {n: np.asarray(inputs[n]) for n in (
        "L0_attn_x", "L0_attn_Wq", "L0_attn_Wk", "L0_attn_Wv", "L0_attn_Wo",
        "L0_ffn_shared_gate_up", "L0_ffn_shared_down", "L1_attn_W_V")}
    for n in ("W_Q", "W_K"):
        a[n] = np.asarray(inputs[f"L1_attn_{n}"]).reshape(D, D // 2, 2).transpose(0, 2, 1).reshape(D, D)
    a["betas_by_head"] = np.asarray(inputs["L0_attn_betas"]).reshape(H, DK).T
    gate_up = np.asarray(inputs["L0_ffn_w_gate_up"]).transpose(1, 0, 2)
    a["gate0"] = gate_up[:, :, :INTER].reshape(D, E0 * INTER)
    a["up0"] = gate_up[:, :, INTER:].reshape(D, E0 * INTER)
    a["down0"] = np.asarray(inputs["L0_ffn_w_down"]).reshape(E0 * INTER, D)
    a["router0"] = np.asarray(inputs["L0_ffn_gate_w"]).T
    a["gate1"] = np.asarray(inputs["L1_ffn_gate_w"]).transpose(2, 0, 1).reshape(D, E1 * INTER)
    a["up1"] = np.asarray(inputs["L1_ffn_up_w"]).transpose(2, 0, 1).reshape(D, E1 * INTER)
    a["down1"] = np.asarray(inputs["L1_ffn_down_w"]).transpose(0, 2, 1).reshape(E1 * INTER, D)
    a["router1"] = np.asarray(inputs["L1_ffn_router_w"]).T
    return a


def kernel(**inputs):
    import numpy as np
    import concourse.bacc as bacc
    from concourse.bass_utils import run_bass_kernel_spmd as run

    nc = bacc.Bacc("TRN2", target_bir_lowering=False, num_devices=1)
    arrays = {**layouts(np, inputs), **shape_constants(np)}
    arrays = {n: np.ascontiguousarray(a) for n, a in arrays.items()}
    ins = {n: nc.dram_tensor(n, a.shape, F32, kind="ExternalInput").ap() for n, a in arrays.items()}
    out = nc.dram_tensor("out", (1, T, D), F32, kind="ExternalOutput").ap()
    build(nc, ins, out)
    r = run(nc, [arrays], core_ids=[0])
    return r.results[0]["out"]
```

```python
from contextlib import ExitStack

import concourse.bass as bass
from concourse import mybir

F32 = mybir.dt.float32
F32R = mybir.dt.float32r
BF16 = mybir.dt.bfloat16
ALU = mybir.AluOpType
ACT = mybir.ActivationFunctionType
AX = mybir.AxisListType

P = 128
T = 1024
D = 256
NT = T // P
KD = D // P
HALF = T // 2
TPH = NT // 2
EPS = 1e-5

H, DK, SEG = 16, 128, 64
NSEG = T // SEG
HQ = 4
NQ = H // HQ
GROUP = 2
MC = DK + 1
SCORE_SCALE = float(1.0 / DK ** 0.5)

GAMMA, SCALE_BASE = 0.96875, 64

INTER = 176
E0, E1 = 16, 8
SHARED = 2 * INTER
LARGE = 1e30


def fr(ap):
    return ap.bitcast(F32)


class Norm:

    def __init__(self, nc, ctx, x, ident):
        def sb(name, shape, dt=F32):
            return ctx.enter_context(nc.sbuf_tensor(name, shape, dt))

        def sem(name):
            return ctx.enter_context(nc.semaphore(name))

        self.x, self.ident = x, ident
        self.stats, self.mean_var = sb("stats", [P, NT, 6]), sb("mean_var", [P, NT, 2])
        self.var_eps, self.power, self.rstd = sb("var_eps", [P, NT]), sb("power", [P, NT]), sb("rstd", [P, NT])
        xn = sb("xn", [P, NT, D])
        self.xn = [xn] * 4
        self.xh, self.xl = sb("xh", [P, KD, T], F32R), sb("xl", [P, KD, T], F32R)
        self.stats_done, self.mean_var_done = sem("norm_stats_done"), sem("norm_mean_var_done")
        self.var_eps_done, self.power_set, self.rstd_done = sem("var_eps_done"), sem("power_set"), sem("rstd_done")
        self.xn_done, self.xT_done, self.xh_done, self.xl_done = (
            sem("xn_done"), sem("xT_done"), sem("xh_done"), sem("xl_done"))

    def set_power(self, pool):
        pool.memset(self.power[:, :], -0.5).then_inc(self.power_set, 1)
        pool.wait_ge(self.power_set, 1)

    def invert(self, pool, n, half):
        tiles = slice(half * TPH, (half + 1) * TPH)
        pool.wait_ge(self.var_eps_done, 2 * n + half + 1)
        pool.tensor_tensor(self.rstd[:, tiles], self.var_eps[:, tiles], self.power[:, tiles], ALU.pow)\
            .then_inc(self.rstd_done, 1)

    def statistics(self, dve, n, half, loaded=None):
        tiles = range(half * TPH, (half + 1) * TPH)
        for j in tiles:
            if loaded is not None and j % 2 == 0:
                dve.wait_ge(loaded[j // 2], 16)
            dve.bn_stats(out=self.stats[:, j, :], in_=self.x[:, j, :]).then_inc(self.stats_done, 1)
        for j in tiles:
            dve.wait_ge(self.stats_done, NT * n + j + 1)
            dve.bn_aggr(out=self.mean_var[:, j, :], in_=self.stats[:, j, :]).then_inc(self.mean_var_done, 1)
        dve.wait_ge(self.mean_var_done, NT * n + (half + 1) * TPH)
        at = slice(half * TPH, (half + 1) * TPH)
        dve.tensor_scalar(self.var_eps[:, at], self.mean_var[:, at, 1], EPS, None, ALU.add)\
           .then_inc(self.var_eps_done, 1)

    def normalise(self, dve, n, half):
        dve.wait_ge(self.rstd_done, 2 * n + half + 1)
        for j in range(half * TPH, (half + 1) * TPH):
            dve.tensor_scalar(self.xn[n][:, j, :], self.x[:, j, :], self.mean_var[:, j, 0:1],
                              self.rstd[:, j:j + 1], ALU.subtract, ALU.mult).then_inc(self.xn_done, 1)

    def turn(self, pe, n, half, banks):
        for k in range(KD):
            b = KD * half + k
            pe.wait_ge(self.xn_done, NT * n + (half + 1) * TPH)
            for t in range(TPH):
                last = pe.transpose(banks[b][:, t * P:(t + 1) * P],
                                    self.xn[n][:, half * TPH + t, k * P:(k + 1) * P], self.ident[:, :])
            last.then_inc(self.xT_done, 1)

    def high(self, act, n, half, banks):
        for k in range(KD):
            b = KD * half + k
            act.wait_ge(self.xT_done, 4 * n + b + 1)
            act.activation(self.xh[:, k, half * HALF:(half + 1) * HALF], banks[b][:, :], ACT.Copy)\
               .then_inc(self.xh_done, 1)

    def low(self, dve, n, half, banks):
        for k in range(KD):
            b = KD * half + k
            dve.wait_ge(self.xh_done, 4 * n + b + 1)
            dve.tensor_tensor(self.xl[:, k, half * HALF:(half + 1) * HALF], banks[b][:, :],
                              fr(self.xh[:, k, half * HALF:(half + 1) * HALF]), ALU.subtract)\
               .then_inc(self.xl_done, 1)

    def wait_split(self, pe, n, half):
        pe.wait_ge(self.xl_done, 4 * n + KD * half + KD)


class Carried:

    def __init__(self, nc, ctx):
        def sem(name):
            return ctx.enter_context(nc.semaphore(name))

        self.space = ctx.enter_context(nc.sbuf_tensor("carried", [P, HQ, T], F32))
        flat = self.space[:, :, :].rearrange("p h t -> p (h t)")
        self.tiles = [flat[:, 3 * D * i:3 * D * (i + 1)].rearrange("p (i d) -> p i d", d=D) for i in range(2)]
        self.retention_w = [flat[:, (6 + 2 * i) * D:(8 + 2 * i) * D].rearrange("p (k d) -> p k d", d=D) for i in range(3)]
        self.y_in = [flat[:, i * D:(i + 4) * D].rearrange("p (t d) -> p t d", d=D) for i in (12, 6)]
        self.tile_loaded = [sem(f"first_tile{i}_loaded") for i in range(2)]
        self.retention_w_loaded = [sem(f"{n}_loaded") for n in ("w_q", "w_k", "w_v")]


class ExpertTiles:

    def __init__(self, experts, weights, shared):
        n_tiles = experts * INTER // P
        self.weights, self.shared = weights, shared
        self.peeled = 2 + n_tiles % 2
        self.before = [("shared", j, min(P, SHARED - j * P)) for j in range(-(-SHARED // P))] if shared else []
        self.before += [("expert", j, P) for j in range(self.peeled)]
        self.turns = (n_tiles - self.peeled) // 2
        nb = len(self.before)
        self.par_of = [(q - nb) % 2 for q in range(nb)]

    def load(self, sp, stage, tile, loaded):
        kind, j, rows = tile
        w = self.weights
        if kind == "shared":
            gate = w["shared_gate_up"][:, j * P:j * P + rows]
            up = w["shared_gate_up"][:, SHARED + j * P:SHARED + j * P + rows]
            down = w["shared_down"][j * P:j * P + rows, :]
        else:
            gate, up = w["gate"][:, bass.ts(j, P)], w["up"][:, bass.ts(j, P)]
            down = w["down"][bass.ts(j, P), :]
        for i, src in ((0, gate), (1, up)):
            dst = stage[:, i, :].rearrange("p (k n) -> p k n", k=KD)[:, :, 0:rows]
            sp.dma_start(dst, src.rearrange("(k p) n -> p k n", p=P)).then_inc(loaded, 16)
        sp.dma_start(stage[0:rows, 2, :], down).then_inc(loaded, 16)

    def load_first(self, sp, carried):
        for q in range(2):
            self.load(sp, carried.tiles[self.par_of[q]], self.before[q], carried.tile_loaded[q])


def split3(pe, out, stationary, moving, first, last, **kw):
    (sh, sl), (mh, ml) = stationary, moving
    pe.matmul(out, sh, mh, start=first, stop=False, **kw)
    pe.matmul(out, sh, ml, start=False, stop=False, **kw)
    return pe.matmul(out, sl, mh, start=False, stop=last, **kw)


def delta_attention(nc, outer, norm, carried, x, ident, ident_ready, scratch, x_in, Wq, Wk, Wv, Wo, betas, mask_in,
                    place_in, next_tiles):
    with ExitStack() as ctx:
        def sb(name, shape, dt=F32):
            return ctx.enter_context(nc.sbuf_tensor(name, shape, dt))

        def sem(name):
            return outer.enter_context(nc.semaphore(name))

        def bank(name):
            return ctx.enter_context(nc.psum_tensor(name, [P, HALF], F32))

        A = [bank(f"ahead{i}") for i in range(2)]
        L = [bank(f"local{i}") for i in range(2)]
        KQ = [bank(f"readings{g}") for g in range(2)]
        MM = [bank(f"memory{g}") for g in range(2)]

        xh, xl = norm.xh, norm.xl
        w_high = [sb(f"w_high{i}", [P, KD, HQ * DK], F32R) for i in range(2)]
        w_low = [sb(f"w_low{i}", [P, KD, HQ * DK], F32R) for i in range(2)]
        w_staged = norm.xn[1][:, 0:TPH, :].rearrange("p t d -> p (t d)").rearrange("p (k n) -> p k n", k=KD)
        probs = norm.xn[1][:, TPH:NT, :].rearrange("p t d -> p (t d)").rearrange("p (t c) -> p t c", c=P)
        wo = sb("wo", [P, H, D])
        ones = sb("ones", [P, 1])
        mask = sb("mask", [P, SEG])
        beta_t, beta_e = sb("beta_t", [P, H]), sb("beta_e", [P, H])
        beta, one_less_beta = sb("beta", [P, H]), sb("one_less_beta", [P, H])
        beta_q, one_less_q = sb("beta_q", [P, HQ]), sb("one_less_q", [P, HQ])
        start = sb("memory_start", [P, GROUP * MC])
        qT, kT = carried.space, sb("kT", [P, HQ, T])
        sqk = sb("sigma", [P, HQ, NT, 4, SEG])
        sk = [sb(f"sigma_k{i}", [P, HALF]) for i in range(2)]
        skt = sb("sigma_k_tokens", [P, HQ, NT, DK])
        v = sb("v", [P, NT, HQ * DK])
        read = sb("memory_reading", [P, 2, HQ, TPH, DK])
        att = sb("attT", [P, 2, HQ, HALF])
        mz = [sb(f"memory_copy{g}", [P, GROUP, MC]) for g in range(2)]
        nr = [sb(f"denominators{g}", [P, GROUP]) for g in range(2)]
        dl = [[sb(f"minus_delta{g}{par}", [P, GROUP, MC]) for par in range(2)] for g in range(2)]
        sm = sb("scores", [P, NT, SEG])
        mx, ssum, rs = sb("score_max", [P, NT]), sb("exp_sum", [P, NT]), sb("exp_sum_inverse", [P, NT])
        y_out, y_in = sb("out_rows", [P, D]), carried.y_in
        place = kT[:, 0, 0:HALF].rearrange("p (t c) -> p t c", c=P)
        at_start = [v[:, TPH + 2 * i:TPH + 2 * i + 2, :] for i in range(2)]
        x_space = x[:, :, :].rearrange("p t d -> p (t d)")
        e = [x_space[:, i * HALF:(i + 1) * HALF] for i in range(2)]
        pTs = [x_space[:, (2 + i) * HALF:(3 + i) * HALF] for i in range(2)]

        x_loaded, mask_loaded, beta_loaded = [sem(f"x_loaded{i}") for i in range(NT // 2)], sem("mask_loaded"), sem("beta_loaded")
        w_loaded, wo_loaded = sem("w_loaded"), sem("wo_loaded")
        start_loaded = [sem(f"start_loaded{i}") for i in range(2)]
        consts_set, beta_exp, beta_step, beta_q_set = (
            sem("consts_set"), sem("beta_exp"), sem("beta_step"), sem("beta_q_set"))
        high_done, low_done = sem("w_high_done"), sem("w_split_done")
        proj_ready, qk_copied, exp_capped, sigma_ready = (
            sem("proj_ready"), sem("qk_copied"), sem("exp_capped"), sem("sigma_ready"))
        sk_ready = sem("sigma_k_in_order")
        v_copied, skt_ready, skt_copied = sem("v_copied"), sem("sigma_k_turned"), sem("sigma_k_copied")
        upd_ready = [sem(f"memory_updated{g}") for g in range(2)]
        mem_copied = [sem(f"memory_copied{g}") for g in range(2)]
        kq_ready = [sem(f"readings_ready{g}") for g in range(2)]
        nr_ready = [sem(f"denominators_ready{g}") for g in range(2)]
        dl_ready = [sem(f"delta_ready{g}") for g in range(2)]
        read_ready = [sem(f"reading_scaled{g}") for g in range(2)]
        sc_ready, masked, max_ready, shifted, exp_ready = (
            sem("scores_ready"), sem("scores_masked"), sem("max_ready"), sem("scores_shifted"), sem("exp_ready"))
        sum_ready, inv_ready, p_ready = sem("exp_sum_ready"), sem("exp_sum_inverted"), sem("probs_ready")
        pT_ready, pTs_ready, bt_ready, bt_copied = (
            sem("probsT_ready"), sem("probsT_copied"), sem("local_ready"), sem("local_copied"))
        at_ready, att_ready, wo_ready, y_copied = (
            sem("readingT_ready"), sem("attT_ready"), sem("out_ready"), sem("out_copied"))

        y_stored, x_added, place_loaded, placed = (
            sem("out_stored"), sem("x_added"), sem("place_loaded"), sem("out_placed"))
        y_loaded, x_reloaded = ([sem(f"{n}{i}") for i in range(2)] for n in ("out_loaded", "x_reloaded"))

        norm.xn[0] = att[:, 0, :, :].rearrange("p h t -> p (h t)").rearrange("p (t d) -> p t d", d=D)
        norm_banks = [*A, *L]

        STAGES, STEPS = 2 * NQ, NSEG // 2
        early = SEG - SEG // NQ
        AHEAD_AT = {u: [("project", u)] for u in range(7)}
        AHEAD_AT |= {7: [("project", 7), ("turn", 0)], 8: [("turn", 1), ("project", 8)],
                     9: [("turn", 2), ("project", 9)], 10: [("turn", 3), ("project", 10)], 11: [("project", 11)]}
        AT_START = [("project", u) for u in range(9)] + [
            ("turn", 0), ("project", 9), ("turn", 1), ("project", 10), ("turn", 2), ("project", 11), ("turn", 3)]
        PROJECT_BANK = (0, 1, 0, 1, 0, 1, 0, 1, 0, 0, 0, 0)
        SIGMA_K_BANK = (0, 1, 1, 1)
        OUT_AT = {12: range(0, 3), 13: range(3, 8), 14: range(8, 10), 15: range(10, 16)}
        LAST_OUT_AT = {7: range(0, 2), 9: range(2, 6), 11: range(6, 10), 13: range(10, 13), 15: range(13, 16)}
        READINGS_AT = {1: 0, 3: 1, 4: 2, 5: 3}
        READINGS_BANK = (1, 1, 0, 1)

        def all_turns(engine, turn):
            turn(0, True, False)
            with engine.Fori(0, NQ - 2) as i:
                turn(i + 1, False, False)
            turn(NQ - 1, False, True)

        def w_cols(w, turn):
            return w[:, bass.ts(turn, HQ * DK)].rearrange("(k p) n -> p k n", p=P)

        with nc.Block() as block:
            @block.sync
            def _(sp):
                x_tiles = x_in.rearrange("a (t p) n -> p (a t) n", p=P)
                for t in range(0, NT, 2):
                    sp.dma_start(x[:, t:t + 2, :], x_tiles[:, t:t + 2, :]).then_inc(x_loaded[t // 2], 16)
                sp.dma_start(w_staged[:, :, :], w_cols(Wq, 0)).then_inc(w_loaded, 16)
                sp.dma_start(mask[:, :], mask_in).then_inc(mask_loaded, 16)
                sp.dma_start(beta_t[:, :], betas).then_inc(beta_loaded, 16)

                def load_weights(w, turn, splits):
                    sp.wait_ge(low_done, splits)
                    sp.dma_start(w_staged[:, :, :], w_cols(w, turn)).then_inc(w_loaded, 16)

                def store_out(it, half, n):
                    tokens = scratch.rearrange("(b s q h m) d -> b s q h m d", b=2, s=STEPS, h=HQ, m=4)
                    sp.wait_ge(y_copied, n + 1)
                    for h in range(HQ):
                        sp.dma_start(tokens[half, :, bass.ds(it, 1), h, :, :],
                                     y_out[32 * h:32 * h + 32, :]).then_inc(y_stored, 16)

                for i, w in enumerate((Wk, Wv)):
                    sp.dma_start(at_start[i][:, :, :], w_cols(w, 0)).then_inc(start_loaded[i], 16)
                sp.dma_start(wo[:, :, :], Wo.rearrange("(i p) n -> p i n", p=P)).then_inc(wo_loaded, 16)
                load_weights(Wq, 0, 1)
                load_weights(Wk, 0, 4)

                def turn(it, first, last):
                    load_weights(Wv, it, 6 * it + 5)
                    if not first:
                        store_out(it - 1, 0, 2 * it - 2)
                    if not last:
                        load_weights(Wq, it + 1, 6 * it + 6)
                        load_weights(Wk, it + 1, 6 * it + 7)
                        load_weights(Wv, it + 1, 6 * it + 8)
                    if not first:
                        store_out(it - 1, 1, 2 * it - 1)
                    if not last:
                        load_weights(Wq, it + 1, 6 * it + 9)
                        load_weights(Wk, it + 1, 6 * it + 10)

                all_turns(sp, turn)
                sp.wait_ge(sigma_ready, 8 * STAGES)
                sp.dma_start(x[:, 0:TPH, :], x_tiles[:, 0:TPH, :]).then_inc(x_reloaded[0], 16)
                sp.wait_ge(sc_ready, 2 * STAGES)
                sp.dma_start(place[:, :, :], place_in).then_inc(place_loaded, 16)
                sp.wait_ge(y_stored, 64 * (STAGES - 2))
                of_segment = scratch.rearrange("(b t par r) d -> b par r t d", b=2, t=TPH, par=2)
                for par in range(2):
                    sp.dma_start(y_in[1][par * SEG:par * SEG + early, :, :], of_segment[1, par, 0:early, :, :])\
                      .then_inc(y_loaded[1], 16)
                next_tiles.load_first(sp, carried)
                sp.wait_ge(bt_ready, 4 * STAGES)
                sp.dma_start(x[:, TPH:NT, :], x_tiles[:, TPH:NT, :]).then_inc(x_reloaded[1], 16)
                store_out(NQ - 1, 0, STAGES - 2)
                sp.wait_ge(y_stored, 64 * (STAGES - 1))
                sp.dma_start(y_in[0], scratch.rearrange("(t p) d -> p t d", p=P)[:, 0:TPH, :]).then_inc(y_loaded[0], 16)

            @block.gpsimd
            def _(pool):
                pool.memset(ones[:, :], 1.0).then_inc(consts_set, 1)
                pool.memset(start[:, :], 0.0).then_inc(consts_set, 1)
                pool.wait_ge(consts_set, 2)
                pool.memset(start[:, :].rearrange("p (g c) -> p g c", g=GROUP)[:, :, DK:MC], -1.0 / DK)\
                    .then_inc(consts_set, 1)
                norm.set_power(pool)
                for half in range(2):
                    norm.invert(pool, 0, half)
                one = ones[:, 0:1].unsqueeze(2).to_broadcast([P, KD, HQ * DK])

                def split(i, n, start=None, first=False):
                    if start is not None:
                        pool.wait_ge(start_loaded[start], 16)
                        w_stage = at_start[start]
                    else:
                        pool.wait_ge(w_loaded, 16 if first else 16 * n - 32)
                        w_stage = w_staged
                    pool.tensor_tensor(w_high[i][:, :, :], w_stage[:, :, :], one, ALU.mult).then_inc(high_done, 1)
                    pool.wait_ge(high_done, n)
                    pool.tensor_tensor(w_low[i][:, :, :], w_stage[:, :, :], fr(w_high[i][:, :, :]),
                                       ALU.subtract).then_inc(low_done, 1)

                def set_constants():
                    for g in range(2):
                        for par in range(2):
                            rows = slice(par * SEG, (par + 1) * SEG)
                            pool.wait_ge(consts_set, 3 + 2 * (2 * g + par))
                            pool.memset(dl[g][par][:, :, :], 0.0).then_inc(consts_set, 1)
                            pool.wait_ge(consts_set, 4 + 2 * (2 * g + par))
                            pool.memset(dl[g][par][rows, :, DK:MC], -1.0).then_inc(consts_set, 1)
                    pool.wait_ge(consts_set, 11)
                    pool.memset(probs[:, :, :], 0.0).then_inc(consts_set, 1)

                def shift_scores(n):
                    pool.wait_ge(max_ready, n + 1)
                    pool.tensor_tensor(sm[:, :, :], sm[:, :, :], mx[:, :].unsqueeze(2).to_broadcast([P, NT, SEG]),
                                       ALU.subtract).then_inc(shifted, 1)

                def probabilities(n, before=True):
                    pool.wait_ge(inv_ready, n + 1)
                    if before:
                        pool.wait_ge(pT_ready, 2 * n)
                    for par in range(2):
                        rows = slice(par * SEG, (par + 1) * SEG)
                        pool.tensor_tensor(probs[rows, :, par * SEG:(par + 1) * SEG], sm[rows, :, :],
                                           rs[rows, :].unsqueeze(2).to_broadcast([SEG, NT, SEG]), ALU.mult)\
                            .then_inc(p_ready, 1)

                def stage(n, first=False, value_weights=True, key_weights=True):
                    if value_weights:
                        pool.wait_ge(low_done, 3 * n + 5)
                    else:
                        pool.wait_ge(p_ready, 4 * n)
                    shift_scores(2 * n)
                    if value_weights:
                        pool.wait_ge(shifted, 2 * n + 1)
                        pool.wait_ge(proj_ready, 12 * n + 16)
                        split(0, 3 * n + 6)
                        pool.wait_ge(low_done, 3 * n + 6)
                    probabilities(2 * n, not first)
                    pool.wait_ge(p_ready, 4 * n + 2)
                    shift_scores(2 * n + 1)
                    probabilities(2 * n + 1)
                    if key_weights:
                        pool.wait_ge(p_ready, 4 * n + 4)
                        pool.wait_ge(proj_ready, 12 * n + 24)
                        split(0, 3 * n + 7)
                        split(1, 3 * n + 8)

                split(0, 1, None, True)
                split(1, 2, 0)
                pool.wait_ge(proj_ready, 4)
                split(0, 3, 1)
                pool.wait_ge(low_done, 3)
                set_constants()
                pool.wait_ge(proj_ready, 12)
                split(0, 4)
                split(1, 5)
                stage(0, True)
                with pool.Fori(0, STAGES - 3) as i:
                    stage(i + 1)
                stage(STAGES - 2, False, True, False)
                stage(STAGES - 1, False, False, False)
                norm.invert(pool, 1, 0)

            @block.tensor
            def _(pe):
                pe.wait_ge(ident_ready, 2)
                for half in range(2):
                    norm.turn(pe, 0, half, norm_banks)

                def wait_copied(what, u):
                    if what == "turn":
                        pe.wait_ge(skt_copied, u + 1)
                    elif u < 8:
                        pe.wait_ge(qk_copied, u + 1)
                    else:
                        pe.wait_ge(v_copied, u - 7)

                def project(n, half, u, free=None, at_start=None):
                    b = A[PROJECT_BANK[u]] if at_start is None else at_start
                    if free is not None:
                        pe.wait_ge(*free)
                    if u % 4 == 0:
                        pe.wait_ge(low_done, 3 * n + u // 4 + 1)
                    if at_start is not None:
                        pass
                    elif 2 <= u < 8:
                        pe.wait_ge(qk_copied, 8 * n + u - 1)
                    elif u == 8:
                        pe.wait_ge(skt_copied, 4 * n + 1)
                    elif u > 8:
                        pe.wait_ge(v_copied, 4 * n + u - 8)
                    for k in range(KD):
                        if u < 8:
                            i, h = u // 4, u % 4
                            cols = slice(half * HALF, (half + 1) * HALF)
                            last = split3(pe, b[:, :],
                                          (w_high[i][:, k, h * DK:(h + 1) * DK], w_low[i][:, k, h * DK:(h + 1) * DK]),
                                          (xh[:, k, cols], xl[:, k, cols]), k == 0, k == KD - 1)
                        else:
                            j = half * TPH + u - 8
                            last = split3(pe, b[:, :], (xh[:, k, j * P:(j + 1) * P], xl[:, k, j * P:(j + 1) * P]),
                                          (w_high[0][:, k, :], w_low[0][:, k, :]), k == 0, k == KD - 1)
                    last.then_inc(proj_ready, 1)

                def turn_sigma_k(n, half, h, at_start=None):
                    b = A[SIGMA_K_BANK[h]] if at_start is None else at_start
                    if at_start is not None:
                        pass
                    elif h < 2:
                        pe.wait_ge(qk_copied, 8 * n + h + 7)
                    else:
                        pe.wait_ge(skt_copied, 4 * n + h)
                    pe.wait_ge(sigma_ready, 8 * n + h + 5)
                    for t in range(TPH):
                        last = pe.transpose(b[:, t * P:(t + 1) * P], sk[h % 2][:, t * P:(t + 1) * P], ident[:, :])
                    last.then_inc(skt_ready, 1)

                def seed(g):
                    pe.matmul(MM[g][:, 0:GROUP * MC], ident[:, :], start[:, :], start=True, stop=True,
                              skip_group_check=True).then_inc(upd_ready[g], 1)

                def read_memory(it, g, s):
                    pair, par = s // 2, s % 2
                    pe.wait_ge(mem_copied[g], 16 * it + s + 1)
                    for hh in range(GROUP):
                        last = pe.matmul(KQ[g][:, hh * MC:(hh + 1) * MC],
                                         sqk[:, GROUP * g + hh, pair, 2 * par:2 * par + 2, :], mz[g][:, hh, :],
                                         start=True, stop=True)
                    last.then_inc(kq_ready[g], 1)

                def update_memory(it, g, s):
                    pair, par = s // 2, s % 2
                    pe.wait_ge(dl_ready[g], 15 * it + s + 1)
                    for hh in range(GROUP):
                        last = pe.matmul(MM[g][:, hh * MC:(hh + 1) * MC], skt[:, GROUP * g + hh, pair, :],
                                         dl[g][par][:, hh, :], start=False, stop=True, skip_group_check=True)
                    last.then_inc(upd_ready[g], 1)

                def scores(n, half, pp):
                    for s in range(STEPS):
                        for hh in range(GROUP):
                            h, pair, par = GROUP * pp + hh, s // 2, s % 2
                            seg = slice((half * STEPS + s) * SEG, (half * STEPS + s + 1) * SEG)
                            at = (hh * TPH + pair) * SEG
                            last = pe.matmul(L[0][par * SEG:(par + 1) * SEG, at:at + SEG], qT[:, h, seg], kT[:, h, seg],
                                             start=True, stop=True)
                    last.then_inc(sc_ready, 1)

                def turn_probs(n, pp, hh):
                    for t in range(TPH):
                        last = pe.transpose(L[hh][:, t * P:(t + 1) * P], probs[:, hh * TPH + t, :], ident[:, :])
                    last.then_inc(pT_ready, 1)

                def local(n, half, pp, hh):
                    h = GROUP * pp + hh
                    pe.wait_ge(pTs_ready, 4 * n + h + 1)
                    for t in range(TPH):
                        last = pe.matmul(L[hh][:, t * P:(t + 1) * P], v[:, half * TPH + t, h * DK:(h + 1) * DK],
                                         pTs[hh][:, t * P:(t + 1) * P], start=True, stop=True)
                    last.then_inc(bt_ready, 1)

                def turn_reading(half, h):
                    for t in range(TPH):
                        last = pe.transpose(L[READINGS_BANK[h]][:, t * P:(t + 1) * P], read[:, half, h, t, :], ident[:, :])
                    last.then_inc(at_ready, 1)

                def project_out(half, part):
                    rows = att[:, half, :, :].rearrange("p h t -> p (h t)")
                    for i in part:
                        last = pe.matmul(A[1][:, 0:D], rows[:, i::H], wo[:, i, :], start=(i == 0), stop=(i == H - 1))
                        if i == H - 1:
                            last.then_inc(wo_ready, 1)

                def slot(it, half, m, first, last):
                    n = 2 * it + half
                    ahead, behind = not (last and half), not (first and not half)
                    if m == 0:
                        if behind:
                            pe.wait_ge(bt_copied, 4 * n - 1)
                        scores(n, half, 0)
                    if m == 6:
                        if behind:
                            pe.wait_ge(att_ready, 4 * n - 1)
                        pe.wait_ge(masked, 2 * n + 1)
                        scores(n, half, 1)
                    if behind and m in READINGS_AT:
                        h = READINGS_AT[m]
                        if h == 0:
                            pe.wait_ge(bt_copied, 4 * n)
                            for g in range(2):
                                pe.wait_ge(read_ready[g], STEPS * n)
                        elif h == 2:
                            pe.wait_ge(masked, 2 * n + 1)
                        else:
                            pe.wait_ge(att_ready, 4 * n - 4 + (h + 1) // 2)
                        turn_reading(1 - half, h)
                    if m == 8:
                        pe.wait_ge(p_ready, 4 * n + 2)
                        pe.wait_ge(masked, 2 * n + 2)
                        turn_probs(n, 0, 0)
                        if behind:
                            pe.wait_ge(att_ready, 4 * n)
                        turn_probs(n, 0, 1)
                    if m == 12:
                        pe.wait_ge(p_ready, 4 * n + 4)
                        for hh in range(2):
                            pe.wait_ge(bt_copied, 4 * n + hh + 1)
                            turn_probs(n, 1, hh)
                    if m in (10, 14):
                        for hh in range(2):
                            local(n, half, (m - 10) // 4, hh)
                    if ahead:
                        for what, u in AHEAD_AT.get(m, ()):
                            if what == "turn":
                                turn_sigma_k(n + 1, 1 - half, u)
                                continue
                            free = None
                            if u == 0:
                                free = v_copied, 4 * n + 4
                            elif u == 1:
                                free = (skt_copied, 4 * n + 4) if first else (y_copied, n - 1)
                            project(n + 1, 1 - half, u, free)
                    out_at = OUT_AT if ahead else LAST_OUT_AT
                    if behind and m in out_at:
                        if m == min(out_at):
                            pe.wait_ge(att_ready, 4 * n)
                            if ahead:
                                pe.wait_ge(skt_copied, 4 * n + 8)
                            else:
                                pe.wait_ge(y_copied, n - 1)
                        project_out(1 - half, out_at[m])

                def turn(it, first, last):
                    for half in range(2):
                        n = 2 * it + half
                        pe.wait_ge(sigma_ready, 8 * n + 8)
                        pe.wait_ge(skt_copied, 4 * n + 4)
                        for at in range(STEPS):
                            s = half * STEPS + at
                            read_memory(it, 0, s)
                            if s:
                                update_memory(it, 1, s - 1)
                            else:
                                seed(1)
                            slot(it, half, 2 * at, first, last)
                            read_memory(it, 1, s)
                            if s < NSEG - 1:
                                update_memory(it, 0, s)
                            elif not last:
                                seed(0)
                            slot(it, half, 2 * at + 1, first, last)

                norm.wait_split(pe, 0, 0)
                for i, (what, u) in enumerate(AT_START):
                    if i == 2:
                        norm.wait_split(pe, 0, 1)
                    if i >= 4:
                        wait_copied(*AT_START[i - 4])
                    if what == "turn":
                        turn_sigma_k(0, 0, u, norm_banks[i % 4])
                    else:
                        project(0, 0, u, None, norm_banks[i % 4])
                wait_copied("project", 11)
                pe.wait_ge(consts_set, 12)
                seed(0)
                pe.wait_ge(wo_loaded, 16)
                all_turns(pe, turn)
                n = STAGES
                for h in range(HQ):
                    if h == 0:
                        pe.wait_ge(bt_copied, 4 * n)
                        for g in range(2):
                            pe.wait_ge(read_ready[g], STEPS * n)
                    elif h != 2:
                        pe.wait_ge(att_ready, 4 * n - 4 + (h + 1) // 2)
                    turn_reading(1, h)
                pe.wait_ge(att_ready, 4 * n)
                pe.wait_ge(y_copied, n - 1)
                project_out(1, range(H))
                pe.wait_ge(place_loaded, 16)
                pe.wait_ge(y_copied, STAGES)
                for t in range(TPH):
                    last = pe.matmul(L[t // 2][:, t % 2 * D:(t % 2 + 1) * D], place[:, t, :], y_out[:, :],
                                     start=True, stop=True)
                    if t % 2:
                        last.then_inc(placed, 1)

            @block.scalar
            def _(act):
                for half in range(2):
                    norm.high(act, 0, half, norm_banks)
                act.wait_ge(beta_loaded, 16)
                act.activation(beta_e[:, :], beta_t[:, :], ACT.Exp, scale=-1.0).then_inc(beta_exp, 1)

                def copy_projection(n, half, u, at_start=None):
                    bank = A[PROJECT_BANK[u]] if at_start is None else at_start
                    act.wait_ge(proj_ready, 12 * n + u + 1)
                    if u < 8:
                        if u >= 2:
                            act.wait_ge(sigma_ready, 8 * n + u - 1)
                        act.activation(e[u % 2][:, :], bank[:, :], ACT.Exp)
                        act.activation((qT, kT)[u // 4][:, u % 4, half * HALF:(half + 1) * HALF], bank[:, :],
                                       ACT.Copy).then_inc(qk_copied, 1)
                    else:
                        act.activation(v[:, half * TPH + u - 8, :], bank[:, :], ACT.Copy).then_inc(v_copied, 1)

                def copy_sigma_k(n, half, h, at_start=None):
                    bank = A[SIGMA_K_BANK[h]] if at_start is None else at_start
                    act.wait_ge(skt_ready, 4 * n + h + 1)
                    act.activation(skt[:, h, half * TPH:(half + 1) * TPH, :],
                                   bank[:, :].rearrange("p (t c) -> p t c", t=TPH), ACT.Copy)\
                       .then_inc(skt_copied, 1)

                def copy_memory(it, g, n):
                    act.wait_ge(upd_ready[g], 16 * it + n + 1)
                    act.activation(mz[g][:, :, :], MM[g][:, 0:GROUP * MC].rearrange("p (h c) -> p h c", h=GROUP),
                                   ACT.Copy).then_inc(mem_copied[g], 1)

                def scale_reading(it, g, s):
                    half, pair, par = s // STEPS, s % STEPS // 2, s % 2
                    rows = slice(SEG, P) if par == 0 else slice(0, SEG)
                    act.wait_ge(nr_ready[g], 16 * it + s + 1)
                    for hh in range(GROUP):
                        last = act.activation(read[rows, half, GROUP * g + hh, pair, :],
                                              KQ[g][rows, hh * MC:hh * MC + DK], ACT.Copy, scale=nr[g][rows, hh:hh + 1])
                    last.then_inc(read_ready[g], 1)

                def exp_scores(n, pp):
                    act.wait_ge(shifted, 2 * n + pp + 1)
                    act.activation(sm[:, :, :], sm[:, :, :], ACT.Exp).then_inc(exp_ready, 1)

                def copy_probs(n, pp):
                    for hh in range(2):
                        act.wait_ge(pT_ready, 4 * n + 2 * pp + hh + 1)
                        act.activation(pTs[hh][:, :], L[hh][:, :], ACT.Copy).then_inc(pTs_ready, 1)

                def scale_local(n, half, pp):
                    for hh in range(2):
                        h = GROUP * pp + hh
                        act.wait_ge(bt_ready, 4 * n + h + 1)
                        act.activation(att[:, half, h, :], L[hh][:, :], ACT.Copy, scale=one_less_q[:, h:h + 1])\
                           .then_inc(bt_copied, 1)

                def copy_out(n, first=False):
                    if not first:
                        act.wait_ge(y_stored, 64 * n)
                    act.wait_ge(wo_ready, n + 1)
                    act.activation(y_out[:, :], A[1][:, 0:D], ACT.Copy).then_inc(y_copied, 1)

                def copy_ahead(it, half, m, last):
                    n = 2 * it + half
                    if not (last and half):
                        for what, u in AHEAD_AT.get(m - 1, ()):
                            (copy_sigma_k if what == "turn" else copy_projection)(n + 1, 1 - half, u)

                def slot(it, half, m, first, last):
                    n = 2 * it + half
                    if m == 0 and not first:
                        copy_out(n - 2, None)
                    if m in (4, 9):
                        exp_scores(n, m // 8)
                    if m in (9, 13):
                        copy_probs(n, (m - 9) // 4)
                    if m in (11, 15):
                        if m == 11 and not half:
                            act.wait_ge(beta_q_set, it + 1)
                        scale_local(n, half, (m - 11) // 4)

                def turn(it, first, last):
                    for half in range(2):
                        for at in range(STEPS):
                            s = half * STEPS + at
                            copy_ahead(it, half, 2 * at, last)
                            copy_memory(it, 1, s)
                            scale_reading(it, 0, s)
                            slot(it, half, 2 * at, first, last)
                            copy_ahead(it, half, 2 * at + 1, last)
                            if s < NSEG - 1:
                                copy_memory(it, 0, s + 1)
                            elif not last:
                                copy_memory(it, 0, NSEG)
                            scale_reading(it, 1, s)
                            slot(it, half, 2 * at + 1, first, last)

                for i, (what, u) in enumerate(AT_START):
                    (copy_sigma_k if what == "turn" else copy_projection)(0, 0, u, norm_banks[i % 4])
                copy_memory(0, 0, 0)
                all_turns(act, turn)
                copy_out(STAGES - 2)
                copy_out(STAGES - 1)

            @block.vector
            def _(dve):
                for half in range(2):
                    norm.statistics(dve, 0, half, x_loaded)
                for half in range(2):
                    norm.normalise(dve, 0, half)
                for half in range(2):
                    norm.low(dve, 0, half, norm_banks)
                dve.wait_ge(beta_exp, 1)
                dve.tensor_scalar(beta_e[:, :], beta_e[:, :], 1.0, None, ALU.add).then_inc(beta_step, 1)
                dve.wait_ge(beta_step, 1)
                dve.reciprocal(beta[:, :], beta_e[:, :]).then_inc(beta_step, 1)
                dve.wait_ge(beta_step, 2)
                dve.tensor_scalar(one_less_beta[:, :], beta[:, :], -1.0, 1.0, ALU.mult, ALU.add).then_inc(beta_step, 1)

                def by_segment(t, par):
                    return t.rearrange("p (a b c) -> p a b c", b=2, c=SEG)[:, :, par, :]

                def sigma(n, half, u):
                    i, h = u // 4, u % 4
                    dve.wait_ge(qk_copied, 8 * n + u + 1)
                    dve.tensor_scalar(e[u % 2][:, :], e[u % 2][:, :], 1.0, None, ALU.min).then_inc(exp_capped, 1)
                    dve.wait_ge(exp_capped, 8 * n + u + 1)
                    natural = (qT, kT)[i][:, h, half * HALF:(half + 1) * HALF]
                    if i:
                        if u >= 6:
                            dve.wait_ge(skt_ready, 4 * n + u - 5)
                        dve.scalar_tensor_tensor(out=sk[h % 2][:, :], in0=natural, scalar=0.0, in1=e[u % 2][:, :],
                                                 op0=ALU.max, op1=ALU.add).then_inc(sk_ready, 1)
                        dve.wait_ge(sk_ready, 4 * n + h + 1)
                    for par in range(2):
                        block_at = 1 + par if i == 0 else 3 * par
                        out = sqk[:, h, half * TPH:(half + 1) * TPH, block_at, :]
                        if i:
                            last = dve.tensor_copy(out, by_segment(sk[h % 2][:, :], par))
                        else:
                            last = dve.scalar_tensor_tensor(out=out, in0=by_segment(natural, par), scalar=0.0,
                                                            in1=by_segment(e[u % 2][:, :], par), op0=ALU.max, op1=ALU.add)
                    last.then_inc(sigma_ready, 1)

                def step(it, g, s):
                    pair, par = s // 2, s % 2
                    rows = slice(par * SEG, (par + 1) * SEG)
                    dve.wait_ge(kq_ready[g], 16 * it + s + 1)
                    both = KQ[g][:, 0:GROUP * MC].rearrange("p (h c) -> p h c", h=GROUP)
                    dve.reciprocal(nr[g][:, :], both[:, :, DK]).then_inc(nr_ready[g], 1)
                    if s == NSEG - 1:
                        return
                    dve.wait_ge(nr_ready[g], 16 * it + s + 1)
                    for hh in range(GROUP):
                        h = GROUP * g + hh
                        last = dve.scalar_tensor_tensor(
                            out=dl[g][par][rows, hh, 0:DK], in0=KQ[g][rows, hh * MC:hh * MC + DK],
                            scalar=nr[g][rows, hh:hh + 1], in1=v[rows, pair, h * DK:(h + 1) * DK],
                            op0=ALU.mult, op1=ALU.subtract)
                    last.then_inc(dl_ready[g], 1)

                def mask_scores(n, before):
                    if before:
                        dve.wait_ge(p_ready, 2 * n)
                    dve.wait_ge(sc_ready, n + 1)
                    dve.scalar_tensor_tensor(
                        out=sm[:, :, :], in0=L[0][:, :].rearrange("p (a c) -> p a c", a=NT), scalar=SCORE_SCALE,
                        in1=mask[:, :].unsqueeze(1).to_broadcast([P, NT, SEG]), op0=ALU.mult, op1=ALU.add)\
                       .then_inc(masked, 1)
                    dve.wait_ge(masked, n + 1)
                    dve.tensor_reduce(mx[:, :], sm[:, :, :], AX.X, ALU.max).then_inc(max_ready, 1)

                def sum_exp(n):
                    dve.wait_ge(exp_ready, n + 1)
                    dve.tensor_reduce(ssum[:, :], sm[:, :, :], AX.X, ALU.add).then_inc(sum_ready, 1)
                    dve.wait_ge(sum_ready, n + 1)
                    dve.reciprocal(rs[:, :], ssum[:, :]).then_inc(inv_ready, 1)

                def add_reading(n, half, h):
                    dve.wait_ge(at_ready, 4 * n + h + 1)
                    src = L[READINGS_BANK[h]][:, :].rearrange("p (a b c) -> p a b c", b=2, c=SEG)
                    dst = att[:, half, h, :].rearrange("p (a b c) -> p a b c", b=2, c=SEG)
                    for par in range(2):
                        last = dve.scalar_tensor_tensor(
                            out=dst[:, :, par, :], in0=src[:, :, 1 - par, :], scalar=beta_q[:, h:h + 1],
                            in1=dst[:, :, par, :], op0=ALU.mult, op1=ALU.add)
                    last.then_inc(att_ready, 1)

                def set_beta(it):
                    dve.tensor_scalar(beta_q[:, :], beta[:, bass.ts(it, HQ)], 1.0, None, ALU.mult)
                    dve.tensor_scalar(one_less_q[:, :], one_less_beta[:, bass.ts(it, HQ)], 1.0, None, ALU.mult)\
                       .then_inc(beta_q_set, 1)

                def slot(it, half, m, first, last):
                    n = 2 * it + half
                    ahead, behind = not (last and half), not (first and not half)
                    if ahead:
                        for what, u in AHEAD_AT.get(m - 2, ()):
                            if what == "project" and u < 8:
                                sigma(n + 1, 1 - half, u)
                    if behind and m - 1 in READINGS_AT:
                        add_reading(n - 1, 1 - half, READINGS_AT[m - 1])
                    if m in (1, 7):
                        mask_scores(2 * n + m // 7, behind or m == 7)
                    if m in (5, 10):
                        sum_exp(2 * n + m // 10)
                    if m == 7 and not half:
                        set_beta(it)

                def turn(it, first, last):
                    for half in range(2):
                        dve.wait_ge(v_copied, 8 * it + 4 * half + 4)
                        for at in range(STEPS):
                            for g in range(2):
                                step(it, g, half * STEPS + at)
                                slot(it, half, 2 * at + g, first, last)

                for u in range(8):
                    sigma(0, 0, u)
                dve.wait_ge(beta_step, 3)
                dve.wait_ge(consts_set, 12)
                dve.wait_ge(mask_loaded, 16)
                all_turns(dve, turn)
                dve.wait_ge(beta_q_set, NQ)
                for h in range(HQ):
                    add_reading(STAGES - 1, 1, h)
                dve.wait_ge(x_reloaded[0], 16)
                dve.wait_ge(y_loaded[0], 16)
                dve.tensor_tensor(x[:, 0:TPH, :], x[:, 0:TPH, :], y_in[0], ALU.add).then_inc(x_added, 1)
                dve.wait_ge(x_added, 1)
                norm.statistics(dve, 1, 0)
                dve.wait_ge(x_reloaded[1], 16)
                dve.wait_ge(y_loaded[1], 32)
                for par in range(2):
                    rows = slice(par * SEG, par * SEG + early)
                    dve.tensor_tensor(x[rows, TPH:NT, :], x[rows, TPH:NT, :], y_in[1][rows, :, :], ALU.add)\
                       .then_inc(x_added, 1)
                norm.normalise(dve, 1, 0)
                dve.wait_ge(x_added, 3)
                for b in range(2):
                    dve.wait_ge(placed, b + 1)
                    at = slice(TPH + 2 * b, TPH + 2 * b + 2)
                    dve.tensor_tensor(x[:, at, :], x[:, at, :], L[b][:, :].rearrange("p (t d) -> p t d", d=D), ALU.add)


def experts_layer(nc, outer, norm, carried, x, ident, ident_ready, tag, experts, w, tiles, next_w=None, out=None):
    with ExitStack() as ctx:
        def sb(name, shape, dt=F32):
            return ctx.enter_context(nc.sbuf_tensor(f"{name}_{tag}", shape, dt))

        def sem(name):
            return outer.enter_context(nc.semaphore(f"{name}_{tag}"))

        def bank(name):
            return ctx.enter_context(nc.psum_tensor(f"{name}_{tag}", [P, HALF], F32))

        E = experts
        shared, before, peeled, turns, par_of = tiles.shared, tiles.before, tiles.peeled, tiles.turns, tiles.par_of
        nb = len(before)
        with_routing = 5 if shared else 2
        shared_units = 2 * (nb - peeled)
        par_count = [par_of.count(0) - 1, par_of.count(1) - 1]
        closing_buf = (0, 2)
        closing = [(0, 0), (1, 0), (0, 1), (1, 1)]
        order = [(n // 2, n % 2) for n in range(2 * nb)]
        total = nb + 2 * turns

        acc = [bank(f"down{i}") for i in range(4)]
        G, U, C, R = bank("gate"), bank("up"), bank("weights"), bank("routing")
        xh, xl = norm.xh, norm.xl
        stage = carried.tiles
        buf_of = par_of[:]
        if shared:
            buf_of[2] = 2
        w_high = [sb(f"w_high{i}", [P, 3, D], F32R) for i in range(3)]
        w_low = [sb(f"w_low{i}", [P, 3, D], F32R) for i in range(3)]
        ones = sb("ones", [P, 1])
        router = sb("router", [P, KD, E])
        router_high, router_low = sb("router_high", [P, KD, E], F32R), sb("router_low", [P, KD, E], F32R)
        rank = sb("rank", [P, E])
        spread32, spread = sb("spread32", [P, E * INTER]), sb("spread", [P, E * INTER], BF16)
        logitsT = sb("logitsT", [E, T])
        s, s2, comb = sb("route", [P, NT, E]), sb("route2", [P, NT, E]), sb("combine", [P, NT, E])
        eq = sb("equal", [P, NT, E])
        best = [sb(f"best{i}", [P, NT, E]) for i in range(2)]
        m = [sb(f"max{i}", [P, NT]) for i in range(4)]
        second_less_best, best_share = sb("second_less_best", [P, NT]), sb("best_share", [P, NT])
        c_part, c_rest = [sb(f"c_part{i}", [P, NT, E], BF16) for i in range(2)], sb("c_rest", [P, NT, E])
        parts = sb("combine_parts", [P, NT, P])
        combT = sb("combT", [P, T], BF16)
        sg = [sb(f"silu{i}", [P, HALF]) for i in range(2)]
        ht = [sb(f"hidden{i}", [P, HALF]) for i in range(2)]
        h_high = [sb(f"h_high{i}", [P, HALF], F32R) for i in range(2)]
        h_low = [sb(f"h_low{i}", [P, HALF], F32R) for i in range(2)]

        loaded = [sem("tiles_loaded0"), sem("tiles_loaded1")]
        high_done, split_done, pool_step = sem("high_done"), sem("tile_split"), sem("pool_step")
        router_loaded, rank_loaded, spread_loaded = sem("router_loaded"), sem("rank_loaded"), sem("spread_loaded")
        router_split, spread_ready = sem("router_split"), sem("spread_ready")
        lT_ready, lT_copied, l_ready = sem("logitsT_ready"), sem("logitsT_copied"), sem("logits_ready")
        route = sem("route_step")
        to_exp, exp_done, comb_ready = sem("route_to_exp"), sem("route_exp"), sem("combine_ready")
        cT_ready, combT_ready = sem("combineT_ready"), sem("combine_parts")
        g_ready, u_ready, c_ready, silu_done = (
            sem("gate_ready"), sem("up_ready"), sem("weights_ready"), sem("silu_done"))
        h1_done, h_done, hh_done, hl_done = sem("gated"), sem("weighted"), sem("h_high_done"), sem("h_low_done")
        down_done, added, stored = sem("down_done"), sem("added"), sem("stored")

        N = 1 if shared else 3

        with nc.Block() as block:
            @block.sync
            def _(sp):
                sp.dma_start(router[:, :, :], w["router"].rearrange("(k p) e -> p k e", p=P))\
                  .then_inc(router_loaded, 16)
                sp.dma_start(rank[:, :], w["rank"]).then_inc(rank_loaded, 16)
                sp.dma_start(spread32[:, :], w["spread"]).then_inc(spread_loaded, 16)
                if shared:
                    for i in range(3):
                        sp.dma_start(carried.retention_w[i], next_w[i].rearrange("(k p) n -> p k n", p=P))\
                          .then_inc(carried.retention_w_loaded[i], 16)
                for q in range(2, nb):
                    sp.wait_ge(split_done, q - 1)
                    tiles.load(sp, stage[par_of[q]], before[q], loaded[par_of[q]])
                with sp.Fori(0, turns) as i:
                    for a in range(2):
                        sp.wait_ge(split_done, 2 * i + nb + a - 1)
                        tiles.load(sp, stage[a], ("expert", 2 * i + peeled + a, P), loaded[a])
                if out is not None:
                    for b in range(4):
                        at = slice(2 * b, 2 * b + 2)
                        sp.wait_ge(added, b + 1)
                        sp.dma_start(out.rearrange("a (t p) n -> p (a t) n", p=P)[:, at, :], x[:, at, :])\
                          .then_inc(stored, 16)
                    sp.wait_ge(stored, 64)

            @block.gpsimd
            def _(pool):
                pool.memset(ones[:, :], 1.0).then_inc(pool_step, 1)
                pool.wait_ge(pool_step, 1)

                def split(par, buf, n, first=False):
                    if not first:
                        pool.tensor_tensor(w_high[buf][:, :, :], stage[par][:, :, :],
                                           ones[:, 0:1].unsqueeze(2).to_broadcast([P, 3, D]), ALU.mult)\
                            .then_inc(high_done, 1)
                    pool.wait_ge(high_done, n)
                    pool.tensor_tensor(w_low[buf][:, :, :], stage[par][:, :, :], fr(w_high[buf][:, :, :]),
                                       ALU.subtract).then_inc(split_done, 1)

                def split_router():
                    pool.wait_ge(router_loaded, 16)
                    pool.tensor_tensor(router_high[:, :, :], router[:, :, :],
                                       ones[:, 0:1].unsqueeze(2).to_broadcast([P, KD, E]), ALU.mult)\
                        .then_inc(pool_step, 1)
                    pool.wait_ge(pool_step, 2)
                    pool.tensor_tensor(router_low[:, :, :], router[:, :, :], fr(router_high[:, :, :]),
                                       ALU.subtract).then_inc(router_split, 1)
                    pool.wait_ge(router_split, 1)
                    pool.memset(parts[:, :, :], 0.0).then_inc(pool_step, 1)
                    pool.wait_ge(pool_step, 3)

                def invert_second_half():
                    norm.invert(pool, N, 1)
                    pool.wait_ge(norm.rstd_done, 2 * N + 2)

                for q in range(2):
                    pool.wait_ge(carried.tile_loaded[q], 48 if shared else 96)
                    split(par_of[q], buf_of[q], q + 1, q == 0)
                    pool.wait_ge(split_done, q + 1)
                    if q == 0:
                        invert_second_half()
                        split_router()
                seen = [0, 0]
                for q in range(2, nb):
                    par = par_of[q]
                    seen[par] += 1
                    pool.wait_ge(loaded[par], 48 * seen[par])
                    used = [n for n in range(2 * nb) if order[n][0] < q and buf_of[order[n][0]] == buf_of[q]]
                    if used:
                        pool.wait_ge(down_done, max(used) + 1)
                    split(par, buf_of[q], q + 1)
                with pool.Fori(0, turns - 1) as i:
                    for a in range(2):
                        pool.wait_ge(loaded[a], 48 * i + 48 * par_count[a] + 48)
                        pool.wait_ge(down_done, 4 * i + 2 * (nb + a) - 2)
                        split(a, a, 2 * i + nb + a + 1)
                for a in range(2):
                    pool.wait_ge(loaded[a], 48 * (turns + par_count[a]))
                    if a == 0:
                        pool.wait_ge(down_done, 2 * total - 6)
                    pool.wait_ge(split_done, total - 2 + a)
                    split(a, closing_buf[a], total - 1 + a)
                if out is None:
                    norm.invert(pool, N + 1, 0)

            def rows_of(q):
                return before[q][2] if q < nb else P

            @block.tensor
            def _(pe):
                pe.wait_ge(ident_ready, 2)
                norm.turn(pe, N, 0, acc)
                norm.wait_split(pe, N, 0)

                def logits(half):
                    if half == 0:
                        pe.wait_ge(router_split, 1)
                    cols = slice(half * HALF, (half + 1) * HALF)
                    for k in range(KD):
                        last = split3(pe, (R, C)[half][0:E, :], (router_high[:, k, :], router_low[:, k, :]),
                                      (xh[:, k, cols], xl[:, k, cols]), k == 0, k == KD - 1)
                    last.then_inc(lT_ready, 1)

                def turn_logits():
                    pe.wait_ge(lT_copied, 2)
                    for t in range(NT):
                        last = pe.transpose(R[:, t * E:(t + 1) * E], logitsT[:, t * P:(t + 1) * P], ident[0:E, 0:E])
                    last.then_inc(l_ready, 1)

                def gate_up(n, half, par, rows, first=False, route=False):
                    cols = slice(half * HALF, (half + 1) * HALF)
                    for i, b in ((0, G), (1, U)):
                        if not first:
                            if i == 0:
                                pe.wait_ge(silu_done, n)
                            else:
                                pe.wait_ge(h1_done, n)
                        for k in range(KD):
                            at = slice(k * P, k * P + rows)
                            last = split3(pe, b[0:rows, :], (w_high[par][:, i, at], w_low[par][:, i, at]),
                                          (xh[:, k, cols], xl[:, k, cols]), k == 0, k == KD - 1)
                        last.then_inc((g_ready, u_ready)[i], 1)
                        if route and i == 0:
                            turn_logits()

                def weights(n, j, half, buf, again=True):
                    if again:
                        pe.wait_ge(h_done, n - 1 - shared_units)
                    pe.matmul((C, R)[buf][:, :], spread[:, bass.ts(j, P)], combT[:, half * HALF:(half + 1) * HALF],
                              start=True, stop=True).then_inc(c_ready, 1)

                def down(n, half, buf, par, rows, first=False):
                    pe.wait_ge(hl_done, n + 1)
                    d = (w_high[par][0:rows, 2, :], w_low[par][0:rows, 2, :])
                    for t in range(TPH):
                        tok = slice(t * P, (t + 1) * P)
                        last = split3(pe, acc[2 * half + t // 2][:, t % 2 * D:(t % 2 + 1) * D],
                                      (h_high[buf][0:rows, tok], h_low[buf][0:rows, tok]), d,
                                      first and t % 2 == 0, True, skip_group_check=True)
                    last.then_inc(down_done, 1)

                def turn_combine():
                    pe.wait_ge(comb_ready, 1)
                    for half in range(2):
                        for t in range(TPH):
                            j = half * TPH + t
                            last = pe.transpose((R, C)[half][:, t * P:(t + 1) * P], parts[:, j, :], ident[:, :])
                        last.then_inc(cT_ready, 1)

                def peeled_weights(n):
                    q, half = order[n]
                    if before[q][0] == "expert":
                        pe.wait_ge(spread_ready, 1)
                        pe.wait_ge(combT_ready, 2)
                        weights(n, before[q][1], half, n % 2, n - 2 >= shared_units)

                def peeled_down(n):
                    q, half = order[n]
                    down(n, half, n % 2, buf_of[q], before[q][2], q == 0)

                for n in range(2 * nb):
                    q, half = order[n]
                    pe.wait_ge(split_done, q + 1)
                    gate_up(n, half, buf_of[q], before[q][2], n == 0, n == 1)
                    if n == 0:
                        norm.turn(pe, N, 1, acc)
                        logits(0)
                        norm.wait_split(pe, N, 1)
                        logits(1)
                    if n == with_routing:
                        turn_combine()
                        if not shared:
                            peeled_weights(0)
                            for m in range(1, n + 1):
                                peeled_weights(m)
                                peeled_down(m - 1)
                            continue
                    if n > with_routing:
                        peeled_weights(n)
                    if n and (shared or n > with_routing):
                        peeled_down(n - 1)
                with pe.Fori(0, turns - 1) as i:
                    for a in range(2):
                        for half in range(2):
                            n = 4 * i + 2 * (nb + a) + half
                            if half == 0:
                                pe.wait_ge(split_done, 2 * i + nb + a + 1)
                            gate_up(n, half, a, P)
                            weights(n, 2 * i + peeled + a, half, half)
                            down(n - 1, 1 - half, 1 - half, a if half else 1 - a, P)
                for c, (a, half) in enumerate(closing):
                    n = 2 * total - 4 + c
                    pe.wait_ge(split_done, total - 1 + a)
                    gate_up(n, half, closing_buf[a], P)
                    weights(n, peeled + 2 * turns - 2 + a, half, n % 2)
                    if c:
                        down(n - 1, closing[c - 1][1], (n - 1) % 2, closing_buf[closing[c - 1][0]], P)
                    else:
                        down(n - 1, 1, 1, 1, P)
                down(2 * total - 1, 1, 1, closing_buf[1], P)

            @block.scalar
            def _(act):
                act.wait_ge(carried.tile_loaded[0], 48 if shared else 96)
                act.activation(w_high[buf_of[0]][:, :, :], stage[par_of[0]][:, :, :], ACT.Copy).then_inc(high_done, 1)
                norm.high(act, N, 0, acc)

                def logits():
                    for half in range(2):
                        act.wait_ge(lT_ready, half + 1)
                        act.activation(logitsT[:, half * HALF:(half + 1) * HALF], (R, C)[half][0:E, :], ACT.Copy)\
                           .then_inc(lT_copied, 1)

                def route_exp():
                    act.wait_ge(to_exp, 1)
                    if shared:
                        act.activation(s[:, :, :], s[:, :, :], ACT.Exp).then_inc(exp_done, 1)
                    else:
                        act.activation(best_share[:, :], second_less_best[:, :], ACT.Exp).then_inc(exp_done, 1)

                def copy_combine():
                    for half in range(2):
                        act.wait_ge(cT_ready, half + 1)
                        act.activation(combT[:, half * HALF:(half + 1) * HALF], (R, C)[half][:, :], ACT.Copy)\
                           .then_inc(combT_ready, 1)

                def silu(n, half, rows):
                    act.wait_ge(g_ready, n + 1)
                    act.activation(sg[half][0:rows, :], G[0:rows, :], ACT.Silu).then_inc(silu_done, 1)

                def high(n, half, rows, again=True, weighted=True):
                    if weighted:
                        act.wait_ge(h_done, n + 1 - shared_units)
                    else:
                        act.wait_ge(h1_done, n + 1)
                    if again:
                        act.wait_ge(down_done, n - 1)
                    act.activation(h_high[half][0:rows, :], ht[half][0:rows, :], ACT.Copy).then_inc(hh_done, 1)

                for n in range(2 * nb):
                    if n == with_routing and not shared:
                        copy_combine()
                    silu(n, n % 2, rows_of(n // 2))
                    if n == 0:
                        norm.high(act, N, 1, acc)
                        logits()
                    if n == (with_routing - 1 if shared else 0):
                        act.wait_ge(spread_loaded, 16)
                        act.activation(spread[:, :], spread32[:, :], ACT.Copy).then_inc(spread_ready, 1)
                    if n == 1:
                        route_exp()
                    if n == with_routing and shared:
                        copy_combine()
                    if n == with_routing and not shared:
                        for m in range(n):
                            high(m, m % 2, rows_of(m // 2), m >= 2)
                    if shared or n >= with_routing:
                        high(n, n % 2, rows_of(n // 2), n >= 2, n >= shared_units)
                with act.Fori(0, turns) as i:
                    for c in range(4):
                        silu(4 * i + 2 * nb + c, c % 2, P)
                        high(4 * i + 2 * nb + c, c % 2, P)

            @block.vector
            def _(dve):
                steps = [0]

                def step(ins):
                    steps[0] += 1
                    ins.then_inc(route, 1)
                    dve.wait_ge(route, steps[0])

                def wide(a):
                    return a[:, :].unsqueeze(2).to_broadcast([P, NT, E])

                def first_max(src, mx, key, out):
                    step(dve.tensor_reduce(mx[:, :], src[:, :, :], AX.X, ALU.max))
                    step(dve.tensor_tensor(eq[:, :, :], src[:, :, :], wide(mx), ALU.is_equal))
                    step(dve.tensor_tensor(eq[:, :, :], eq[:, :, :],
                                           rank[:, :].unsqueeze(1).to_broadcast([P, NT, E]), ALU.mult))
                    step(dve.tensor_reduce(key[:, :], eq[:, :, :], AX.X, ALU.max))
                    step(dve.tensor_tensor(out[:, :, :], eq[:, :, :], wide(key), ALU.is_equal))

                def parts_of_combine():
                    step(dve.tensor_copy(c_part[0][:, :, :], comb[:, :, :]))
                    step(dve.tensor_tensor(c_rest[:, :, :], comb[:, :, :], c_part[0][:, :, :], ALU.subtract))
                    step(dve.tensor_copy(c_part[1][:, :, :], c_rest[:, :, :]))
                    dve.wait_ge(pool_step, 3)
                    dve.tensor_copy(parts[:, :, 0:E], c_part[0][:, :, :])
                    dve.tensor_copy(parts[:, :, 32:32 + E], c_part[1][:, :, :])
                    dve.tensor_tensor(parts[:, :, 64:64 + E], c_rest[:, :, :], c_part[1][:, :, :], ALU.subtract)\
                       .then_inc(comb_ready, 1)

                def without_best():
                    step(dve.scalar_tensor_tensor(out=s2[:, :, :], in0=best[0][:, :, :], scalar=-LARGE, in1=s[:, :, :],
                                                  op0=ALU.mult, op1=ALU.add))

                def softmax_to_exp():
                    step(dve.tensor_reduce(m[0][:, :], s[:, :, :], AX.X, ALU.max))
                    dve.tensor_tensor(s[:, :, :], s[:, :, :], wide(m[0]), ALU.subtract).then_inc(to_exp, 1)

                def softmax():
                    dve.wait_ge(exp_done, 1)
                    step(dve.tensor_reduce(m[1][:, :], s[:, :, :], AX.X, ALU.add))
                    step(dve.reciprocal(m[2][:, :], m[1][:, :]))
                    step(dve.tensor_tensor(s[:, :, :], s[:, :, :], wide(m[2]), ALU.mult))

                def gate(n, half, rows):
                    dve.wait_ge(u_ready, n + 1)
                    dve.wait_ge(silu_done, n + 1)
                    dve.tensor_tensor(ht[half][0:rows, :], sg[half][0:rows, :], U[0:rows, :], ALU.mult)\
                       .then_inc(h1_done, 1)

                def weigh(n, half):
                    dve.wait_ge(h1_done, n + 1)
                    dve.wait_ge(c_ready, n + 1 - shared_units)
                    dve.tensor_tensor(ht[half][:, :], ht[half][:, :], (C, R)[half][:, :], ALU.mult).then_inc(h_done, 1)

                def low(n, half, rows):
                    dve.wait_ge(hh_done, n + 1)
                    dve.tensor_tensor(h_low[half][0:rows, :], ht[half][0:rows, :], fr(h_high[half][0:rows, :]),
                                      ALU.subtract).then_inc(hl_done, 1)

                def unit(n, half, rows, weighted):
                    gate(n, half, rows)
                    if weighted:
                        weigh(n, half)
                    low(n, half, rows)

                norm.statistics(dve, N, 1)
                norm.low(dve, N, 0, acc)
                norm.normalise(dve, N, 1)
                norm.low(dve, N, 1, acc)
                if shared:
                    unit(0, 0, rows_of(0), False)
                else:
                    gate(0, 0, P)
                    gate(1, 1, P)
                dve.wait_ge(rank_loaded, 16)
                dve.wait_ge(l_ready, 1)
                step(dve.tensor_copy(s[:, :, :], R[:, 0:NT * E].rearrange("p (t e) -> p t e", t=NT)))
                if shared:
                    softmax_to_exp()
                    for n in range(1, with_routing):
                        unit(n, n % 2, rows_of(n // 2), False)
                        if n == 1:
                            softmax()
                            first_max(s, m[0], m[1], best[0])
                        if n == 2:
                            without_best()
                            first_max(s2, m[2], m[3], best[1])
                        if n == 3:
                            step(dve.tensor_tensor(best[0][:, :, :], best[0][:, :, :], best[1][:, :, :], ALU.add))
                            step(dve.tensor_tensor(comb[:, :, :], s[:, :, :], best[0][:, :, :], ALU.mult))
                            parts_of_combine()
                    begun = with_routing
                else:
                    first_max(s, m[0], m[1], best[0])
                    without_best()
                    step(dve.tensor_reduce(m[2][:, :], s2[:, :, :], AX.X, ALU.max))
                    dve.tensor_tensor(second_less_best[:, :], m[2][:, :], m[0][:, :], ALU.subtract).then_inc(to_exp, 1)
                    dve.wait_ge(exp_done, 1)
                    step(dve.tensor_scalar(best_share[:, :], best_share[:, :], 1.0, None, ALU.add))
                    step(dve.reciprocal(m[1][:, :], best_share[:, :]))
                    step(dve.tensor_tensor(comb[:, :, :], best[0][:, :, :], wide(m[1]), ALU.mult))
                    parts_of_combine()
                    for n in range(2):
                        weigh(n, n)
                        low(n, n, P)
                    begun = 2
                for n in range(begun, 2 * nb):
                    unit(n, n % 2, rows_of(n // 2), before[n // 2][0] == "expert")
                def add_half(half):
                    dve.wait_ge(down_done, 2 * total - 2 + 2 * half)
                    for b in (2 * half, 2 * half + 1):
                        dve.tensor_tensor(x[:, 2 * b:2 * b + 2, :], x[:, 2 * b:2 * b + 2, :],
                                          acc[b][:, :].rearrange("p (t d) -> p t d", t=2), ALU.add).then_inc(added, 1)
                    dve.wait_ge(added, 2 * half + 2)

                with dve.Fori(0, turns - 1) as i:
                    for c in range(4):
                        unit(4 * i + 2 * nb + c, c % 2, P, True)
                for c in range(4):
                    unit(2 * total - 4 + c, c % 2, P, True)
                    if c == 2:
                        add_half(0)
                if out is None:
                    norm.statistics(dve, N + 1, 0)
                add_half(1)
                if out is None:
                    norm.normalise(dve, N + 1, 0)


def retention(nc, outer, norm, carried, x, ident, ident_ready, tables, decay_in, next_tiles):
    with ExitStack() as ctx:
        def sb(name, shape, dt=F32):
            return ctx.enter_context(nc.sbuf_tensor(f"{name}_r", shape, dt))

        def sem(name):
            return outer.enter_context(nc.semaphore(f"{name}_r"))

        B = [ctx.enter_context(nc.psum_tensor(f"bank{i}_r", [P, HALF], F32)) for i in range(8)]
        xh, xl = norm.xh, norm.xl
        w_stage, w_loaded = carried.retention_w, carried.retention_w_loaded
        w_high = [sb(f"w_high{i}", [P, KD, D], F32R) for i in range(3)]
        w_low = [sb(f"w_low{i}", [P, KD, D], F32R) for i in range(3)]
        ones = sb("ones", [P, 1])
        cos_sin = sb("cos_sin", [P, 4, T])
        decay = sb("decay", [P, T])
        prod = [sb(f"product{i}", [P, 4, HALF]) for i in range(2)]
        turned = [sb(f"turned{i}", [P, KD, HALF]) for i in range(2)]
        qk_high = [sb(f"{n}_high", [P, KD, T], F32R) for n in "qk"]
        qk_low = [sb(f"{n}_low", [P, KD, T], F32R) for n in "qk"]
        v = sb("v", [P, NT, D])
        att = [sb(f"att{i}", [P, T - i * P]) for i in range(NT)]

        tables_loaded, decay_loaded, ones_set = sem("tables_loaded"), sem("decay_loaded"), sem("ones_set")
        high_done, w_split = sem("w_high_done"), sem("w_split")
        proj_ready, prod_done, turn_done = sem("proj_ready"), sem("products_done"), sem("turn_done")
        qk_high_done, qk_split = sem("qk_high_done"), sem("qk_split")
        v_ready, v_copied = sem("v_ready"), sem("v_copied")
        s_ready, att_done, out_ready, added = sem("scores_ready"), sem("att_done"), sem("out_ready"), sem("added")

        units = [(0, 0), (1, 0), (0, 1), (1, 1)]
        unit_banks = [(B[4], B[5]), (B[6], B[7]), (B[0], B[1]), (B[2], B[3])]
        chunks = [(i, c, min(HALF, T - c)) for i in range(NT) for c in range(i * P, T, HALF)]
        chunks_to = [sum(1 for c in chunks if c[0] <= i) for i in range(NT)]

        with nc.Block() as block:
            @block.sync
            def _(sp):
                for i, t in enumerate(tables):
                    sp.dma_start(cos_sin[:, i, :], t).then_inc(tables_loaded, 16)
                sp.dma_start(decay[:, :], decay_in).then_inc(decay_loaded, 16)
                next_tiles.load_first(sp, carried)

            @block.gpsimd
            def _(pool):
                pool.memset(ones[:, :], 1.0).then_inc(ones_set, 1)
                pool.wait_ge(ones_set, 1)
                for i in range(3):
                    pool.wait_ge(w_loaded[i], 16)
                    if i:
                        pool.tensor_tensor(w_high[i][:, :, :], w_stage[i][:, :, :],
                                           ones[:, 0:1].unsqueeze(2).to_broadcast([P, KD, D]), ALU.mult)\
                            .then_inc(high_done, 1)
                    pool.wait_ge(high_done, i + 1)
                    pool.tensor_tensor(w_low[i][:, :, :], w_stage[i][:, :, :], fr(w_high[i][:, :, :]),
                                       ALU.subtract).then_inc(w_split, 1)
                    if i == 0:
                        pool.wait_ge(w_split, 1)
                        norm.invert(pool, 2, 1)
                        pool.wait_ge(norm.rstd_done, 6)
                for u in range(4):
                    if u >= 2:
                        pool.wait_ge(qk_split, u - 1)
                    for part, op in ((0, ALU.subtract), (1, ALU.add)):
                        pool.wait_ge(prod_done, 2 * u + part + 1)
                        pool.tensor_tensor(turned[u % 2][:, part, :], prod[u % 2][:, 2 * part, :],
                                           prod[u % 2][:, 2 * part + 1, :], op).then_inc(turn_done, 1)
                norm.invert(pool, 3, 0)

            @block.tensor
            def _(pe):
                pe.wait_ge(ident_ready, 2)
                norm.turn(pe, 2, 0, B[0:4])

                def project(u):
                    qk, half = units[u]
                    norm.wait_split(pe, 2, half)
                    pe.wait_ge(w_split, qk + 1)
                    cols = slice(half * HALF, (half + 1) * HALF)
                    for c in range(KD):
                        for k in range(KD):
                            last = split3(pe, unit_banks[u][c][:, :],
                                          (w_high[qk][:, k, c * P:(c + 1) * P], w_low[qk][:, k, c * P:(c + 1) * P]),
                                          (xh[:, k, cols], xl[:, k, cols]), k == 0, k == KD - 1)
                        last.then_inc(proj_ready, 1)

                project(0)
                norm.turn(pe, 2, 1, B[0:4])
                project(1)
                project(2)
                project(3)
                pe.wait_ge(w_split, 3)
                for j in range(NT):
                    if j % 4 == 0:
                        pe.wait_ge(prod_done, j // 2 + 2)
                    for k in range(KD):
                        last = split3(pe, B[4 + j // 2][:, j % 2 * D:(j % 2 + 1) * D],
                                      (xh[:, k, j * P:(j + 1) * P], xl[:, k, j * P:(j + 1) * P]),
                                      (w_high[2][:, k, :], w_low[2][:, k, :]), k == 0, k == KD - 1)
                    last.then_inc(v_ready, 1)

                def scores(i):
                    for n, (tile, c, w) in enumerate(chunks):
                        if tile != i:
                            continue
                        pe.wait_ge(qk_split, 3 + i // TPH)
                        if n == 2:
                            pe.wait_ge(prod_done, 8)
                        if n >= 4:
                            pe.wait_ge(att_done, n - 3)
                        for k in range(KD):
                            last = split3(pe, B[n % 4][:, 0:w],
                                          (qk_high[1][:, k, i * P:(i + 1) * P], qk_low[1][:, k, i * P:(i + 1) * P]),
                                          (qk_high[0][:, k, c:c + w], qk_low[0][:, k, c:c + w]), k == 0, k == KD - 1)
                        last.then_inc(s_ready, 1)

                def output(i):
                    pe.wait_ge(v_copied, 4)
                    pe.wait_ge(att_done, chunks_to[i])
                    for j in range(i, NT):
                        last = pe.matmul(B[4 + j // 2][:, j % 2 * D:(j % 2 + 1) * D], att[i][:, (j - i) * P:(j - i + 1) * P],
                                         v[:, i, :], start=(i == 0 and j % 2 == 0), stop=True, skip_group_check=True)
                        if j == i and i % 2:
                            last.then_inc(out_ready, 1)

                scores(0)
                for i in range(NT):
                    if i < NT - 1:
                        scores(i + 1)
                    output(i)

            @block.scalar
            def _(act):
                act.wait_ge(w_loaded[0], 16)
                act.activation(w_high[0][:, :, :], w_stage[0][:, :, :], ACT.Copy).then_inc(high_done, 1)
                for half in range(2):
                    norm.high(act, 2, half, B[0:4])

                def high(u):
                    qk, half = units[u]
                    act.wait_ge(turn_done, 2 * u + 2)
                    act.activation(qk_high[qk][:, :, half * HALF:(half + 1) * HALF], turned[u % 2][:, :, :], ACT.Copy)\
                       .then_inc(qk_high_done, 1)

                def copy_v(b):
                    act.wait_ge(v_ready, 2 * b + 2)
                    act.activation(v[:, 2 * b:2 * b + 2, :], B[4 + b][:, :].rearrange("p (t d) -> p t d", t=2), ACT.Copy)\
                       .then_inc(v_copied, 1)

                high(0)
                high(1)
                copy_v(0)
                copy_v(1)
                high(2)
                copy_v(2)
                copy_v(3)
                high(3)

            @block.vector
            def _(dve):
                norm.statistics(dve, 2, 1)
                norm.low(dve, 2, 0, B[0:4])
                norm.normalise(dve, 2, 1)
                norm.low(dve, 2, 1, B[0:4])
                dve.wait_ge(tables_loaded, 64)
                dve.wait_ge(decay_loaded, 16)

                def products(u):
                    qk, half = units[u]
                    cols = slice(half * HALF, (half + 1) * HALF)
                    even, odd = unit_banks[u]
                    cos, sin = cos_sin[:, 2 * qk, cols], cos_sin[:, 2 * qk + 1, cols]
                    dve.wait_ge(proj_ready, 2 * u + 2)
                    if u >= 2:
                        dve.wait_ge(turn_done, 2 * u - 2)
                    for part, (a, b) in enumerate(((even, odd), (odd, even))):
                        dve.tensor_tensor(prod[u % 2][:, 2 * part, :], a[:, :], cos, ALU.mult)
                        dve.tensor_tensor(prod[u % 2][:, 2 * part + 1, :], b[:, :], sin, ALU.mult).then_inc(prod_done, 1)

                def low(u):
                    qk, half = units[u]
                    cols = slice(half * HALF, (half + 1) * HALF)
                    dve.wait_ge(qk_high_done, u + 1)
                    dve.tensor_tensor(qk_low[qk][:, :, cols], turned[u % 2][:, :, :], fr(qk_high[qk][:, :, cols]),
                                      ALU.subtract).then_inc(qk_split, 1)

                products(0)
                products(1)
                low(0)
                products(2)
                low(1)
                products(3)
                low(2)
                low(3)
                def decay_scores(i):
                    for n, (tile, c, w) in enumerate(chunks):
                        if tile == i:
                            dve.wait_ge(s_ready, n + 1)
                            at = c - i * P
                            dve.tensor_tensor(att[i][:, at:at + w], B[n % 4][:, 0:w], decay[:, at:at + w], ALU.mult)\
                               .then_inc(att_done, 1)

                def add_half(half):
                    for b in (2 * half, 2 * half + 1):
                        dve.wait_ge(out_ready, b + 1)
                        dve.tensor_tensor(x[:, 2 * b:2 * b + 2, :], x[:, 2 * b:2 * b + 2, :],
                                          B[4 + b][:, :].rearrange("p (t d) -> p t d", t=2), ALU.add).then_inc(added, 1)
                    dve.wait_ge(added, 2 * half + 2)

                for i in range(NT):
                    decay_scores(i)
                    if i == NT - 3:
                        add_half(0)
                        norm.statistics(dve, 3, 0)
                norm.normalise(dve, 3, 0)
                add_half(1)


def build(nc, ins, out):
    with ExitStack() as outer:
        x = outer.enter_context(nc.sbuf_tensor("x", [P, NT, D], F32))
        ident = outer.enter_context(nc.sbuf_tensor("ident", [P, P], F32))
        ident_ready = outer.enter_context(nc.semaphore("ident_ready"))
        norm = Norm(nc, outer, x, ident)
        with nc.Block() as block:
            @block.gpsimd
            def _(pool):
                pool.memset(ident[:, :], 0.0).then_inc(ident_ready, 1)
                pool.wait_ge(ident_ready, 1)
                pool.affine_select(out=ident[:, :], in_=ident[:, :], compare_op=ALU.not_equal, fill=1.0, base=0,
                                   pattern=[[-1, P]], channel_multiplier=1).then_inc(ident_ready, 1)
        scratch = nc.dram_tensor("attention_out", (T, D), F32).ap()
        mixture0 = {
            "router": ins["router0"], "gate": ins["gate0"], "up": ins["up0"], "down": ins["down0"],
            "shared_gate_up": ins["L0_ffn_shared_gate_up"], "shared_down": ins["L0_ffn_shared_down"],
            "rank": ins["rank0"], "spread": ins["spread0"]}
        mixture1 = {
            "router": ins["router1"], "gate": ins["gate1"], "up": ins["up1"], "down": ins["down1"],
            "rank": ins["rank1"], "spread": ins["spread1"]}
        tiles0, tiles1 = ExpertTiles(E0, mixture0, True), ExpertTiles(E1, mixture1, False)
        carried = Carried(nc, outer)
        common = nc, outer, norm, carried, x, ident, ident_ready
        delta_attention(*common, scratch, ins["L0_attn_x"], ins["L0_attn_Wq"], ins["L0_attn_Wk"], ins["L0_attn_Wv"],
                        ins["L0_attn_Wo"], ins["betas_by_head"], ins["causal_mask"],
                        ins["place_rows"], tiles0)
        experts_layer(*common, "e0", E0, mixture0, tiles0,
                      next_w=(ins["W_Q"], ins["W_K"], ins["L1_attn_W_V"]))
        retention(*common, [ins[n] for n in ("cos_q", "sin_q", "cos_k", "sin_k")], ins["decay"], tiles1)
        experts_layer(*common, "e1", E1, mixture1, tiles1, out=out)


def shape_constants(np):
    s = np.arange(P)[:, None] % SEG
    tables = {"causal_mask": np.where(np.arange(SEG)[None, :] <= s, 0.0, -LARGE)}
    row, per_turn = np.arange(P), SEG // NQ
    head, segment, m = row // 32, row % 32 // 4, row % 4
    place = np.zeros((P, TPH, P))
    place[row, segment // 2, segment % 2 * SEG + (NQ - 1) * per_turn + 4 * head + m] = 1.0
    tables["place_rows"] = place
    pair, pos = np.arange(P, dtype=np.float32), np.arange(T, dtype=np.float32)
    scale_vec = (2 * pair + np.float32(0.4 * D)) / np.float32(1.4 * D)
    scale = scale_vec[:, None] ** (pos / np.float32(SCALE_BASE))[None, :]
    angle = pos[None, :] * (np.float32(1) / np.float32(10000) ** (pair / np.float32(P)))[:, None]
    for name, sc in (("q", scale), ("k", np.float32(1) / scale)):
        tables[f"cos_{name}"], tables[f"sin_{name}"] = np.cos(angle) * sc, np.sin(angle) * sc
    distance = np.arange(T)[None, :] - np.arange(P)[:, None]
    tables["decay"] = np.where(distance >= 0, np.float32(GAMMA) ** np.maximum(distance, 0).astype(np.float32), 0.0)
    for n, e in ((0, E0), (1, E1)):
        tables[f"rank{n}"] = np.tile(e - np.arange(e), (P, 1))
        spread = np.zeros((P, e * INTER))
        for part in range(3):
            spread[32 * part + np.arange(e * INTER) // INTER, np.arange(e * INTER)] = 1.0
        tables[f"spread{n}"] = spread
    return {n: a.astype(np.float32) for n, a in tables.items()}


def layouts(np, inputs):
    a = {n: np.asarray(inputs[n]) for n in (
        "L0_attn_x", "L0_attn_Wq", "L0_attn_Wk", "L0_attn_Wv", "L0_attn_Wo",
        "L0_ffn_shared_gate_up", "L0_ffn_shared_down", "L1_attn_W_V")}
    for n in ("W_Q", "W_K"):
        a[n] = np.asarray(inputs[f"L1_attn_{n}"]).reshape(D, D // 2, 2).transpose(0, 2, 1).reshape(D, D)
    a["betas_by_head"] = np.asarray(inputs["L0_attn_betas"]).reshape(H, DK).T
    gate_up = np.asarray(inputs["L0_ffn_w_gate_up"]).transpose(1, 0, 2)
    a["gate0"] = gate_up[:, :, :INTER].reshape(D, E0 * INTER)
    a["up0"] = gate_up[:, :, INTER:].reshape(D, E0 * INTER)
    a["down0"] = np.asarray(inputs["L0_ffn_w_down"]).reshape(E0 * INTER, D)
    a["router0"] = np.asarray(inputs["L0_ffn_gate_w"]).T
    a["gate1"] = np.asarray(inputs["L1_ffn_gate_w"]).transpose(2, 0, 1).reshape(D, E1 * INTER)
    a["up1"] = np.asarray(inputs["L1_ffn_up_w"]).transpose(2, 0, 1).reshape(D, E1 * INTER)
    a["down1"] = np.asarray(inputs["L1_ffn_down_w"]).transpose(0, 2, 1).reshape(E1 * INTER, D)
    a["router1"] = np.asarray(inputs["L1_ffn_router_w"]).T
    return a


def kernel(**inputs):
    import numpy as np
    import concourse.bacc as bacc
    from concourse.bass_utils import run_bass_kernel_spmd as run

    nc = bacc.Bacc("TRN2", target_bir_lowering=False, num_devices=1)
    arrays = {**layouts(np, inputs), **shape_constants(np)}
    arrays = {n: np.ascontiguousarray(a) for n, a in arrays.items()}
    ins = {n: nc.dram_tensor(n, a.shape, F32, kind="ExternalInput").ap() for n, a in arrays.items()}
    out = nc.dram_tensor("out", (1, T, D), F32, kind="ExternalOutput").ap()
    build(nc, ins, out)
    r = run(nc, [arrays], core_ids=[0])
    return r.results[0]["out"]
```
